# Optimizing a Trainium2 kernel written in Bass

```python
import numpy as np
import jax
import jax.numpy as jnp

def _softmax(x, axis=-1):
    return jax.nn.softmax(x, axis=axis)

def _gelu(x):
    return jax.nn.gelu(x, approximate=True)

def _silu(x):
    return jax.nn.silu(x)

def _sigmoid(x):
    return jax.nn.sigmoid(x)

def _layernorm(x, axis=-1, eps=1e-05):
    m = jnp.mean(x, axis=axis, keepdims=True)
    v = jnp.var(x, axis=axis, keepdims=True)
    return (x - m) / jnp.sqrt(v + eps)

def _scatter_add(tgt, idx, src, axis=0):
    return tgt.at[idx].add(src)

def _segment_sum(src, seg, n):
    return jax.ops.segment_sum(src, seg, n)
kernel_name = 'mk_xattn_ffn_d4_seqx_r8_e91ff7'

def setup_inputs(seed: int=0):
    np.random.seed(seed)
    _w = jnp.asarray

    def _rec_inputs():
        import jax
        import jax.numpy as jnp
        _rk = jax.random.key(seed)
        x = -0.0002928 + 1 * jax.random.normal(jax.random.fold_in(_rk, 1), (128, 64, 128), jnp.float32)
        _lenS = 64 - jax.random.randint(jax.random.fold_in(_rk, 7), (128,), 0, max(1, 64 // 4) + 1, jnp.int32)
        _lenS2 = 64 - jax.random.randint(jax.random.fold_in(_rk, 8), (128,), 0, max(1, 64 // 4) + 1, jnp.int32)
        _ctx_1024P = jax.random.normal(jax.random.fold_in(_rk, 11), (128, 16, 128), jnp.float32)
        _ctx_1024c = jax.random.dirichlet(jax.random.fold_in(_rk, 511), 0.3 * jnp.ones((16,), jnp.float32), (128, 64))
        _ctx_1024t = jnp.einsum('bsk,bkd->bsd', _ctx_1024c, _ctx_1024P)
        _ctx_1024t = _ctx_1024t * jax.lax.rsqrt(jnp.mean(jnp.square(_ctx_1024t)) + 1e-12) * 0.953939
        ctx_1024 = -1.39393e-06 + 0.999914 * (_ctx_1024t + 0.3 * jax.random.normal(jax.random.fold_in(_rk, 611), (128, 64, 128), jnp.float32))
        _validS = jnp.arange(64)[None, :] < _lenS[:, None]
        _validS2 = jnp.arange(64)[None, :] < _lenS2[:, None]
        _causal = jnp.tril(jnp.ones((64, 64), dtype=bool))
        mask_Bx1xSxS2_if1 = jnp.where(jnp.ones((128, 1, 64, 64), dtype=bool), 1, 0).astype(jnp.int32)
        mask_Bx1x1xS2_bk0 = jnp.logical_not(jnp.broadcast_to(_validS2[:, None, None, :], (128, 1, 1, 64)))
        mask_Bx1xSxS2_ik1 = jnp.where(jnp.broadcast_to(_validS2[:, None, None, :], (128, 1, 64, 64)), 1, 0).astype(jnp.int32)
        mask_BxSxS2_ik1 = jnp.where(jnp.broadcast_to(_validS2[:, None, :], (128, 64, 64)), 1, 0).astype(jnp.int32)
        return (x, ctx_1024, mask_Bx1xSxS2_if1, mask_Bx1x1xS2_bk0, mask_Bx1xSxS2_ik1, mask_BxSxS2_ik1)
    x, ctx_1024, mask_Bx1xSxS2_if1, mask_Bx1x1xS2_bk0, mask_Bx1xSxS2_ik1, mask_BxSxS2_ik1 = _rec_inputs()

    def _L0_xattn_setup():
        import jax, jax.numpy as jnp
        import numpy as np
        D_MODEL = 128
        HEADS = 16
        D_K = D_MODEL // HEADS
        NEG = -1000000000.0
        key = jax.random.key(seed)
        ks = jax.random.split(key, 12)
        B, S = (2, 256)
        inp = {'q': jax.random.normal(ks[0], (B, S, D_MODEL), jnp.float32), 'k': jax.random.normal(ks[1], (B, S, D_MODEL), jnp.float32), 'v': jax.random.normal(ks[2], (B, S, D_MODEL), jnp.float32), 'mask': jnp.ones((B, 1, S, S), jnp.int32), 'W_q': jax.random.normal(ks[3], (D_MODEL, D_MODEL), jnp.float32) / np.sqrt(D_MODEL), 'b_q': jnp.zeros((D_MODEL,), jnp.float32), 'W_k': jax.random.normal(ks[4], (D_MODEL, D_MODEL), jnp.float32) / np.sqrt(D_MODEL), 'b_k': jnp.zeros((D_MODEL,), jnp.float32), 'W_v': jax.random.normal(ks[5], (D_MODEL, D_MODEL), jnp.float32) / np.sqrt(D_MODEL), 'b_v': jnp.zeros((D_MODEL,), jnp.float32), 'W_o': jax.random.normal(ks[6], (D_MODEL, D_MODEL), jnp.float32) / np.sqrt(D_MODEL), 'b_o': jnp.zeros((D_MODEL,), jnp.float32)}
        return inp
    _L0_xattn_all = _L0_xattn_setup()
    _L0_xattn_in = {k: v for k, v in _L0_xattn_all.items() if k in ('W_q', 'b_q', 'W_k', 'b_k', 'W_v', 'b_v', 'W_o', 'b_o')}
    del _L0_xattn_all

    def _L0_ffn_setup():
        import jax, jax.numpy as jnp
        import numpy as np
        THRESHOLD = 0.1
        key = jax.random.key(seed)
        k1, k2, k3 = jax.random.split(key, 3)
        B, S, D, E = (4, 512, 128, 8)
        inputs = jax.random.normal(k1, (B, S, D), dtype=jnp.float32)
        gate_w = jax.random.normal(k2, (D, E), dtype=jnp.float32) * 0.02
        gate_b = jnp.zeros((E,), dtype=jnp.float32)
        expert_w = jax.random.normal(k3, (E, D, D), dtype=jnp.float32) * 0.02
        expert_b = jnp.zeros((E, D), dtype=jnp.float32)
        return {'inputs': inputs, 'gate_w': gate_w, 'gate_b': gate_b, 'expert_w': expert_w, 'expert_b': expert_b}
    _L0_ffn_all = _L0_ffn_setup()
    _L0_ffn_in = {k: v for k, v in _L0_ffn_all.items() if k in ('gate_w', 'gate_b', 'expert_w', 'expert_b')}
    del _L0_ffn_all

    def _L1_xattn_setup():
        import math
        import jax, jax.numpy as jnp
        import numpy as np
        NUM_BUCKETS = 32
        MAX_DISTANCE = 128
        H = 16
        D_MODEL = 128
        D_K = D_MODEL // H

        def _relative_position_bucket(relative_position):
            nb = NUM_BUCKETS // 2
            buckets = (relative_position > 0).astype(jnp.int32) * nb
            rp = jnp.abs(relative_position)
            max_exact = nb // 2
            is_small = rp < max_exact
            rp_large = max_exact + (jnp.log(jnp.maximum(rp, 1).astype(jnp.float32) / max_exact) / math.log(MAX_DISTANCE / max_exact) * (nb - max_exact)).astype(jnp.int32)
            rp_large = jnp.minimum(rp_large, nb - 1)
            return buckets + jnp.where(is_small, rp, rp_large)
        key = jax.random.key(seed)
        ks = jax.random.split(key, 8)
        B, T_k, T_q = (4, 256, 128)
        std = D_MODEL ** (-0.5)
        inp = {'src': jax.random.normal(ks[0], (B, T_k, D_MODEL), dtype=jnp.float32), 'dst': jax.random.normal(ks[1], (B, T_q, D_MODEL), dtype=jnp.float32), 'mask': jax.random.randint(ks[2], (B, 1, 1, T_k), 0, 2).astype(bool), 'Wq': jax.random.normal(ks[3], (D_MODEL, D_MODEL), dtype=jnp.float32) * std, 'Wk': jax.random.normal(ks[4], (D_MODEL, D_MODEL), dtype=jnp.float32) * std, 'Wv': jax.random.normal(ks[5], (D_MODEL, D_MODEL), dtype=jnp.float32) * std, 'Wo': jax.random.normal(ks[6], (D_MODEL, D_MODEL), dtype=jnp.float32) * std, 'rel_bias': jax.random.normal(ks[7], (H, NUM_BUCKETS), dtype=jnp.float32) * NUM_BUCKETS ** (-0.5)}
        return inp
    _L1_xattn_all = _L1_xattn_setup()
    _L1_xattn_in = {k: v for k, v in _L1_xattn_all.items() if k in ('Wq', 'Wk', 'Wv', 'Wo', 'rel_bias')}
    del _L1_xattn_all

    def _L1_ffn_setup():
        import jax, jax.numpy as jnp
        import numpy as np
        D_MODEL = 128
        HIDDEN = 512
        N_ROUTING = 2
        key = jax.random.key(seed)
        ks = jax.random.split(key, 10)
        s = 0.02
        x = jax.random.normal(ks[0], (4, 512, D_MODEL), dtype=jnp.float32)
        gate_w = jax.random.normal(ks[1], (N_ROUTING, D_MODEL), dtype=jnp.float32) * s
        w1 = jax.random.normal(ks[2], (N_ROUTING, D_MODEL, HIDDEN), dtype=jnp.float32) * s
        b1 = jax.random.normal(ks[3], (N_ROUTING, HIDDEN), dtype=jnp.float32) * s
        w2 = jax.random.normal(ks[4], (N_ROUTING, HIDDEN, D_MODEL), dtype=jnp.float32) * s
        b2 = jax.random.normal(ks[5], (N_ROUTING, D_MODEL), dtype=jnp.float32) * s
        sw1 = jax.random.normal(ks[6], (D_MODEL, HIDDEN), dtype=jnp.float32) * s
        sb1 = jax.random.normal(ks[7], (HIDDEN,), dtype=jnp.float32) * s
        sw2 = jax.random.normal(ks[8], (HIDDEN, D_MODEL), dtype=jnp.float32) * s
        sb2 = jax.random.normal(ks[9], (D_MODEL,), dtype=jnp.float32) * s
        return {'x': x, 'gate_w': gate_w, 'w1': w1, 'b1': b1, 'w2': w2, 'b2': b2, 'sw1': sw1, 'sb1': sb1, 'sw2': sw2, 'sb2': sb2}
    _L1_ffn_all = _L1_ffn_setup()
    _L1_ffn_in = {k: v for k, v in _L1_ffn_all.items() if k in ('gate_w', 'w1', 'b1', 'w2', 'b2', 'sw1', 'sb1', 'sw2', 'sb2')}
    del _L1_ffn_all

    def _L2_xattn_setup():
        import jax, jax.numpy as jnp
        import numpy as np
        E = 128
        H = 16
        DH = E // H
        EPS = 1e-09

        def _split_heads(x):
            B, S, _ = x.shape
            return x.reshape(B, S, H, DH).transpose(0, 2, 1, 3)
        key = jax.random.key(seed)
        ks = jax.random.split(key, 12)
        B, S = (2, 256)
        scale = 1.0 / np.sqrt(E)
        inp = {'query': jax.random.normal(ks[0], (B, S, E), dtype=jnp.float32), 'key': jax.random.normal(ks[1], (B, S, E), dtype=jnp.float32), 'value': jax.random.normal(ks[2], (B, S, E), dtype=jnp.float32), 'mask': jax.random.randint(ks[3], (B, 1, S, S), 0, 2, dtype=jnp.int32), 'Wq': jax.random.normal(ks[4], (E, E), dtype=jnp.float32) * scale, 'bq': jnp.zeros((E,), dtype=jnp.float32), 'Wk': jax.random.normal(ks[5], (E, E), dtype=jnp.float32) * scale, 'bk': jnp.zeros((E,), dtype=jnp.float32), 'Wv': jax.random.normal(ks[6], (E, E), dtype=jnp.float32) * scale, 'bv': jnp.zeros((E,), dtype=jnp.float32), 'Wo': jax.random.normal(ks[7], (E, E), dtype=jnp.float32) * scale, 'bo': jnp.zeros((E,), dtype=jnp.float32)}
        return inp
    _L2_xattn_all = _L2_xattn_setup()
    _L2_xattn_in = {k: v for k, v in _L2_xattn_all.items() if k in ('Wq', 'bq', 'Wk', 'bk', 'Wv', 'bv', 'Wo', 'bo')}
    del _L2_xattn_all

    def _L2_ffn_setup():
        import jax, jax.numpy as jnp
        import numpy as np
        B, T, C, I, E = (4, 256, 128, 352, 7)

        def _swiglu(h, w1, w2, w3):
            return jax.nn.silu(h @ w1.T) * (h @ w3.T) @ w2.T
        key = jax.random.key(seed)
        ks = jax.random.split(key, 9)
        sc_c = 1.0 / np.sqrt(C)
        sc_i = 1.0 / np.sqrt(I)
        return {'x': jax.random.normal(ks[0], (B, T, C), jnp.float32), 'router_w': jax.random.normal(ks[1], (E, C), jnp.float32) * sc_c, 'routing_bias': jnp.zeros((E,), jnp.float32), 'sw1': jax.random.normal(ks[2], (I, C), jnp.float32) * sc_c, 'sw2': jax.random.normal(ks[3], (C, I), jnp.float32) * sc_i, 'sw3': jax.random.normal(ks[4], (I, C), jnp.float32) * sc_c, 'ew1': jax.random.normal(ks[5], (E, I, C), jnp.float32) * sc_c, 'ew2': jax.random.normal(ks[6], (E, C, I), jnp.float32) * sc_i, 'ew3': jax.random.normal(ks[7], (E, I, C), jnp.float32) * sc_c}
    _L2_ffn_all = _L2_ffn_setup()
    _L2_ffn_in = {k: v for k, v in _L2_ffn_all.items() if k in ('router_w', 'routing_bias', 'sw1', 'sw2', 'sw3', 'ew1', 'ew2', 'ew3')}
    del _L2_ffn_all

    def _L3_xattn_setup():
        import jax, jax.numpy as jnp
        import numpy as np
        NEG = -9000000000000000.0
        EPS = 1e-05
        key = jax.random.key(seed)
        k1, k2, k3, k4 = jax.random.split(key, 4)
        B, S, D = (4, 256, 128)
        q = jax.random.normal(k1, (B, S, D), dtype=jnp.float32)
        k = jax.random.normal(k2, (B, S, D), dtype=jnp.float32)
        v = jax.random.normal(k3, (B, S, D), dtype=jnp.float32)
        mask = jax.random.randint(k4, (B, S, S), 0, 2, dtype=jnp.int32)
        gamma = jnp.ones((D,), dtype=jnp.float32)
        beta = jnp.zeros((D,), dtype=jnp.float32)
        return {'q': q, 'k': k, 'v': v, 'mask': mask, 'gamma': gamma, 'beta': beta}
    _L3_xattn_all = _L3_xattn_setup()
    _L3_xattn_in = {k: v for k, v in _L3_xattn_all.items() if k in ('gamma', 'beta')}
    del _L3_xattn_all

    def _L3_ffn_setup():
        import jax, jax.numpy as jnp
        import numpy as np
        N_HEADS = 16
        NUM_EXPERTS = 4
        TOP_K = 2
        D_MODEL = 128
        GATE_HID = 128
        key = jax.random.key(seed)
        ks = jax.random.split(key, 12)
        B, T, C, E = (2, 128, D_MODEL, NUM_EXPERTS)
        s = 1.0 / np.sqrt(C)
        return {'hidden_states': jax.random.normal(ks[0], (B, T, C), jnp.float32), 'Wq': jax.random.normal(ks[1], (E, C, C), jnp.float32) * s, 'bq': jnp.zeros((E, C), jnp.float32), 'Wk': jax.random.normal(ks[2], (E, C, C), jnp.float32) * s, 'bk': jnp.zeros((E, C), jnp.float32), 'Wv': jax.random.normal(ks[3], (E, C, C), jnp.float32) * s, 'bv': jnp.zeros((E, C), jnp.float32), 'Wg1': jax.random.normal(ks[4], (C, GATE_HID), jnp.float32) * s, 'bg1': jnp.zeros((GATE_HID,), jnp.float32), 'Wg2': jax.random.normal(ks[5], (GATE_HID, E), jnp.float32) / np.sqrt(GATE_HID), 'bg2': jnp.zeros((E,), jnp.float32), 'Wo': jax.random.normal(ks[6], (C, C), jnp.float32) * s, 'bo': jnp.zeros((C,), jnp.float32)}
    _L3_ffn_all = _L3_ffn_setup()
    _L3_ffn_in = {k: v for k, v in _L3_ffn_all.items() if k in ('Wq', 'bq', 'Wk', 'bk', 'Wv', 'bv', 'Wg1', 'bg1', 'Wg2', 'bg2', 'Wo', 'bo')}
    del _L3_ffn_all
    return {'x': x, 'ctx_1024': ctx_1024, 'mask_Bx1xSxS2_if1': mask_Bx1xSxS2_if1, 'mask_Bx1x1xS2_bk0': mask_Bx1x1xS2_bk0, 'mask_Bx1xSxS2_ik1': mask_Bx1xSxS2_ik1, 'mask_BxSxS2_ik1': mask_BxSxS2_ik1, 'L0_xattn_W_q': _L0_xattn_in['W_q'], 'L0_xattn_b_q': _L0_xattn_in['b_q'], 'L0_xattn_W_k': _L0_xattn_in['W_k'], 'L0_xattn_b_k': _L0_xattn_in['b_k'], 'L0_xattn_W_v': _L0_xattn_in['W_v'], 'L0_xattn_b_v': _L0_xattn_in['b_v'], 'L0_xattn_W_o': _L0_xattn_in['W_o'], 'L0_xattn_b_o': _L0_xattn_in['b_o'], 'L0_ffn_gate_w': _L0_ffn_in['gate_w'], 'L0_ffn_gate_b': _L0_ffn_in['gate_b'], 'L0_ffn_expert_w': _L0_ffn_in['expert_w'], 'L0_ffn_expert_b': _L0_ffn_in['expert_b'], 'L1_xattn_Wq': _L1_xattn_in['Wq'], 'L1_xattn_Wk': _L1_xattn_in['Wk'], 'L1_xattn_Wv': _L1_xattn_in['Wv'], 'L1_xattn_Wo': _L1_xattn_in['Wo'], 'L1_xattn_rel_bias': _L1_xattn_in['rel_bias'], 'L1_ffn_gate_w': _L1_ffn_in['gate_w'], 'L1_ffn_w1': _L1_ffn_in['w1'], 'L1_ffn_b1': _L1_ffn_in['b1'], 'L1_ffn_w2': _L1_ffn_in['w2'], 'L1_ffn_b2': _L1_ffn_in['b2'], 'L1_ffn_sw1': _L1_ffn_in['sw1'], 'L1_ffn_sb1': _L1_ffn_in['sb1'], 'L1_ffn_sw2': _L1_ffn_in['sw2'], 'L1_ffn_sb2': _L1_ffn_in['sb2'], 'L2_xattn_Wq': _L2_xattn_in['Wq'], 'L2_xattn_bq': _L2_xattn_in['bq'], 'L2_xattn_Wk': _L2_xattn_in['Wk'], 'L2_xattn_bk': _L2_xattn_in['bk'], 'L2_xattn_Wv': _L2_xattn_in['Wv'], 'L2_xattn_bv': _L2_xattn_in['bv'], 'L2_xattn_Wo': _L2_xattn_in['Wo'], 'L2_xattn_bo': _L2_xattn_in['bo'], 'L2_ffn_router_w': _L2_ffn_in['router_w'], 'L2_ffn_routing_bias': _L2_ffn_in['routing_bias'], 'L2_ffn_sw1': _L2_ffn_in['sw1'], 'L2_ffn_sw2': _L2_ffn_in['sw2'], 'L2_ffn_sw3': _L2_ffn_in['sw3'], 'L2_ffn_ew1': _L2_ffn_in['ew1'], 'L2_ffn_ew2': _L2_ffn_in['ew2'], 'L2_ffn_ew3': _L2_ffn_in['ew3'], 'L3_xattn_gamma': _L3_xattn_in['gamma'], 'L3_xattn_beta': _L3_xattn_in['beta'], 'L3_ffn_Wq': _L3_ffn_in['Wq'], 'L3_ffn_bq': _L3_ffn_in['bq'], 'L3_ffn_Wk': _L3_ffn_in['Wk'], 'L3_ffn_bk': _L3_ffn_in['bk'], 'L3_ffn_Wv': _L3_ffn_in['Wv'], 'L3_ffn_bv': _L3_ffn_in['bv'], 'L3_ffn_Wg1': _L3_ffn_in['Wg1'], 'L3_ffn_bg1': _L3_ffn_in['bg1'], 'L3_ffn_Wg2': _L3_ffn_in['Wg2'], 'L3_ffn_bg2': _L3_ffn_in['bg2'], 'L3_ffn_Wo': _L3_ffn_in['Wo'], 'L3_ffn_bo': _L3_ffn_in['bo']}

def reference(x, ctx_1024, mask_Bx1xSxS2_if1, mask_Bx1x1xS2_bk0, mask_Bx1xSxS2_ik1, mask_BxSxS2_ik1, L0_xattn_W_q, L0_xattn_b_q, L0_xattn_W_k, L0_xattn_b_k, L0_xattn_W_v, L0_xattn_b_v, L0_xattn_W_o, L0_xattn_b_o, L0_ffn_gate_w, L0_ffn_gate_b, L0_ffn_expert_w, L0_ffn_expert_b, L1_xattn_Wq, L1_xattn_Wk, L1_xattn_Wv, L1_xattn_Wo, L1_xattn_rel_bias, L1_ffn_gate_w, L1_ffn_w1, L1_ffn_b1, L1_ffn_w2, L1_ffn_b2, L1_ffn_sw1, L1_ffn_sb1, L1_ffn_sw2, L1_ffn_sb2, L2_xattn_Wq, L2_xattn_bq, L2_xattn_Wk, L2_xattn_bk, L2_xattn_Wv, L2_xattn_bv, L2_xattn_Wo, L2_xattn_bo, L2_ffn_router_w, L2_ffn_routing_bias, L2_ffn_sw1, L2_ffn_sw2, L2_ffn_sw3, L2_ffn_ew1, L2_ffn_ew2, L2_ffn_ew3, L3_xattn_gamma, L3_xattn_beta, L3_ffn_Wq, L3_ffn_bq, L3_ffn_Wk, L3_ffn_bk, L3_ffn_Wv, L3_ffn_bv, L3_ffn_Wg1, L3_ffn_bg1, L3_ffn_Wg2, L3_ffn_bg2, L3_ffn_Wo, L3_ffn_bo):
    import jax
    import jax.numpy as jnp

    def _L0_xattn_ref(q, k, v, mask, W_q, b_q, W_k, b_k, W_v, b_v, W_o, b_o):
        import jax, jax.numpy as jnp
        import numpy as np
        D_MODEL = 128
        HEADS = 16
        D_K = D_MODEL // HEADS
        NEG = -1000000000.0
        B, S, _ = q.shape
        query = q @ W_q + b_q
        key_ = k @ W_k + b_k
        value = v @ W_v + b_v
        query = query.reshape(B, S, HEADS, D_K).transpose(0, 2, 1, 3)
        key_ = key_.reshape(B, S, HEADS, D_K).transpose(0, 2, 1, 3)
        value = value.reshape(B, S, HEADS, D_K).transpose(0, 2, 1, 3)
        scores = jnp.einsum('bhqd,bhkd->bhqk', query, key_) / np.sqrt(D_K).astype(np.float32)
        scores = jnp.where(mask == 0, jnp.float32(NEG), scores)
        attn = jax.nn.softmax(scores, axis=-1)
        x = jnp.einsum('bhqk,bhkd->bhqd', attn, value)
        x = x.transpose(0, 2, 1, 3).reshape(B, S, HEADS * D_K)
        return x @ W_o + b_o

    def _L0_ffn_ref(inputs, gate_w, gate_b, expert_w, expert_b):
        import jax, jax.numpy as jnp
        import numpy as np
        THRESHOLD = 0.1
        d = inputs.shape[-1]
        x = inputs.reshape(-1, d)
        gate_logits = jax.nn.softmax(x @ gate_w + gate_b, axis=-1)
        selected = (gate_logits >= THRESHOLD).astype(x.dtype)
        weights = gate_logits * selected
        wsum = jnp.sum(weights, axis=-1, keepdims=True)
        weights = weights / jnp.where(wsum == 0, jnp.ones_like(wsum), wsum)
        E = expert_w.shape[0]
        out = jnp.zeros((x.shape[0], expert_w.shape[-1]), dtype=x.dtype)
        for e in range(E):
            out = out + weights[:, e:e + 1] * (x @ expert_w[e] + expert_b[e])
        return out.reshape(*inputs.shape[:-1], out.shape[-1])

    def _L1_xattn_ref(src, dst, mask, Wq, Wk, Wv, Wo, rel_bias):
        import math
        import jax, jax.numpy as jnp
        import numpy as np
        NUM_BUCKETS = 32
        MAX_DISTANCE = 128
        H = 16
        D_MODEL = 128
        D_K = D_MODEL // H

        def _relative_position_bucket(relative_position):
            nb = NUM_BUCKETS // 2
            buckets = (relative_position > 0).astype(jnp.int32) * nb
            rp = jnp.abs(relative_position)
            max_exact = nb // 2
            is_small = rp < max_exact
            rp_large = max_exact + (jnp.log(jnp.maximum(rp, 1).astype(jnp.float32) / max_exact) / math.log(MAX_DISTANCE / max_exact) * (nb - max_exact)).astype(jnp.int32)
            rp_large = jnp.minimum(rp_large, nb - 1)
            return buckets + jnp.where(is_small, rp, rp_large)
        B, T_k, _ = src.shape
        T_q = dst.shape[1]
        q = (dst @ Wq.T).reshape(B, T_q, H, D_K)
        k = (src @ Wk.T).reshape(B, T_k, H, D_K)
        v = (src @ Wv.T).reshape(B, T_k, H, D_K)
        scores = jnp.einsum('bqhd,bkhd->bhqk', q, k)
        rel_pos = jnp.arange(T_k)[None, :] - jnp.arange(T_q)[:, None]
        rp_bucket = _relative_position_bucket(rel_pos)
        bias = rel_bias[:, rp_bucket]
        scores = scores + bias[None]
        scores = jnp.where(mask, scores, -1000000000.0)
        attn = jax.nn.softmax(scores, axis=-1)
        out = jnp.einsum('bhqk,bkhd->bqhd', attn, v).reshape(B, T_q, H * D_K)
        return out @ Wo.T

    def _L1_ffn_ref(x, gate_w, w1, b1, w2, b2, sw1, sb1, sw2, sb2):
        import jax, jax.numpy as jnp
        import numpy as np
        D_MODEL = 128
        HIDDEN = 512
        N_ROUTING = 2
        B, S, D = x.shape
        xf = x.reshape(-1, D)
        gate_scores = xf @ gate_w.T
        gate_probs = jax.nn.softmax(gate_scores, axis=-1)
        top1 = jnp.argmax(gate_probs, axis=-1)
        one_hot = jax.nn.one_hot(top1, N_ROUTING, dtype=xf.dtype)
        masked = xf[None, :, :] * one_hot.T[:, :, None]
        h = jax.nn.relu(jnp.einsum('end,edh->enh', masked, w1) + b1[:, None, :])
        expert_out = jnp.einsum('enh,ehd->end', h, w2) + b2[:, None, :]
        routing_output = expert_out.sum(axis=0)
        shared = jax.nn.relu(xf @ sw1 + sb1) @ sw2 + sb2
        return (routing_output + shared).reshape(B, S, D)

    def _L2_xattn_ref(query, key, value, mask, Wq, bq, Wk, bk, Wv, bv, Wo, bo):
        import jax, jax.numpy as jnp
        import numpy as np
        E = 128
        H = 16
        DH = E // H
        EPS = 1e-09

        def _split_heads(x):
            B, S, _ = x.shape
            return x.reshape(B, S, H, DH).transpose(0, 2, 1, 3)
        q = _split_heads(query @ Wq.T + bq)
        k = _split_heads(key @ Wk.T + bk)
        v = _split_heads(value @ Wv.T + bv)
        scores = jnp.einsum('bhqd,bhkd->bhqk', q, k) / np.sqrt(DH)
        scores = jnp.where(mask == 0, jnp.float32(EPS), scores)
        out = jnp.einsum('bhqk,bhkd->bhqd', scores, v)
        B, _, S, _ = out.shape
        out = out.transpose(0, 2, 1, 3).reshape(B, S, E)
        return out @ Wo.T + bo

    def _L2_ffn_ref(x, router_w, routing_bias, sw1, sw2, sw3, ew1, ew2, ew3):
        import jax, jax.numpy as jnp
        import numpy as np
        B, T, C, I, E = (4, 256, 128, 352, 7)

        def _swiglu(h, w1, w2, w3):
            return jax.nn.silu(h @ w1.T) * (h @ w3.T) @ w2.T
        b, t, c = x.shape
        shared_out = _swiglu(x, sw1, sw2, sw3)
        logits = jnp.clip(x @ router_w.T + routing_bias, -50.0, 50.0)
        probs = jax.nn.sigmoid(logits)
        num_switched = 1
        topk_probs, topk_idx = jax.lax.top_k(probs, num_switched)
        topk_probs = jnp.clip(topk_probs, 1e-08, 1.0 - 1e-08)
        xf = x.reshape(-1, c)
        sel = topk_idx.reshape(-1)
        p = topk_probs.reshape(-1)
        switched = jnp.zeros_like(xf)
        n_experts = ew1.shape[0]
        for e in range(n_experts):
            y = _swiglu(xf, ew1[e], ew2[e], ew3[e])
            w = jnp.where(sel == e, p, 0.0)
            switched = switched + w[:, None] * y
        switched = switched.reshape(b, t, c)
        total_weight = 0.5 + topk_probs.sum(axis=-1)
        total_weight = jnp.clip(total_weight[..., None] + 1e-08, 0.5, 2.0)
        return 0.5 / total_weight * shared_out + switched / total_weight

    def _L3_xattn_ref(q, k, v, mask, gamma, beta):
        import jax, jax.numpy as jnp
        import numpy as np
        NEG = -9000000000000000.0
        EPS = 1e-05
        d_k = q.shape[-1]
        logits = jnp.einsum('bsd,btd->bst', q, k) / jnp.sqrt(jnp.asarray(d_k, q.dtype))
        logits = jnp.where(mask == 0, jnp.asarray(NEG, logits.dtype), logits)
        attn = jax.nn.softmax(logits, axis=-1)
        x = jnp.einsum('bst,btd->bsd', attn, v)
        mu = jnp.mean(x, axis=-1, keepdims=True)
        var = jnp.mean(jnp.square(x - mu), axis=-1, keepdims=True)
        xhat = (x - mu) * jax.lax.rsqrt(var + EPS)
        return xhat * gamma + beta

    def _L3_ffn_ref(hidden_states, Wq, bq, Wk, bk, Wv, bv, Wg1, bg1, Wg2, bg2, Wo, bo):
        import jax, jax.numpy as jnp
        import numpy as np
        N_HEADS = 16
        NUM_EXPERTS = 4
        TOP_K = 2
        D_MODEL = 128
        GATE_HID = 128
        B, T, C = hidden_states.shape
        H = N_HEADS
        D = C // H
        pooled = hidden_states.mean(axis=1)
        logits = jax.nn.relu(pooled @ Wg1 + bg1) @ Wg2 + bg2
        vals, idx = jax.lax.top_k(logits, TOP_K)
        sm = jax.nn.softmax(vals, axis=-1)
        weights = jnp.zeros_like(logits).at[jnp.arange(B)[:, None], idx].set(sm)

        def moe_proj(W, b):
            Wc = jnp.einsum('be,ecd->bcd', weights, W)
            bc = weights @ b
            return jnp.einsum('btc,bcd->btd', hidden_states, Wc) + bc[:, None, :]
        q = moe_proj(Wq, bq).reshape(B, T, H, D)
        k = moe_proj(Wk, bk).reshape(B, T, H, D)
        v = moe_proj(Wv, bv).reshape(B, T, H, D)
        scores = jnp.einsum('bthd,bshd->bhts', q, k) / np.sqrt(D).astype(np.float32)
        attn = jax.nn.softmax(scores, axis=-1)
        out = jnp.einsum('bhts,bshd->bthd', attn, v).reshape(B, T, C)
        return out @ Wo + bo
    x = x + _L0_xattn_ref(_layernorm(x, axis=-1), ctx_1024, ctx_1024, mask_Bx1xSxS2_if1, L0_xattn_W_q, L0_xattn_b_q, L0_xattn_W_k, L0_xattn_b_k, L0_xattn_W_v, L0_xattn_b_v, L0_xattn_W_o, L0_xattn_b_o)
    x = x + _L0_ffn_ref(_layernorm(x, axis=-1), L0_ffn_gate_w, L0_ffn_gate_b, L0_ffn_expert_w, L0_ffn_expert_b)
    x = x + _L1_xattn_ref(ctx_1024, _layernorm(x, axis=-1), mask_Bx1x1xS2_bk0, L1_xattn_Wq, L1_xattn_Wk, L1_xattn_Wv, L1_xattn_Wo, L1_xattn_rel_bias)
    x = x + _L1_ffn_ref(_layernorm(x, axis=-1), L1_ffn_gate_w, L1_ffn_w1, L1_ffn_b1, L1_ffn_w2, L1_ffn_b2, L1_ffn_sw1, L1_ffn_sb1, L1_ffn_sw2, L1_ffn_sb2)
    x = x + _L2_xattn_ref(_layernorm(x, axis=-1), ctx_1024, ctx_1024, mask_Bx1xSxS2_ik1, L2_xattn_Wq, L2_xattn_bq, L2_xattn_Wk, L2_xattn_bk, L2_xattn_Wv, L2_xattn_bv, L2_xattn_Wo, L2_xattn_bo)
    x = x + _L2_ffn_ref(_layernorm(x, axis=-1), L2_ffn_router_w, L2_ffn_routing_bias, L2_ffn_sw1, L2_ffn_sw2, L2_ffn_sw3, L2_ffn_ew1, L2_ffn_ew2, L2_ffn_ew3)
    x = x + _L3_xattn_ref(_layernorm(x, axis=-1), ctx_1024, ctx_1024, mask_BxSxS2_ik1, L3_xattn_gamma, L3_xattn_beta)
    x = x + _L3_ffn_ref(_layernorm(x, axis=-1), L3_ffn_Wq, L3_ffn_bq, L3_ffn_Wk, L3_ffn_bk, L3_ffn_Wv, L3_ffn_bv, L3_ffn_Wg1, L3_ffn_bg1, L3_ffn_Wg2, L3_ffn_bg2, L3_ffn_Wo, L3_ffn_bo)
    return x

_drawn_inputs = setup_inputs


def setup_inputs(seed=0):
    import zlib

    import numpy as np

    out = dict(_drawn_inputs(seed))
    spreads = {'L0_xattn_b_q': (0.0, 0.355),
     'L0_xattn_b_k': (0.0, 2.0),
     'L0_xattn_b_v': (0.0, 0.1),
     'L0_xattn_b_o': (0.0, 0.1),
     'L0_ffn_gate_b': (0.0, 0.301),
     'L0_ffn_expert_b': (0.0, 0.1),
     'L2_xattn_bq': (0.0, 0.1),
     'L2_xattn_bk': (0.0, 0.1),
     'L2_xattn_bv': (0.0, 0.1),
     'L2_xattn_bo': (0.0, 0.8),
     'L2_ffn_routing_bias': (0.0, 0.8),
     'L3_xattn_gamma': (1.0, 0.6),
     'L3_xattn_beta': (0.0, 2.0),
     'L3_ffn_bq': (0.0, 2.0),
     'L3_ffn_bk': (0.0, 2.0),
     'L3_ffn_bv': (0.0, 2.0),
     'L3_ffn_bg1': (0.0, 2.0),
     'L3_ffn_bg2': (0.0, 2.0),
     'L3_ffn_bo': (0.0, 2.0)}
    factors = {'L1_xattn_rel_bias': 2.823,
     'L1_ffn_b1': 8.0,
     'L1_ffn_sb1': 8.0,
     'L1_ffn_sb2': 3.411,
     'L2_ffn_router_w': 3.29,
     'L2_ffn_sw1': 5.18,
     'L2_ffn_sw2': 4.84,
     'L2_ffn_sw3': 4.833,
     'L2_ffn_ew1': 3.278,
     'L2_ffn_ew2': 3.083,
     'L2_ffn_ew3': 3.088,
     'L3_ffn_Wq': 21.495,
     'L3_ffn_Wk': 8.0,
     'L3_ffn_Wg1': 4.487,
     'L3_ffn_Wg2': 3.437}
    for name, (base, spread) in spreads.items():
        noise = np.random.default_rng([zlib.crc32(name.encode()), seed]).standard_normal(out[name].shape)
        drawn = base * np.exp(spread * noise) if base else spread * noise
        out[name] = jnp.asarray(drawn.astype(out[name].dtype))
    for name, factor in factors.items():
        out[name] = (out[name] * factor).astype(out[name].dtype)
    return out
```

```python
from contextlib import ExitStack
import math

import numpy as np
import concourse.bass as bass
from concourse import mybir

ALU = mybir.AluOpType
ACT = mybir.ActivationFunctionType
AX = mybir.AxisListType
F32 = mybir.dt.float32
F32R = mybir.dt.float32r
BF16 = mybir.dt.bfloat16
I32 = mybir.dt.int32
U8 = mybir.dt.uint8

P = 128
S = 64
B2 = 2
H = 16
DH = P // H
RING = 4
EPS = 1e-5
MASKED = -(2.0 ** 100)


def wait(eng, sem, n, last=None):
    if isinstance(n, int):
        if last is not None:
            n = min(n, last)
        if n <= 0:
            return
    eng.wait_ge(sem, n)


def run_steps(eng, count, depth, ring, step):
    head = depth + ring
    assert depth % ring == 0 and (count - head) % ring == 0 and count >= head
    for i in range(head):
        step(i, i % ring)
    if count > head:
        with eng.Fori(0, (count - head) // ring) as turn:
            for r in range(ring):
                step(turn * ring + (head + r), r)
    for i in range(count, count + depth):
        step(i, i % ring)


def rel_bucket(rp, buckets=32, max_distance=128):
    nb = buckets // 2
    out = (rp > 0).astype(np.int32) * nb
    rp = np.abs(rp)
    exact = nb // 2
    large = exact + (np.log(np.maximum(rp, 1).astype(np.float32) / np.float32(exact))
                     / np.float32(math.log(max_distance / exact)) * np.float32(nb - exact)).astype(np.int32)
    return out + np.where(rp < exact, rp, np.minimum(large, nb - 1))


class Core:
    pass


def allocate(c, nc, ctx, NT):
    c.nc, c.NT = nc, NT
    c.sb = lambda name, shape, dt=F32: ctx.enter_context(nc.sbuf_tensor(name, shape, dt))
    c.x = c.sb("x_all", [P, NT, P])
    c.stats = c.sb("ln_stats", [P, NT, 6])
    c.rstd = c.sb("ln_rstd", [P, NT])
    c.nmr = c.sb("ln_neg_mean_rstd", [P, NT])
    c.ln_tmp = c.sb("ln_tmp", [P, 3, NT])
    c.ident = c.sb("ident", [P, P])
    c.ident_bf = c.sb("ident_bf", [P, P], BF16)
    c.head_of_row = c.sb("head_of_row", [P, 4])
    c.ones_row = c.sb("ones_row", [1, P])


def build_constants(c, sems):
    with ExitStack() as ctx:
        block = ctx.enter_context(c.nc.Block())
        made = sems("const_made")

        @block.gpsimd
        def _(pool):
            n = 0

            def made_next(instruction):
                nonlocal n
                n += 1
                instruction.then_inc(made, 1)
                pool.wait_ge(made, n)

            made_next(pool.memset(c.ident[:, :], 0.0))
            made_next(pool.memset(c.head_of_row[:, :], 1.0))
            made_next(pool.memset(c.ones_row[:, :], 1.0))
            made_next(pool.affine_select(out=c.ident[:, :], in_=c.ident[:, :], compare_op=ALU.not_equal, fill=1.0,
                                         base=0, pattern=[[-1, P]], channel_multiplier=1))
            made_next(pool.tensor_copy(c.ident_bf[:, :], c.ident[:, :]))
            for g in range(4):
                part = c.head_of_row[32 * g:32 * g + 32, :]
                made_next(pool.affine_select(out=part, in_=part, compare_op=ALU.is_ge, fill=0.0,
                                             base=0, pattern=[[-8, 4]], channel_multiplier=1))
                made_next(pool.affine_select(out=part, in_=part, compare_op=ALU.is_ge, fill=0.0,
                                             base=7, pattern=[[8, 4]], channel_multiplier=-1))


def load_weights(c, parts, sems):
    with ExitStack() as ctx:
        block = ctx.enter_context(c.nc.Block())
        s_sp, s_act = sems("weights_sp"), sems("weights_act")
        half = (len(parts) + 1) // 2

        @block.sync
        def _(sp):
            for dst, src in parts[:half]:
                sp.dma_start(dst, src).then_inc(s_sp, 16)
            sp.wait_ge(s_sp, 16 * half)

        @block.scalar
        def _(act):
            for dst, src in parts[half:]:
                act.dma_start(dst, src).then_inc(s_act, 16)
            if parts[half:]:
                act.wait_ge(s_act, 16 * (len(parts) - half))


def load_x(c, x_dram, sems):
    NT = c.NT
    CH = 8
    with ExitStack() as ctx:
        block = ctx.enter_context(c.nc.Block())
        landed = [sems(f"x_landed{q}") for q in range(NT // CH)]
        stats_made = sems("x_stats_made")

        @block.sync
        def _(sp):
            for q in range(NT // CH):
                sp.dma_start(c.x[:, q * CH:(q + 1) * CH, :],
                             x_dram[q * CH * P:(q + 1) * CH * P, :].rearrange("(t p) d -> p t d", p=P)
                             ).then_inc(landed[q], 16)

        @block.vector
        def _(dve):
            for q in range(NT // CH):
                dve.wait_ge(landed[q], 16)
                for t in range(q * CH, (q + 1) * CH):
                    dve.bn_stats(c.stats[:, t, :], c.x[:, t, :]).then_inc(stats_made, 1)
            dve.wait_ge(stats_made, NT)


def layernorm_scales(c, name, sems):
    with ExitStack() as ctx:
        block = ctx.enter_context(c.nc.Block())
        step, var_made, root_made = sems(name + "_ln"), sems(name + "_var"), sems(name + "_root")
        st = c.stats
        mean_e, m2_e, mean_o, m2_o = st[:, :, 1], st[:, :, 2], st[:, :, 4], st[:, :, 5]
        mean, diff, var = c.ln_tmp[:, 0, :], c.ln_tmp[:, 1, :], c.ln_tmp[:, 2, :]

        @block.vector
        def _(dve):
            dve.tensor_tensor(mean, mean_e, mean_o, ALU.add).then_inc(step, 1)
            dve.tensor_tensor(diff, mean_e, mean_o, ALU.subtract).then_inc(step, 1)
            dve.tensor_tensor(var, m2_e, m2_o, ALU.add).then_inc(step, 1)
            dve.wait_ge(step, 3)
            dve.scalar_tensor_tensor(out=diff, in0=diff, scalar=P / 4.0, in1=diff,
                                     op0=ALU.mult, op1=ALU.mult).then_inc(step, 1)
            dve.wait_ge(step, 4)
            dve.tensor_tensor(var, var, diff, ALU.add).then_inc(step, 1)
            dve.wait_ge(step, 5)
            dve.tensor_scalar(var, var, 1.0 / P, EPS, ALU.mult, ALU.add).then_inc(var_made, 1)
            dve.wait_ge(root_made, 1)
            dve.reciprocal(c.rstd[:, :], diff).then_inc(step, 1)
            dve.wait_ge(step, 6)
            dve.scalar_tensor_tensor(out=c.nmr[:, :], in0=mean, scalar=-0.5, in1=c.rstd[:, :],
                                     op0=ALU.mult, op1=ALU.mult).then_inc(step, 1)
            dve.wait_ge(step, 7)

        @block.scalar
        def _(act):
            act.wait_ge(var_made, 1)
            act.activation(diff, var, ACT.Sqrt).then_inc(root_made, 1)


def attention(c, name, sems, w, linear=False, mask=None, key_mask=False, rel=None, scale=1.0,
              ctxT=None, q_bias=None, k_bias=None, v_bias_col=None, v_bias_row=None, out_bias=None,
              moe=None):
    nc, NT = c.nc, c.NT
    DEPTH = 8
    NE = 4 if moe else 1
    masked = mask is not None
    with ExitStack() as ctx:
        sb = lambda n, shape, dt=F32: ctx.enter_context(nc.sbuf_tensor(f"{name}_{n}", shape, dt))
        pb = lambda n, shape: ctx.enter_context(nc.psum_tensor(f"{name}_{n}", shape, F32))
        sem = lambda n: sems(f"{name}_{n}")
        xhat = sb("xhat", [P, RING, NE, P])
        xT = sb("xT", [P, RING, NE, P])
        ctx_sb = None if moe else sb("ctxT", [P, RING, P])
        still = sb("still", [P, RING, P])
        flat = sb("flat", [P, RING, P])
        wide = sb("wide", [P, RING, B2, 4, S])
        Pr = sb("probs", [P, 2, H, S])
        On = sb("On", [P, RING, P])
        oT = sb("oT", [P, RING, P])
        less = sb("less_max", [P, 2, H, S])
        PT = sb("probs_T", [P, 2, 8, P])
        Vb = sb("Vblk", [P, RING, B2, 8, 2, DH + 1])
        mx = sb("mx", [P, RING, H])
        rden = sb("rden", [P, RING, H])
        if masked:
            M_raw = sb("mask_raw", [P, RING, S], U8 if key_mask else I32)
            if linear:
                keep = sb("keep", [P, RING, S])
                fill = sb("fill", [P, RING, S])
            else:
                Mb = sb("mask_bias", [P, RING, S], BF16)

        psS = pb("S", [P, 1024])
        psPT = pb("PT", [P, 1024])
        psT = pb("T", [P, 512])
        psQKV = pb("QKV", [P, 512])
        psO = pb("O", [P, 512])
        psOY = pb("OY", [P, 512])

        ctx_loaded = [] if moe else [sem(f"ctx_loaded{r}") for r in range(RING)]
        mask_loaded = [sem(f"mask_loaded{r}") for r in range(RING)] if masked else []
        xn_made = sem("xn_made") if moe else None
        xhat_made, xT_done, xT_kept = sem("xhat_made"), sem("xT_done"), sem("xT_kept")
        qk_done, qk_kept, v_done, v_kept = sem("qk_done"), sem("qk_kept"), sem("v_done"), sem("v_kept")
        wide_made, mask_made, s_rows, s_done = sem("wide_made"), sem("mask_made"), sem("s_rows"), sem("s_done")
        max_made, less_made, p_made = sem("max_made"), sem("less_made"), sem("p_made")
        pt0_done, pt1_done, pt0_kept, pt1_kept = sem("pt0_done"), sem("pt1_done"), sem("pt0_kept"), sem("pt1_kept")
        o_done, rden_made, on_made = sem("o_done"), sem("rden_made"), sem("on_made")
        oT_done, oT_kept, y_done = sem("oT_done"), sem("oT_kept"), sem("y_done")
        x_based, x_summed, stats_made, zeroed = sem("x_based"), sem("x_summed"), sem("stats_made"), sem("zeroed")

        def at(i, r, lag):
            u = i - lag
            if not isinstance(u, int) or 0 <= u < NT:
                yield u, (r - lag) % RING

        def turns(u, s, n):
            return (u - s) * (n // RING) + n

        block = ctx.enter_context(nc.Block())

        @block.sync
        def _(sp):
            def step(i, r):
                for u, s in at(i, r, 0):
                    if not moe:
                        wait(sp, v_done, u - 3)
                        sp.dma_start(ctx_sb[:, s, :], ctxT[:, bass.ds(u * P, P)]).then_inc(ctx_loaded[s], 16)
                    if masked:
                        wait(sp, mask_made, u - 3)
                        if key_mask:
                            for b in range(B2):
                                sp.dma_start(M_raw[S * b:S * b + S, s, :],
                                             mask[bass.ds(u * B2 + b, 1), :].broadcast_to([S, S])
                                             ).then_inc(mask_loaded[s], 16)
                        else:
                            sp.dma_start(M_raw[:, s, :], mask[bass.ds(u * P, P), :]).then_inc(mask_loaded[s], 16)
            if not moe or masked:
                run_steps(sp, NT, DEPTH, RING, step)

        @block.gpsimd
        def _(pool):
            pool.memset(Vb[:, :, :, :, :, :], 0.0).then_inc(zeroed, 1)
            pool.wait_ge(zeroed, 1)
            pool.memset(Vb[0:S, :, :, :, 0, DH:DH + 1], 1.0).then_inc(zeroed, 1)
            pool.memset(Vb[S:P, :, :, :, 1, DH:DH + 1], 1.0).then_inc(zeroed, 1)
            pool.wait_ge(zeroed, 3)

            def step(i, r):
                if linear:
                    for u, s in at(i, r, 4):
                        wait(pool, less_made, u + 1)
                        wait(pool, pt1_done, u - 1)
                        pool.tensor_tensor(Pr[:, s % 2], less[:, s % 2],
                                           fill[:, s, :].unsqueeze(1).broadcast_to([P, H, S]), ALU.add
                                           ).then_inc(p_made, 1)
                for u, s in at(i, r, 3):
                    wait(pool, qk_kept, u + 1)
                    wait(pool, s_done, u - 3)
                    pool.tensor_tensor(
                        wide[:, s],
                        flat[:, s, :].rearrange("p (b n) -> p b n", b=B2).unsqueeze(2).broadcast_to([P, B2, 4, S]),
                        c.head_of_row[:, :].unsqueeze(1).unsqueeze(3).broadcast_to([P, B2, 4, S]),
                        ALU.mult).then_inc(wide_made, 1)
            run_steps(pool, NT, DEPTH, RING, step)

        @block.tensor
        def _(pe):
            def step(i, r):
                for u, s in at(i, r, 4):
                    wait(pe, wide_made, u + 1)
                    wait(pe, less_made, u)
                    if masked and not linear:
                        wait(pe, mask_made, u + 1)
                        for hb in range(2):
                            pe.matmul(psS[:, 512 * hb:512 * hb + 512], c.ident_bf[:, :],
                                      Mb[:, s, :].unsqueeze(1).broadcast_to([P, 8, S]),
                                      start=True, stop=True, skip_group_check=True)
                    if rel is not None:
                        for hb in range(2):
                            for part in ("hi", "lo"):
                                pe.matmul(psS[:, 512 * hb:512 * hb + 512], rel["flip"][:, :],
                                          rel[part][:, 8 * hb:8 * hb + 8, :].rearrange("p h k -> p (h k)"),
                                          start=False, stop=True, skip_group_check=True)
                    for order, g in enumerate((0, 2, 1, 3)):
                        if order >= 2:
                            pe.wait_ge(s_rows, 2 * u + order - 1)
                        for b in range(B2):
                            mm = pe.matmul(psS[S * b:S * b + S, 256 * g:256 * g + 256],
                                           still[32 * g:32 * g + 32, s, S * b:S * b + S],
                                           wide[32 * g:32 * g + 32, s, b].rearrange("p j n -> p (j n)"),
                                           start=order < 2 and (linear or not masked), stop=True,
                                           skip_group_check=True)
                        if order < 2:
                            mm.then_inc(s_rows, 1)
                    mm.then_inc(s_done, 1)
                for u, s in at(i, r, 4):
                    wait(pe, qk_kept, u + 2, NT)
                    wait(pe, v_kept, u)
                    for b in range(B2):
                        for h in range(2):
                            o = psQKV[S * h:S * h + S, 256 + S * b:256 + S * b + S].rearrange("p (g d) -> p g d", d=DH)
                            for e in range(NE):
                                src = xT[:, s, e, :] if moe else ctx_sb[:, s, :]
                                mm = pe.matmul(o, src[:, b * S:b * S + S],
                                               w["v"][:, e, :].rearrange("k (g h d) -> k g h d", g=8, h=2)[:, :, h, :],
                                               start=b == 0 and e == 0, stop=e == NE - 1, skip_group_check=True)
                            if v_bias_row is not None:
                                mm = pe.matmul(o, c.ones_row[:, 0:S],
                                               v_bias_row[:, :].rearrange("k (g h d) -> k g h d", g=8, h=2)[:, :, h, :],
                                               start=False, stop=True, skip_group_check=True)
                    mm.then_inc(v_done, 1)
                for u, s in at(i, r, 1):
                    wait(pe, xhat_made, u + 1)
                    wait(pe, xT_kept, u)
                    for e in range(NE):
                        mm = pe.transpose(psT[:, P * e:P * e + P], xhat[:, s, e, :], c.ident[:, :])
                    mm.then_inc(xT_done, 1)
                for u, s in at(i, r, 7):
                    wait(pe, on_made, u + 1)
                    wait(pe, x_summed, u - 1)
                    pe.transpose(psOY[:, 0:P], On[:, s, :], c.ident[:, :]).then_inc(oT_done, 1)
                for u, s in at(i, r, 5):
                    wait(pe, p_made, u + 1)
                    for half, (kept, done) in enumerate(((pt0_kept, pt0_done), (pt1_kept, pt1_done))):
                        wait(pe, kept, u)
                        for gj in range(4 * half, 4 * half + 4):
                            mm = pe.transpose(psPT[:, P * gj:P * gj + P],
                                              Pr[:, s % 2, 2 * gj:2 * gj + 2, :].rearrange("p h k -> p (h k)"),
                                              c.ident[:, :])
                        mm.then_inc(done, 1)
                for u, s in at(i, r, 2):
                    wait(pe, xT_kept, u + 1)
                    wait(pe, qk_kept, u)
                    wait(pe, v_kept, u - 1)
                    if not moe:
                        wait(pe, ctx_loaded[s], turns(u, s, 16))
                    for o, key in ((0, "q"), (P, "k")):
                        for e in range(NE):
                            src = ctx_sb[:, s, :] if key == "k" and not moe else xT[:, s, e, :]
                            mm = pe.matmul(psQKV[:, o:o + P], w[key][:, e, :], src,
                                           start=o == 0 and e == 0, stop=e == NE - 1, skip_group_check=True)
                    mm.then_inc(qk_done, 1)
                for u, s in at(i, r, 8):
                    wait(pe, oT_kept, u + 2, NT)
                    wait(pe, x_summed, u)
                    pe.matmul(psOY[:, P:2 * P], oT[:, s, :], w["o"][:, :], start=True, stop=True
                              ).then_inc(y_done, 1)
                for u, s in at(i, r, 6):
                    wait(pe, on_made, u)
                    wait(pe, v_kept, u + 1)
                    wait(pe, pt0_kept, u + 1)
                    wait(pe, pt1_kept, u + 1)
                    for b in range(B2):
                        for gj in range(8):
                            mm = pe.matmul(psO[S * b:S * b + S, 18 * gj:18 * gj + 18],
                                           PT[:, s % 2, gj, S * b:S * b + S],
                                           Vb[:, s, b, gj].rearrange("p h d -> p (h d)"),
                                           start=gj == 0, stop=True, skip_group_check=True)
                    mm.then_inc(o_done, 1)
            run_steps(pe, NT, DEPTH, RING, step)

        @block.scalar
        def _(act):
            act.wait_ge(zeroed, 3)

            def step(i, r):
                for u, s in at(i, r, 4):
                    wait(act, v_done, u + 1)
                    wait(act, o_done, u - 3)
                    for h in range(2):
                        last = act.activation(
                            Vb[S * h:S * h + S, s, :, :, h, 0:DH],
                            psQKV[S * h:S * h + S, 256:384].rearrange("p (b g d) -> p b g d", b=B2, g=8), ACT.Copy)
                    last.then_inc(v_kept, 1)
                for u, s in at(i, r, 1):
                    wait(act, xT_done, u + 1)
                    wait(act, v_done if moe else qk_done, u - 3)
                    act.activation(xT[:, s].rearrange("p e n -> p (e n)"), psT[:, 0:P * NE], ACT.Copy
                                   ).then_inc(xT_kept, 1)
                for u, s in at(i, r, 7):
                    wait(act, oT_done, u + 1)
                    wait(act, y_done, u - 3)
                    if moe:
                        for b in range(B2):
                            last = act.activation(oT[:, s, S * b:S * b + S], psOY[:, S * b:S * b + S], ACT.Identity,
                                                  bias=moe["v_bias"][:, bass.ds(B2 * u + b, 1)])
                        last.then_inc(oT_kept, 1)
                    elif v_bias_col is not None:
                        act.activation(oT[:, s, :], psOY[:, 0:P], ACT.Identity, bias=v_bias_col).then_inc(oT_kept, 1)
                    else:
                        act.activation(oT[:, s, :], psOY[:, 0:P], ACT.Copy).then_inc(oT_kept, 1)
                for u, s in at(i, r, 5):
                    wait(act, pt0_done, u + 1)
                    wait(act, o_done, u - 1)
                    act.activation(PT[:, s % 2, 0:4, :].rearrange("p g n -> p (g n)"), psPT[:, 0:512], ACT.Copy
                                   ).then_inc(pt0_kept, 1)
                for u, s in at(i, r, 2):
                    wait(act, qk_done, u + 1)
                    wait(act, s_done, u - 3)
                    wait(act, wide_made, u - 3)
                    qd, kd = still, flat
                    if moe:
                        for b in range(B2):
                            cols = slice(S * b, S * b + S)
                            act.activation(qd[:, s, cols], psQKV[:, cols], ACT.Identity, scale=scale,
                                           bias=moe["q_bias"][:, bass.ds(B2 * u + b, 1)])
                            last = act.activation(kd[:, s, cols], psQKV[:, P + S * b:P + S * b + S], ACT.Identity,
                                                  bias=moe["k_bias"][:, bass.ds(B2 * u + b, 1)])
                        last.then_inc(qk_kept, 1)
                    elif q_bias is not None:
                        act.activation(qd[:, s, :], psQKV[:, 0:P], ACT.Identity, scale=scale, bias=q_bias)
                        act.activation(kd[:, s, :], psQKV[:, P:2 * P], ACT.Identity, bias=k_bias).then_inc(qk_kept, 1)
                    else:
                        act.activation(qd[:, s, :], psQKV[:, 0:P], ACT.Copy)
                        act.activation(kd[:, s, :], psQKV[:, P:2 * P], ACT.Copy).then_inc(qk_kept, 1)
                if not linear:
                    for u, s in at(i, r, 4):
                        wait(act, less_made, u + 1)
                        wait(act, pt1_done, u - 1)
                        act.activation(Pr[:, s % 2].rearrange("p h n -> p (h n)"),
                                       less[:, s % 2].rearrange("p h n -> p (h n)"), ACT.Exp).then_inc(p_made, 1)
            run_steps(act, NT, DEPTH, RING, step)

        @block.vector
        def _(dve):
            def step(i, r):
                for u, s in at(i, r, 4):
                    wait(dve, s_done, u + 1)
                    S3 = psS[:, :].rearrange("p (h k) -> p h k", k=S)
                    if linear:
                        wait(dve, mask_made, u + 1)
                        wait(dve, p_made, u - 1)
                        dve.tensor_tensor(less[:, s % 2], S3, keep[:, s, :].unsqueeze(1).broadcast_to([P, H, S]),
                                          ALU.mult).then_inc(less_made, 1)
                    else:
                        dve.tensor_reduce(mx[:, s, :], S3, AX.X, ALU.max).then_inc(max_made, 1)
                        wait(dve, max_made, u + 1)
                        wait(dve, p_made, u - 1)
                        dve.tensor_tensor(less[:, s % 2], S3, mx[:, s, :].unsqueeze(2).broadcast_to([P, H, S]),
                                          ALU.subtract).then_inc(less_made, 1)
                for u, s in at(i, r, 0):
                    wait(dve, xT_done, u - 3)
                    if moe:
                        dve.tensor_scalar(moe["xn"][:, s, :], c.x[:, u, :], c.rstd[:, bass.ds(u, 1)],
                                          c.nmr[:, bass.ds(u, 1)], ALU.mult, ALU.add).then_inc(xn_made, 1)
                        wait(dve, xn_made, u + 1)
                        for e in range(NE):
                            last = dve.tensor_scalar(xhat[:, s, e, :], moe["xn"][:, s, :],
                                                     moe["w_tok"][:, u, e:e + 1], None, ALU.mult)
                        last.then_inc(xhat_made, 1)
                    else:
                        dve.tensor_scalar(xhat[:, s, 0, :], c.x[:, u, :], c.rstd[:, bass.ds(u, 1)],
                                          c.nmr[:, bass.ds(u, 1)], ALU.mult, ALU.add).then_inc(xhat_made, 1)
                    if out_bias is not None:
                        wait(dve, xhat_made, u + 1)
                        dve.tensor_tensor(c.x[:, u, :], c.x[:, u, :], out_bias, ALU.add).then_inc(x_based, 1)
                if masked:
                    for u, s in at(i, r, 2):
                        wait(dve, mask_loaded[s], turns(u, s, 32 if key_mask else 16))
                        if linear:
                            wait(dve, p_made, u - 3)
                            dve.tensor_scalar(keep[:, s], M_raw[:, s], 0.0, None, ALU.not_equal)
                            dve.tensor_scalar(fill[:, s], M_raw[:, s], 0.0, 1e-9, ALU.is_equal, ALU.mult
                                              ).then_inc(mask_made, 1)
                        else:
                            wait(dve, s_done, u - 3)
                            dve.tensor_scalar(Mb[:, s], M_raw[:, s], 0.0, MASKED, ALU.is_equal, ALU.mult
                                              ).then_inc(mask_made, 1)
                for u, s in at(i, r, 5):
                    wait(dve, pt1_done, u + 1)
                    wait(dve, o_done, u - 1)
                    dve.tensor_copy(PT[:, s % 2, 4:8, :].rearrange("p g n -> p (g n)"), psPT[:, 512:1024]
                                    ).then_inc(pt1_kept, 1)
                for u, s in at(i, r, 8):
                    wait(dve, y_done, u + 1)
                    if out_bias is not None:
                        wait(dve, x_based, u + 1)
                    dve.tensor_tensor(c.x[:, u, :], psOY[:, P:2 * P], c.x[:, u, :], ALU.add).then_inc(x_summed, 1)
                    wait(dve, x_summed, u + 1)
                    dve.bn_stats(c.stats[:, u, :], c.x[:, u, :]).then_inc(stats_made, 1)
                for u, s in at(i, r, 6):
                    wait(dve, o_done, u + 1)
                    wait(dve, oT_done, u - 3)
                    Ov = psO[:, 0:144].rearrange("p (h d) -> p h d", d=DH + 1)
                    if linear:
                        dve.tensor_copy(On[:, s, :].rearrange("p (h d) -> p h d", d=DH), Ov[:, :, 0:DH]
                                        ).then_inc(on_made, 1)
                    else:
                        dve.reciprocal(rden[:, s, :].unsqueeze(2), Ov[:, :, DH:DH + 1]).then_inc(rden_made, 1)
                        wait(dve, rden_made, u + 1)
                        dve.tensor_tensor(On[:, s, :].rearrange("p (h d) -> p h d", d=DH), Ov[:, :, 0:DH],
                                          rden[:, s, :].unsqueeze(2).broadcast_to([P, H, DH]), ALU.mult
                                          ).then_inc(on_made, 1)
            run_steps(dve, NT, DEPTH, RING, step)
            dve.wait_ge(stats_made, NT)


def split_weights(c, name, parts, sems):
    nc = c.nc
    with ExitStack() as ctx:
        staged = [ctx.enter_context(nc.sbuf_tensor(f"{name}_staged{i}", shape, F32))
                  for i, (shape, _, _, _) in enumerate(parts)]
        load_weights(c, [(pick(t), src) for t, (_, loads, _, _) in zip(staged, parts) for pick, src in loads],
                     lambda n: sems(f"{name}_{n}"))
        block = ctx.enter_context(nc.Block())
        hi_made, lo_made = sems(name + "_hi"), sems(name + "_lo")

        @block.scalar
        def _(act):
            for t, (shape, _, hi, lo) in zip(staged, parts):
                act.activation(hi, t[tuple(slice(None) for _ in shape)], ACT.Copy).then_inc(hi_made, 1)

        @block.vector
        def _(dve):
            for i, (t, (shape, _, hi, lo)) in enumerate(zip(staged, parts)):
                dve.wait_ge(hi_made, i + 1)
                dve.tensor_tensor(lo, t[tuple(slice(None) for _ in shape)], hi, ALU.subtract).then_inc(lo_made, 1)
            dve.wait_ge(lo_made, len(parts))


def products(pe, out, whi, wlo, xhi, xlo, first=True, last=True):
    pe.matmul(out, whi, xlo, start=first, stop=False, skip_group_check=True)
    pe.matmul(out, wlo, xhi, start=False, stop=False, skip_group_check=True)
    return pe.matmul(out, whi, xhi, start=False, stop=last, skip_group_check=True)


GT = 4
N4 = GT * P


class Front:

    def __init__(self, c, name, ctx, sems):
        nc = c.nc
        self.c = c
        self.xhat = ctx.enter_context(nc.sbuf_tensor(name + "_xhat", [P, 2, GT, P], F32))
        self.xh = ctx.enter_context(nc.sbuf_tensor(name + "_xh", [P, 2, N4], F32R))
        self.xl = ctx.enter_context(nc.sbuf_tensor(name + "_xl", [P, 2, N4], F32R))
        self.psT = ctx.enter_context(nc.psum_tensor(name + "_psT", [P, N4], F32))
        self.xhat_made, self.xT_done = sems(name + "_xhat_made"), sems(name + "_xT_done")
        self.hi_made, self.lo_made = sems(name + "_xh_made"), sems(name + "_xl_made")

    def vector_norm(self, dve, u, s):
        wait(dve, self.xT_done, u - 1)
        for k in range(GT):
            t = u * GT + k
            last = dve.tensor_scalar(self.xhat[:, s, k, :], self.c.x[:, t, :], self.c.rstd[:, bass.ds(t, 1)],
                                     self.c.nmr[:, bass.ds(t, 1)], ALU.mult, ALU.add)
        last.then_inc(self.xhat_made, 1)

    def tensor_transpose(self, pe, u, s):
        wait(pe, self.xhat_made, u + 1)
        wait(pe, self.lo_made, u)
        for k in range(GT):
            last = pe.transpose(self.psT[:, P * k:P * k + P], self.xhat[:, s, k, :], self.c.ident[:, :])
        last.then_inc(self.xT_done, 1)

    def scalar_hi(self, act, u, s):
        wait(act, self.xT_done, u + 1)
        act.activation(self.xh[:, s, :], self.psT[:, :], ACT.Copy).then_inc(self.hi_made, 1)

    def vector_lo(self, dve, u, s):
        wait(dve, self.hi_made, u + 1)
        dve.tensor_tensor(self.xl[:, s, :], self.psT[:, :], self.xh[:, s, :], ALU.subtract).then_inc(self.lo_made, 1)


def steps_of(NG):
    def at(i, r, lag):
        u = i - lag
        if not isinstance(u, int) or 0 <= u < NG:
            yield u, (r - lag) % 2
    return at


def gate_logits(c, name, sems, gate, bias, E):
    nc, NG = c.nc, c.NT // GT
    with ExitStack() as ctx:
        f = Front(c, name, ctx, sems)
        lT = ctx.enter_context(nc.sbuf_tensor(name + "_logitsT", [P, 2, N4], F32))
        psL = ctx.enter_context(nc.psum_tensor(name + "_psL", [P, N4], F32))
        psG = ctx.enter_context(nc.psum_tensor(name + "_psG", [P, N4], F32))
        l_done, l_kept = sems(name + "_l_done"), sems(name + "_l_kept")
        g_done, g_kept, cleared = sems(name + "_g_done"), sems(name + "_g_kept"), sems(name + "_cleared")
        block = ctx.enter_context(nc.Block())
        at = steps_of(NG)

        @block.vector
        def _(dve):
            def step(i, r):
                for u, s in at(i, r, 0):
                    f.vector_norm(dve, u, s)
                    wait(dve, l_done, u - 1)
                    f.vector_lo(dve, u, s)
                for u, s in at(i, r, 1):
                    wait(dve, g_done, u + 1)
                    dve.tensor_copy(c.logits[:, bass.ds(u * GT, GT), 0:E],
                                    psG[:, :].rearrange("p (t e) -> p t e", e=P)[:, :, 0:E]).then_inc(g_kept, 1)
            run_steps(dve, NG, 2, 2, step)
            dve.wait_ge(g_kept, NG)

        @block.gpsimd
        def _(pool):
            pool.memset(lT[:, :, :], 0.0).then_inc(cleared, 1)

        @block.scalar
        def _(act):
            act.wait_ge(cleared, 1)

            def step(i, r):
                for u, s in at(i, r, 0):
                    wait(act, l_done, u - 1)
                    f.scalar_hi(act, u, s)
                    wait(act, l_done, u + 1)
                    wait(act, g_done, u - 1)
                    act.activation(lT[0:E, s, :], psL[0:E, :], ACT.Identity, bias=bias).then_inc(l_kept, 1)
            run_steps(act, NG, 2, 2, step)

        @block.tensor
        def _(pe):
            def step(i, r):
                for u, s in at(i, r, 0):
                    f.tensor_transpose(pe, u, s)
                    wait(pe, f.lo_made, u + 1)
                    wait(pe, l_kept, u)
                    products(pe, psL[0:E, :], gate[0], gate[1], f.xh[:, s, :], f.xl[:, s, :]).then_inc(l_done, 1)
                for u, s in at(i, r, 0):
                    wait(pe, l_kept, u + 1)
                    wait(pe, g_kept, u)
                    for k in range(GT):
                        last = pe.transpose(psG[:, P * k:P * k + P], lT[:, s, P * k:P * k + P], c.ident[:, :])
                    last.then_inc(g_done, 1)
            run_steps(pe, NG, 2, 2, step)


def chain(eng, sem):
    n = 0

    def run(instruction):
        nonlocal n
        n += 1
        instruction.then_inc(sem, 1)
        eng.wait_ge(sem, n)
    return run


def soft_moe(c, name, sems, ew_hi, ew_lo, eb_blocks, E=8, THRESHOLD=0.1):
    nc, NT, NG = c.nc, c.NT, c.NT // GT
    with ExitStack() as ctx:
        block = ctx.enter_context(nc.Block())
        red = ctx.enter_context(nc.sbuf_tensor(name + "_red", [P, NT], F32))
        less, ex, step = sems(name + "_less"), sems(name + "_exp"), sems(name + "_gates")
        L = c.logits[:, :, 0:E]
        R = red[:, :].unsqueeze(2).broadcast_to([P, NT, E])

        @block.vector
        def _(dve):
            run = chain(dve, step)
            run(dve.tensor_reduce(red[:, :], L, AX.X, ALU.max))
            dve.tensor_tensor(L, L, R, ALU.subtract).then_inc(less, 1)
            dve.wait_ge(ex, 1)
            run(dve.tensor_reduce(red[:, :], L, AX.X, ALU.add))
            run(dve.reciprocal(red[:, :], red[:, :]))
            run(dve.tensor_tensor(L, L, R, ALU.mult))
            run(dve.scalar_tensor_tensor(out=L, in0=L, scalar=THRESHOLD, in1=L, op0=ALU.is_ge, op1=ALU.mult))
            run(dve.tensor_reduce(red[:, :], L, AX.X, ALU.add))
            run(dve.scalar_tensor_tensor(out=red[:, :], in0=red[:, :], scalar=0.0, in1=red[:, :],
                                         op0=ALU.is_equal, op1=ALU.add))
            run(dve.reciprocal(red[:, :], red[:, :]))
            run(dve.tensor_tensor(L, L, R, ALU.mult))

        @block.scalar
        def _(act):
            act.wait_ge(less, 1)
            act.activation(L, L, ACT.Exp).then_inc(ex, 1)

    with ExitStack() as ctx:
        f = Front(c, name, ctx, sems)
        wq = ctx.enter_context(nc.sbuf_tensor(name + "_w4", [P, 2, GT * E], F32))
        wT = ctx.enter_context(nc.sbuf_tensor(name + "_w4T", [GT * E, 2, P], F32))
        psE = ctx.enter_context(nc.psum_tensor(name + "_psE", [P, 2, E * P], F32))
        psW = ctx.enter_context(nc.psum_tensor(name + "_psW", [P, N4], F32))
        psB = ctx.enter_context(nc.psum_tensor(name + "_psB", [P, N4], F32))
        wq_made, wT_done, wT_kept = sems(name + "_w4_made"), sems(name + "_w4T_done"), sems(name + "_w4T_kept")
        bias_done, bias_summed = sems(name + "_bias_done"), sems(name + "_bias_summed")
        e_done, summed, stats_made = sems(name + "_e_done"), sems(name + "_summed"), sems(name + "_stats")
        block = ctx.enter_context(nc.Block())
        at = steps_of(NG)

        @block.tensor
        def _(pe):
            def step(i, r):
                for u, s in at(i, r, 0):
                    f.tensor_transpose(pe, u, s)
                    wait(pe, wq_made, u + 1)
                    wait(pe, wT_kept, u)
                    pe.transpose(psW[0:GT * E, 0:P], wq[:, s, :], c.ident[:, :]).then_inc(wT_done, 1)
                for u, s in at(i, r, 1):
                    wait(pe, wT_kept, u + 1)
                    wait(pe, bias_summed, u)
                    pe.matmul(psB[:, :], wT[:, s, :], eb_blocks, start=True, stop=True).then_inc(bias_done, 1)
                    wait(pe, f.lo_made, u + 1)
                    for k in range(GT):
                        t = u * GT + k
                        tok = slice(P * k, P * k + P)
                        wait(pe, summed, (t - 1) * E)
                        for half in range(2):
                            cols = slice(512 * half, 512 * half + 512)
                            out = psE[:, k % 2, cols]
                            pe.matmul(out, f.xl[:, s, tok], ew_hi[:, cols], start=True, stop=False,
                                      skip_group_check=True)
                            pe.matmul(out, f.xh[:, s, tok], ew_lo[:, cols], start=False, stop=False,
                                      skip_group_check=True)
                            mm = pe.matmul(out, f.xh[:, s, tok], ew_hi[:, cols], start=False, stop=True,
                                           skip_group_check=True)
                        mm.then_inc(e_done, 1)
            run_steps(pe, NG, 2, 2, step)

        @block.scalar
        def _(act):
            def step(i, r):
                for u, s in at(i, r, 0):
                    wait(act, e_done, (u - 1) * GT)
                    f.scalar_hi(act, u, s)
                    wait(act, wT_done, u + 1)
                    wait(act, bias_done, u - 1)
                    act.activation(wT[:, s, :], psW[0:GT * E, 0:P], ACT.Copy).then_inc(wT_kept, 1)
            run_steps(act, NG, 2, 2, step)

        @block.vector
        def _(dve):
            def step(i, r):
                for u, s in at(i, r, 0):
                    f.vector_norm(dve, u, s)
                    wait(dve, wT_done, u - 1)
                    dve.tensor_copy(wq[:, s, :].rearrange("p (t e) -> p t e", e=E),
                                    c.logits[:, bass.ds(u * GT, GT), 0:E]).then_inc(wq_made, 1)
                    wait(dve, e_done, (u - 1) * GT)
                    f.vector_lo(dve, u, s)
                for u, s in at(i, r, 1):
                    wait(dve, bias_done, u + 1)
                    dve.tensor_tensor(c.x[:, bass.ds(u * GT, GT), :],
                                      psB[:, :].rearrange("p (t d) -> p t d", d=P),
                                      c.x[:, bass.ds(u * GT, GT), :], ALU.add).then_inc(bias_summed, 1)
                    wait(dve, bias_summed, u + 1)
                    for k in range(GT):
                        t = u * GT + k
                        wait(dve, e_done, t + 1)
                        for e in range(E):
                            if e:
                                wait(dve, summed, t * E + e)
                            dve.scalar_tensor_tensor(out=c.x[:, t, :], in0=psE[:, k % 2, P * e:P * e + P],
                                                     scalar=c.logits[:, t, e:e + 1], in1=c.x[:, t, :],
                                                     op0=ALU.mult, op1=ALU.add).then_inc(summed, 1)
                        wait(dve, summed, t * E + E)
                        dve.bn_stats(c.stats[:, t, :], c.x[:, t, :]).then_inc(stats_made, 1)
            run_steps(dve, NG, 2, 2, step)
            dve.wait_ge(stats_made, NT)


def routed_relu(c, name, sems, gd, w1, b1, w2, out_bias, HC=4):
    nc, NT, NG = c.nc, c.NT, c.NT // GT
    UNITS = 3 * HC
    with ExitStack() as ctx:
        f = Front(c, name, ctx, sems)
        sb = lambda n, shape, dt=F32: ctx.enter_context(nc.sbuf_tensor(f"{name}_{n}", shape, dt))
        pb = lambda n, shape: ctx.enter_context(nc.psum_tensor(f"{name}_{n}", shape, F32))
        sem = lambda n: sems(f"{name}_{n}")
        eh, el = sb("eh", [P, 2, 2, N4], F32R), sb("el", [P, 2, 2, N4], F32R)
        h = sb("h", [P, 2, N4])
        hh, hl = sb("hh", [P, 2, N4], F32R), sb("hl", [P, 2, N4], F32R)
        ysb = sb("y", [P, 2, N4])
        psD, psH, psY, psO = pb("D", [P, N4]), pb("H", [P, 2, N4]), pb("Y", [P, 2, N4]), pb("O", [P, N4])
        d_done, masked = sem("d_done"), sem("masked")
        h_done, h_kept, hh_made, hl_made = sem("h_done"), sem("h_kept"), sem("hh_made"), sem("hl_made")
        used, y_done, y_kept, o_done = sem("used"), sem("y_done"), sem("y_kept"), sem("o_done")
        based, summed, stats_made, split0 = sem("based"), sem("summed"), sem("stats"), sem("split0")
        block = ctx.enter_context(nc.Block())
        at = steps_of(NG)

        @block.tensor
        def _(pe):
            def second(u, s, q):
                n = u * UNITS + q
                wait(pe, hl_made, n + 1)
                if q == 0:
                    wait(pe, y_kept, u - 1)
                mm = products(pe, psY[:, s, :], w2[0][:, q, :], w2[1][:, q, :], hh[:, q % 2, :], hl[:, q % 2, :],
                              first=q == 0, last=q == UNITS - 1)
                mm.then_inc(used, 1)

            def step(i, r):
                for q in range(UNITS):
                    for u, s in at(i, r, 1):
                        n = u * UNITS + q
                        if q == 0:
                            wait(pe, split0, u + 1)
                        wait(pe, h_kept, n - 1)
                        e = q // HC
                        xh, xl = (f.xh[:, s, :], f.xl[:, s, :]) if e == 2 else (eh[:, s, e, :], el[:, s, e, :])
                        products(pe, psH[:, q % 2, :], w1[0][:, q * P:q * P + P], w1[1][:, q * P:q * P + P],
                                 xh, xl).then_inc(h_done, 1)
                        if q >= 2:
                            second(u, s, q - 2)
                    for u, s in at(i, r, 2):
                        if q < 2:
                            second(u, s, q + UNITS - 2)
                        if q == 3:
                            wait(pe, y_kept, u + 1)
                            wait(pe, summed, u * GT)
                            for k in range(GT):
                                mm = pe.transpose(psO[:, P * k:P * k + P], ysb[:, s, P * k:P * k + P],
                                                  c.ident[:, :])
                            mm.then_inc(o_done, 1)
                    for u, s in at(i, r, 0):
                        if q == 5:
                            f.tensor_transpose(pe, u, s)
                        if q == 8:
                            wait(pe, f.lo_made, u + 1)
                            wait(pe, masked, 2 * u)
                            products(pe, psD[:, :], gd[0], gd[1], f.xh[:, s, :], f.xl[:, s, :]).then_inc(d_done, 1)
            run_steps(pe, NG, 2, 2, step)

        @block.scalar
        def _(act):
            def step(i, r):
                for q in range(UNITS):
                    for u, s in at(i, r, 1):
                        n = u * UNITS + q
                        wait(act, h_done, n + 1)
                        wait(act, hh_made, n - 1)
                        wait(act, hl_made, n - 1)
                        act.activation(h[:, q % 2, :], psH[:, q % 2, :], ACT.Relu, bias=b1[:, q:q + 1]
                                       ).then_inc(h_kept, 1)
                    for u, s in at(i, r, 2):
                        if q == 1:
                            wait(act, used, u * UNITS + UNITS)
                            wait(act, o_done, u - 1)
                            act.activation(ysb[:, s, :], psY[:, s, :], ACT.Copy).then_inc(y_kept, 1)
                    for u, s in at(i, r, 0):
                        if q == 5:
                            wait(act, h_done, (u - 1) * UNITS)
                            f.scalar_hi(act, u, s)
            run_steps(act, NG, 2, 2, step)

        @block.gpsimd
        def _(pool):
            def step(i, r):
                for q in range(UNITS):
                    for u, s in at(i, r, 1):
                        n = u * UNITS + q
                        wait(pool, hh_made, n + 1)
                        wait(pool, used, n - 1)
                        pool.tensor_tensor(hl[:, q % 2, :], h[:, q % 2, :], hh[:, q % 2, :], ALU.subtract
                                           ).then_inc(hl_made, 1)
                    for u, s in at(i, r, 0):
                        if q == 10:
                            wait(pool, masked, 2 * u + 2)
                            pool.tensor_tensor(eh[:, s, 0, :], f.xh[:, s, :], eh[:, s, 1, :], ALU.subtract)
                            pool.tensor_tensor(el[:, s, 0, :], f.xl[:, s, :], el[:, s, 1, :], ALU.subtract
                                               ).then_inc(split0, 1)
            run_steps(pool, NG, 2, 2, step)

        @block.vector
        def _(dve):
            def step(i, r):
                for q in range(UNITS):
                    for u, s in at(i, r, 1):
                        n = u * UNITS + q
                        wait(dve, h_kept, n + 1)
                        wait(dve, used, n - 1)
                        dve.tensor_copy(hh[:, q % 2, :], h[:, q % 2, :]).then_inc(hh_made, 1)
                    for u, s in at(i, r, 2):
                        xs = c.x[:, bass.ds(u * GT, GT), :]
                        if q == 3:
                            dve.tensor_tensor(xs, xs, out_bias.unsqueeze(1).broadcast_to([P, GT, P]), ALU.add
                                              ).then_inc(based, 1)
                        if q == 4:
                            wait(dve, based, u + 1)
                            wait(dve, o_done, u + 1)
                            for k in range(GT):
                                t = u * GT + k
                                dve.tensor_tensor(c.x[:, t, :], psO[:, P * k:P * k + P], c.x[:, t, :], ALU.add
                                                  ).then_inc(summed, 1)
                        if q == 5:
                            for k in range(GT):
                                t = u * GT + k
                                wait(dve, summed, t + 1)
                                dve.bn_stats(c.stats[:, t, :], c.x[:, t, :]).then_inc(stats_made, 1)
                    for u, s in at(i, r, 0):
                        if q == 4:
                            f.vector_norm(dve, u, s)
                        if q == 6:
                            wait(dve, h_done, (u - 1) * UNITS)
                            f.vector_lo(dve, u, s)
                        if q == 9:
                            wait(dve, d_done, u + 1)
                            wait(dve, f.lo_made, u + 1)
                            for dst, src in ((eh, f.xh), (el, f.xl)):
                                dve.scalar_tensor_tensor(out=dst[:, s, 1, :], in0=psD[:, :], scalar=0.0,
                                                         in1=src[:, s, :], op0=ALU.is_gt, op1=ALU.mult
                                                         ).then_inc(masked, 1)
            run_steps(dve, NG, 2, 2, step)
            dve.wait_ge(stats_made, NT)


def routed_swiglu(c, name, sems, w1, w3, w2, I, E=7):
    nc, NT, NG = c.nc, c.NT, c.NT // GT
    chunks = [(o, min(P, I - o)) for o in range(0, I, P)]
    IC = len(chunks)
    UNITS = (E + 1) * IC
    with ExitStack() as octx:
        onehot = octx.enter_context(nc.sbuf_tensor(name + "_onehot", [P, NT, E], BF16))
        w_routed = octx.enter_context(nc.sbuf_tensor(name + "_w_routed", [P, NT], F32))
        w_shared = octx.enter_context(nc.sbuf_tensor(name + "_w_shared", [P, NT], F32))
        with ExitStack() as ctx:
            red = ctx.enter_context(nc.sbuf_tensor(name + "_red", [P, NT], F32))
            first = ctx.enter_context(nc.sbuf_tensor(name + "_first", [P, E], F32))
            block = ctx.enter_context(nc.Block())
            clipped, sig, step = sems(name + "_clipped"), sems(name + "_sigmoid"), sems(name + "_route")
            L = c.logits[:, :, 0:E]
            R = red[:, :].unsqueeze(2).broadcast_to([P, NT, E])

            @block.vector
            def _(dve):
                run = chain(dve, step)
                for e in range(E):
                    run(dve.memset(first[:, e:e + 1], float(E - e)))
                dve.tensor_scalar(L, L, -50.0, 50.0, ALU.max, ALU.min).then_inc(clipped, 1)
                dve.wait_ge(sig, 1)
                run(dve.tensor_reduce(red[:, :], L, AX.X, ALU.max))
                run(dve.tensor_scalar(w_routed[:, :], red[:, :], 1e-8, 1.0 - 1e-8, ALU.max, ALU.min))
                run(dve.tensor_scalar(w_shared[:, :], w_routed[:, :], 0.5, 1e-8, ALU.add, ALU.add))
                run(dve.tensor_scalar(w_shared[:, :], w_shared[:, :], 0.5, 2.0, ALU.max, ALU.min))
                run(dve.reciprocal(w_shared[:, :], w_shared[:, :]))
                run(dve.tensor_tensor(w_routed[:, :], w_routed[:, :], w_shared[:, :], ALU.mult))
                run(dve.tensor_scalar(w_shared[:, :], w_shared[:, :], 0.5, None, ALU.mult))
                run(dve.tensor_tensor(L, L, R, ALU.is_equal))
                run(dve.tensor_tensor(L, L, first[:, :].unsqueeze(1).broadcast_to([P, NT, E]), ALU.mult))
                run(dve.tensor_reduce(red[:, :], L, AX.X, ALU.max))
                run(dve.tensor_tensor(onehot[:, :, :], L, R, ALU.is_equal))

            @block.scalar
            def _(act):
                act.wait_ge(clipped, 1)
                act.activation(L, L, ACT.Sigmoid).then_inc(sig, 1)

        ctx = octx
        f = Front(c, name, ctx, sems)
        sb = lambda n, shape, dt=F32: ctx.enter_context(nc.sbuf_tensor(f"{name}_{n}", shape, dt))
        pb = lambda n, shape: ctx.enter_context(nc.psum_tensor(f"{name}_{n}", shape, F32))
        sem = lambda n: sems(f"{name}_{n}")
        hot = sb("hot", [P, 2, GT * E], BF16)
        eh, el = sb("eh", [P, 2, N4], F32R), sb("el", [P, 2, N4], F32R)
        act_sb = sb("act", [P, 2, N4])
        h = sb("h", [P, 2, N4])
        hh, hl = sb("hh", [P, 2, N4], F32R), sb("hl", [P, 2, N4], F32R)
        ysb = sb("y", [P, 2, N4])
        psM, psA, psG, psY = pb("M", [P, N4]), pb("A", [P, 2, N4]), pb("G", [P, 2, N4]), pb("Y", [P, 2, N4])
        hot_made, m_done, masked = sem("hot_made"), sem("m_done"), sem("masked")
        a_done, a_kept, h_made, hh_made, hl_made = (sem("a_done"), sem("a_kept"), sem("h_made"), sem("hh_made"),
                                                    sem("hl_made"))
        used, y_kept, o_done = sem("used"), sem("y_kept"), sem("o_done")
        summed, stats_made = sem("summed"), sem("stats")
        block = ctx.enter_context(nc.Block())
        at = steps_of(NG)
        ROUTED = E * IC

        @block.tensor
        def _(pe):
            def masks(u, s, e):
                wait(pe, hot_made, u + 1)
                wait(pe, masked, 2 * (u * E + e))
                for k in range(GT):
                    mm = pe.matmul(psM[:, P * k:P * k + P],
                                   hot[:, s, k * E + e:k * E + e + 1].broadcast_to([P, P]), c.ident_bf[:, :],
                                   start=k == 0, stop=True, skip_group_check=True)
                mm.then_inc(m_done, 1)

            def second(u, q):
                n = u * UNITS + q
                k = chunks[q % IC][1]
                wait(pe, hl_made, n + 1)
                shared = int(q >= ROUTED)
                if q in (0, ROUTED):
                    wait(pe, y_kept, 2 * u - 1 + shared)
                products(pe, psY[:, shared, :], w2[0][0:k, q, :], w2[1][0:k, q, :], hh[0:k, q % 2, :],
                         hl[0:k, q % 2, :], first=q in (0, ROUTED), last=q in (ROUTED - 1, UNITS - 1)
                         ).then_inc(used, 1)

            def transpose_back(u, which):
                wait(pe, y_kept, 2 * u + 1 + which)
                wait(pe, summed, (2 * u + which) * GT)
                wait(pe, f.lo_made, u + 2, NG)
                for k in range(GT):
                    mm = pe.transpose(f.psT[:, P * k:P * k + P], ysb[:, which, P * k:P * k + P], c.ident[:, :])
                mm.then_inc(o_done, 1)

            def step(i, r):
                for q in range(UNITS):
                    for u, s in at(i, r, 1):
                        n = u * UNITS + q
                        e, j = divmod(q, IC)
                        if j == 0 and q == 0:
                            masks(u, s, 0)
                        if j == 0 and e < E:
                            wait(pe, masked, 2 * (u * E + e + 1))
                        if e + 1 < E and j == 1:
                            masks(u, s, e + 1)
                        wait(pe, a_kept, n - 1)
                        wait(pe, h_made, n - 1)
                        o, k = chunks[j]
                        xh, xl = (f.xh[:, s, :], f.xl[:, s, :]) if e == E else (eh[:, e % 2, :], el[:, e % 2, :])
                        cols = slice(e * I + o, e * I + o + k)
                        products(pe, psA[0:k, q % 2, :], w1[0][:, cols], w1[1][:, cols], xh, xl)
                        products(pe, psG[0:k, q % 2, :], w3[0][:, cols], w3[1][:, cols], xh, xl
                                 ).then_inc(a_done, 1)
                        if q >= 2:
                            second(u, q - 2)
                    for u, s in at(i, r, 2):
                        if q < 2:
                            second(u, q + UNITS - 2)
                        if q == 3:
                            transpose_back(u, 0)
                        if q == 6:
                            transpose_back(u, 1)
                    for u, s in at(i, r, 0):
                        if q == 9:
                            wait(pe, summed, 2 * GT * (u - 1))
                            f.tensor_transpose(pe, u, s)
            run_steps(pe, NG, 2, 2, step)

        @block.scalar
        def _(act):
            def keep_y(u, which):
                wait(act, used, u * UNITS + (ROUTED, UNITS)[which])
                wait(act, o_done, 2 * u - 1 + which)
                act.activation(ysb[:, which, :], psY[:, which, :], ACT.Copy).then_inc(y_kept, 1)

            def step(i, r):
                for q in range(UNITS):
                    for u, s in at(i, r, 2):
                        if q == 2:
                            keep_y(u, 1)
                    for u, s in at(i, r, 0):
                        if q == 9:
                            wait(act, a_done, (u - 1) * UNITS)
                            f.scalar_hi(act, u, s)
                    for u, s in at(i, r, 1):
                        n = u * UNITS + q
                        k = chunks[q % IC][1]
                        wait(act, a_done, n + 1)
                        wait(act, h_made, n - 1)
                        act.activation(act_sb[0:k, q % 2, :], psA[0:k, q % 2, :], ACT.Silu).then_inc(a_kept, 1)
                        wait(act, h_made, n + 1)
                        wait(act, used, n - 1)
                        act.activation(hh[0:k, q % 2, :], h[0:k, q % 2, :], ACT.Copy).then_inc(hh_made, 1)
                        if q == UNITS - 1:
                            keep_y(u, 0)
            run_steps(act, NG, 2, 2, step)

        @block.gpsimd
        def _(pool):
            def step(i, r):
                for u, s in at(i, r, 1):
                    for q in range(UNITS):
                        n = u * UNITS + q
                        k = chunks[q % IC][1]
                        wait(pool, hh_made, n + 1)
                        wait(pool, used, n - 1)
                        pool.tensor_tensor(hl[0:k, q % 2, :], h[0:k, q % 2, :], hh[0:k, q % 2, :], ALU.subtract
                                           ).then_inc(hl_made, 1)
            run_steps(pool, NG, 2, 2, step)

        @block.vector
        def _(dve):
            def add_y(u, which):
                wait(dve, o_done, 2 * u + 1 + which)
                w = (w_routed, w_shared)[which]
                if which:
                    wait(dve, summed, (2 * u + 1) * GT)
                for k in range(GT):
                    t = u * GT + k
                    dve.scalar_tensor_tensor(out=c.x[:, t, :], in0=f.psT[:, P * k:P * k + P],
                                             scalar=w[:, bass.ds(t, 1)], in1=c.x[:, t, :],
                                             op0=ALU.mult, op1=ALU.add).then_inc(summed, 1)

            def step(i, r):
                def mask(u, s, e):
                    wait(dve, m_done, u * E + e + 1)
                    wait(dve, a_done, u * UNITS + (e - 1) * IC if e >= 2 else (u - 1) * UNITS + ROUTED)
                    for dst, src in ((eh, f.xh), (el, f.xl)):
                        dve.tensor_tensor(dst[:, e % 2, :], psM[:, :], src[:, s, :], ALU.mult).then_inc(masked, 1)

                for q in range(UNITS):
                    for u, s in at(i, r, 1):
                        n = u * UNITS + q
                        e, j = divmod(q, IC)
                        k = chunks[j][1]
                        if q == 0:
                            wait(dve, f.lo_made, u + 1)
                            mask(u, s, 0)
                        if j == 1 and e + 1 < E:
                            mask(u, s, e + 1)
                        wait(dve, a_kept, n + 1)
                        wait(dve, hl_made, n - 1)
                        wait(dve, hh_made, n - 1)
                        dve.tensor_tensor(h[0:k, q % 2, :], psG[0:k, q % 2, :], act_sb[0:k, q % 2, :], ALU.mult
                                          ).then_inc(h_made, 1)
                    for u, s in at(i, r, 2):
                        if q == 4:
                            add_y(u, 0)
                        if q == 7:
                            add_y(u, 1)
                            for k in range(GT):
                                t = u * GT + k
                                wait(dve, summed, (2 * u + 1) * GT + k + 1)
                                dve.bn_stats(c.stats[:, t, :], c.x[:, t, :]).then_inc(stats_made, 1)
                    for u, s in at(i, r, 0):
                        if q == 4:
                            wait(dve, m_done, (u - 1) * E)
                            dve.tensor_copy(hot[:, s, :].rearrange("p (t e) -> p t e", e=E),
                                            onehot[:, bass.ds(u * GT, GT), :]).then_inc(hot_made, 1)
                            f.vector_norm(dve, u, s)
                        if q == 10:
                            wait(dve, a_done, (u - 1) * UNITS)
                            f.vector_lo(dve, u, s)
            run_steps(dve, NG, 2, 2, step)
            dve.wait_ge(stats_made, NT)
def relative_bias(c, name, sems, rel_dram, scratch, rel):
    nc = c.nc
    buckets = rel_bucket(np.arange(2 * S - 1) - (S - 1))
    with ExitStack() as ctx:
        table = ctx.enter_context(nc.sbuf_tensor(name + "_table", [H, 32], F32))
        line = ctx.enter_context(nc.sbuf_tensor(name + "_line", [H, 2 * S], F32))
        bias = ctx.enter_context(nc.sbuf_tensor(name + "_bias", [P, H, S], F32))
        flip = ctx.enter_context(nc.sbuf_tensor(name + "_flip", [P, P], F32))
        loaded, lined, written = sems(name + "_loaded"), sems(name + "_lined"), sems(name + "_written")
        spread, flipped, split = sems(name + "_spread"), sems(name + "_flipped"), sems(name + "_split")
        block = ctx.enter_context(nc.Block())

        @block.sync
        def _(sp):
            sp.dma_start(table[:, :], rel_dram).then_inc(loaded, 16)
            sp.wait_ge(lined, 2 * S)
            sp.dma_start(scratch, line[:, :]).then_inc(written, 16)
            sp.wait_ge(written, 16)
            for b in range(B2):
                sp.dma_start(bias[S * b:S * b + S, :, :], bass.AP(scratch.tensor, 0, [[1, S], [2 * S, H], [1, S]])
                             ).then_inc(spread, 16)

        @block.gpsimd
        def _(pool):
            run = chain(pool, flipped)
            run(pool.memset(flip[:, :], 0.0))
            for total in (S - 1, S - 1 + P):
                run(pool.affine_select(out=flip[:, :], in_=flip[:, :], compare_op=ALU.not_equal, fill=1.0,
                                       base=-total, pattern=[[1, P]], channel_multiplier=1))
            run(pool.tensor_copy(rel["flip"][:, :], flip[:, :]))

        @block.vector
        def _(dve):
            dve.wait_ge(loaded, 16)
            for j, bucket in enumerate(list(buckets) + [0]):
                dve.tensor_copy(line[:, j:j + 1], table[:, int(bucket):int(bucket) + 1]).then_inc(lined, 1)
            dve.wait_ge(spread, 32)
            dve.tensor_copy(rel["hi"][:, :, :], bias[:, :, :]).then_inc(split, 1)
            dve.wait_ge(split, 1)
            dve.tensor_tensor(rel["lo"][:, :, :], bias[:, :, :], rel["hi"][:, :, :], ALU.subtract).then_inc(split, 1)
            dve.wait_ge(split, 2)


def context_attention(c, name, sems, ctx_dram, ctxT, mask, gamma, beta, scale):
    nc, NT = c.nc, c.NT
    DEPTH = 4
    with ExitStack() as octx:
        o_all = octx.enter_context(nc.sbuf_tensor(name + "_o_all", [P, NT, P], F32))
        with ExitStack() as ctx:
            sb = lambda n, shape, dt=F32: ctx.enter_context(nc.sbuf_tensor(f"{name}_{n}", shape, dt))
            pb = lambda n, shape: ctx.enter_context(nc.psum_tensor(f"{name}_{n}", shape, F32))
            sem = lambda n: sems(f"{name}_{n}")
            xhat, xT = sb("xhat", [P, RING, P]), sb("xT", [P, RING, P])
            kT, v = sb("ctxT", [P, RING, P]), sb("ctx", [P, RING, P])
            m_raw, mb = sb("mask_raw", [P, RING, S], I32), sb("mask_bias", [P, RING, S])
            sc, less = sb("scores", [P, RING, S]), sb("less_max", [P, RING])
            pr, prT = sb("probs", [P, RING, P]), sb("probs_T", [P, RING, P])
            den = sb("den", [P, RING])
            psX, psS, psP, psO = (pb("X", [P, 2, 512]), pb("S", [P, 2, 512]), pb("P", [P, 2, 512]),
                                  pb("O", [P, 2, 512]))
            k_loaded = [sem(f"ctxT_loaded{r}") for r in range(RING)]
            v_loaded = [sem(f"ctx_loaded{r}") for r in range(RING)]
            m_loaded = [sem(f"mask_loaded{r}") for r in range(RING)]
            zeroed, xhat_made, xT_done, xT_kept = sem("zeroed"), sem("xhat_made"), sem("xT_done"), sem("xT_kept")
            mb_made, s_done, scored, max_made = sem("mb_made"), sem("s_done"), sem("scored"), sem("max_made")
            p_made, pT_done, pT_kept, o_done = sem("p_made"), sem("pT_done"), sem("pT_kept"), sem("o_done")
            den_made, o_kept, stats_made = sem("den_made"), sem("o_kept"), sem("stats")
            block = ctx.enter_context(nc.Block())

            def at(i, r, lag):
                u = i - lag
                if not isinstance(u, int) or 0 <= u < NT:
                    yield u, (r - lag) % RING

            def turns(u, s):
                return (u - s) * 4 + 16

            @block.sync
            def _(sp):
                def step(i, r):
                    for u, s in at(i, r, 0):
                        rows = bass.ds(u * P, P)
                        wait(sp, s_done, u - 3)
                        sp.dma_start(kT[:, s, :], ctxT[:, rows]).then_inc(k_loaded[s], 16)
                        wait(sp, mb_made, u - 3)
                        sp.dma_start(m_raw[:, s, :], mask[rows, :]).then_inc(m_loaded[s], 16)
                        wait(sp, o_done, u - 3)
                        sp.dma_start(v[:, s, :], ctx_dram[rows, :]).then_inc(v_loaded[s], 16)
                run_steps(sp, NT, DEPTH, RING, step)

            @block.gpsimd
            def _(pool):
                pool.memset(pr[:, :, :], 0.0).then_inc(zeroed, 1)

            @block.tensor
            def _(pe):
                def step(i, r):
                    for u, s in at(i, r, 3):
                        wait(pe, pT_kept, u + 1)
                        wait(pe, v_loaded[s], turns(u, s))
                        wait(pe, o_kept, u - 1)
                        pe.matmul(psO[:, s % 2, 0:P], prT[:, s, :], v[:, s, :], start=True, stop=True
                                  ).then_inc(o_done, 1)
                    for u, s in at(i, r, 2):
                        wait(pe, p_made, u + 1)
                        wait(pe, pT_kept, u - 1)
                        pe.transpose(psP[:, s % 2, 0:P], pr[:, s, :], c.ident[:, :]).then_inc(pT_done, 1)
                    for u, s in at(i, r, 1):
                        wait(pe, k_loaded[s], turns(u, s))
                        wait(pe, xT_kept, u + 1)
                        wait(pe, scored, u - 1)
                        for b in range(B2):
                            half = slice(S * b, S * b + S)
                            mm = pe.matmul(psS[half, s % 2, 0:S], xT[:, s, half], kT[:, s, half],
                                           start=True, stop=True, skip_group_check=True)
                        mm.then_inc(s_done, 1)
                    for u, s in at(i, r, 0):
                        wait(pe, xhat_made, u + 1)
                        wait(pe, xT_kept, u - 1)
                        pe.transpose(psX[:, s % 2, 0:P], xhat[:, s, :], c.ident[:, :]).then_inc(xT_done, 1)
                run_steps(pe, NT, DEPTH, RING, step)

            @block.scalar
            def _(act):
                act.wait_ge(zeroed, 1)

                def step(i, r):
                    for u, s in at(i, r, 2):
                        wait(act, pT_done, u + 1)
                        wait(act, o_done, u - 3)
                        act.activation(prT[:, s, :], psP[:, s % 2, 0:P], ACT.Copy).then_inc(pT_kept, 1)
                    for u, s in at(i, r, 1):
                        wait(act, max_made, u + 1)
                        wait(act, pT_done, u - 3)
                        wait(act, o_kept, u - 3)
                        for b in range(B2):
                            half = slice(S * b, S * b + S)
                            last = act.activation(pr[half, s, half], sc[half, s, :], ACT.Exp,
                                                  bias=less[half, s:s + 1], accum_out=den[half, s:s + 1])
                        last.then_inc(p_made, 1)
                    for u, s in at(i, r, 0):
                        wait(act, xT_done, u + 1)
                        wait(act, s_done, u - 3)
                        act.activation(xT[:, s, :], psX[:, s % 2, 0:P], ACT.Copy).then_inc(xT_kept, 1)
                run_steps(act, NT, DEPTH, RING, step)

            @block.vector
            def _(dve):
                def step(i, r):
                    for u, s in at(i, r, 1):
                        wait(dve, s_done, u + 1)
                        wait(dve, p_made, u - 3)
                        wait(dve, mb_made, u + 1)
                        dve.scalar_tensor_tensor(out=sc[:, s, :], in0=psS[:, s % 2, 0:S], scalar=scale,
                                                 in1=mb[:, s, :], op0=ALU.mult, op1=ALU.add).then_inc(scored, 1)
                    for u, s in at(i, r, 0):
                        wait(dve, xT_done, u - 3)
                        dve.tensor_scalar(xhat[:, s, :], c.x[:, u, :], c.rstd[:, bass.ds(u, 1)],
                                          c.nmr[:, bass.ds(u, 1)], ALU.mult, ALU.add).then_inc(xhat_made, 1)
                        wait(dve, m_loaded[s], turns(u, s))
                        dve.tensor_scalar(mb[:, s, :], m_raw[:, s, :], 0.0, MASKED, ALU.is_equal, ALU.mult
                                          ).then_inc(mb_made, 1)
                    for u, s in at(i, r, 1):
                        wait(dve, scored, u + 1)
                        dve.tensor_reduce(less[:, s:s + 1], sc[:, s, :], AX.X, ALU.max, negate=True
                                          ).then_inc(max_made, 1)
                    for u, s in at(i, r, 3):
                        wait(dve, p_made, u + 1)
                        dve.reciprocal(den[:, s:s + 1], den[:, s:s + 1]).then_inc(den_made, 1)
                        wait(dve, o_done, u + 1)
                        wait(dve, den_made, u + 1)
                        dve.tensor_scalar(o_all[:, u, :], psO[:, s % 2, 0:P], den[:, s:s + 1], None, ALU.mult
                                          ).then_inc(o_kept, 1)
                        wait(dve, o_kept, u + 1)
                        dve.bn_stats(c.stats[:, u, :], o_all[:, u, :]).then_inc(stats_made, 1)
                run_steps(dve, NT, DEPTH, RING, step)
                dve.wait_ge(stats_made, NT)

        layernorm_scales(c, name + "_o", sems)
        with ExitStack() as ctx:
            normed, scaled, summed = sems(name + "_normed"), sems(name + "_scaled"), sems(name + "_summed")
            based, stats2 = sems(name + "_based"), sems(name + "_stats2")
            block = ctx.enter_context(nc.Block())

            @block.scalar
            def _(act):
                with act.Fori(0, NT) as t:
                    act.activation(o_all[:, t, :], o_all[:, t, :], ACT.Identity, bias=c.nmr[:, bass.ds(t, 1)],
                                   scale=c.rstd[:, bass.ds(t, 1)]).then_inc(normed, 1)

            @block.gpsimd
            def _(pool):
                with pool.Fori(0, NT // GT) as u:
                    o4 = o_all[:, bass.ds(u * GT, GT), :]
                    x4 = c.x[:, bass.ds(u * GT, GT), :]
                    pool.tensor_tensor(x4, x4, beta.unsqueeze(1).broadcast_to([P, GT, P]), ALU.add)
                    pool.wait_ge(normed, (u + 1) * GT)
                    pool.tensor_tensor(o4, o4, gamma.unsqueeze(1).broadcast_to([P, GT, P]), ALU.mult
                                       ).then_inc(scaled, 1)

            @block.vector
            def _(dve):
                with dve.Fori(0, NT // GT) as u:
                    o4 = o_all[:, bass.ds(u * GT, GT), :]
                    x4 = c.x[:, bass.ds(u * GT, GT), :]
                    dve.wait_ge(scaled, u + 1)
                    dve.tensor_tensor(x4, x4, o4, ALU.add).then_inc(summed, 1)
                    dve.wait_ge(summed, u + 1)
                    for k in range(GT):
                        dve.bn_stats(c.stats[:, u * GT + k, :], c.x[:, u * GT + k, :]).then_inc(stats2, 1)
                dve.wait_ge(stats2, NT)


def mixture_gates(c, name, sems, wg1, bg1, wg2, bg2, bias_w, scratch, moe, scale, E=4, TOP_K=2):
    nc, NT = c.nc, c.NT
    NB = B2 * NT
    with ExitStack() as ctx:
        sb = lambda n, shape, dt=F32: ctx.enter_context(nc.sbuf_tensor(f"{name}_{n}", shape, dt))
        pb = lambda n, shape: ctx.enter_context(nc.psum_tensor(f"{name}_{n}", shape, F32))
        sem = lambda n: sems(f"{name}_{n}")
        xhat = sb("xhat", [P, 2, GT, P])
        mean_of = sb("mean_of", [P, B2])
        pooled, hidden = sb("pooled", [P, NB]), sb("hidden", [P, NB])
        lg, red, rank = sb("lg", [NB, E]), sb("red", [NB, 1]), sb("rank", [NB, E])
        pair, tie, w, wT = sb("pair", [NB, E, E]), sb("tie", [NB, E, E]), sb("w", [NB, E]), sb("wT", [E, NB])
        earlier = sb("earlier", [NB, E, E])
        psP, psH, psL, psW, psB = (pb("P", [P, 512]), pb("Hd", [P, 512]), pb("L", [P, 512]), pb("W", [P, 512]),
                                   pb("B", [P, 512]))
        const, xhat_made, pooled_done = sem("const"), sem("xhat_made"), sem("pooled_done")
        pe_done, act_done, dve_step = sem("pe_done"), sem("act_done"), sem("dve")
        w_made, exp_in, written, spread = sem("w_made"), sem("exp_in"), sem("written"), sem("spread")
        lg_made, wT_made = sem("lg_made"), sem("wT_made")
        block = ctx.enter_context(nc.Block())

        @block.gpsimd
        def _(pool):
            run = chain(pool, const)
            for b in range(B2):
                for half in range(B2):
                    run(pool.memset(mean_of[S * half:S * half + S, b:b + 1], 1.0 / S if half == b else 0.0))
            for e in range(E):
                for j in range(E):
                    run(pool.memset(earlier[:, e, j:j + 1], 1.0 if j < e else 0.0))

        @block.vector
        def _(dve):
            run = chain(dve, dve_step)
            dve.wait_ge(const, B2 * B2 + E * E)

            def step(u, s):
                wait(dve, pooled_done, (u - 1) * GT)
                for k in range(GT):
                    t = u * GT + k
                    last = dve.tensor_scalar(xhat[:, s, k, :], c.x[:, t, :], c.rstd[:, bass.ds(t, 1)],
                                             c.nmr[:, bass.ds(t, 1)], ALU.mult, ALU.add)
                last.then_inc(xhat_made, 1)
            run_steps(dve, NT // GT, 0, 2, step)
            dve.wait_ge(pe_done, 2)
            dve.tensor_tensor(lg[:, :], psL[0:NB, 0:E], bg2, ALU.add).then_inc(lg_made, 1)
            dve.wait_ge(lg_made, 1)
            run(dve.tensor_reduce(red[:, :], lg[:, :], AX.X, ALU.max))
            mine = lg[:, :].unsqueeze(2).broadcast_to([NB, E, E])
            other = lg[:, :].unsqueeze(1).broadcast_to([NB, E, E])
            run(dve.tensor_tensor(pair[:, :, :], other, mine, ALU.is_gt))
            run(dve.tensor_tensor(tie[:, :, :], other, mine, ALU.is_equal))
            run(dve.tensor_tensor(tie[:, :, :], tie[:, :, :], earlier[:, :, :], ALU.mult))
            run(dve.tensor_tensor(pair[:, :, :], pair[:, :, :], tie[:, :, :], ALU.add))
            run(dve.tensor_reduce(rank[:, :], pair[:, :, :], AX.X, ALU.add))
            run(dve.tensor_scalar(rank[:, :], rank[:, :], float(TOP_K), None, ALU.is_lt))
            dve.tensor_scalar(lg[:, :], lg[:, :], red[:, 0:1], None, ALU.subtract).then_inc(exp_in, 1)
            dve.wait_ge(act_done, 3)
            run(dve.tensor_tensor(w[:, :], lg[:, :], rank[:, :], ALU.mult))
            run(dve.tensor_reduce(red[:, :], w[:, :], AX.X, ALU.add))
            run(dve.reciprocal(red[:, :], red[:, :]))
            dve.tensor_scalar(w[:, :], w[:, :], red[:, 0:1], None, ALU.mult).then_inc(w_made, 1)
            dve.wait_ge(pe_done, 3)
            dve.tensor_copy(wT[:, :], psW[0:E, 0:NB]).then_inc(wT_made, 1)
            dve.wait_ge(pe_done, 4)
            run(dve.tensor_scalar(moe["q_bias"][:, 0:NB], psB[:, 0:NB], scale, None, ALU.mult))
            run(dve.tensor_copy(moe["k_bias"][:, 0:NB], psB[:, P:P + NB]))
            run(dve.tensor_copy(moe["v_bias"][:, 0:NB], psB[:, 2 * P:2 * P + NB]))

        @block.tensor
        def _(pe):
            def step(u, s):
                wait(pe, xhat_made, u + 1)
                for k in range(GT):
                    t = u * GT + k
                    pe.matmul(psP[:, bass.ds(t * B2, B2)], xhat[:, s, k, :], mean_of[:, :], start=True,
                              stop=True, skip_group_check=True).then_inc(pooled_done, 1)
            run_steps(pe, NT // GT, 0, 2, step)
            pe.wait_ge(act_done, 1)
            pe.matmul(psH[:, 0:NB], wg1, pooled[:, :], start=True, stop=True).then_inc(pe_done, 1)
            pe.wait_ge(act_done, 2)
            pe.matmul(psL[0:NB, 0:E], hidden[:, :], wg2, start=True, stop=True).then_inc(pe_done, 1)
            pe.wait_ge(w_made, 1)
            pe.transpose(psW[0:E, 0:NB], w[:, :], c.ident[0:NB, 0:NB]).then_inc(pe_done, 1)
            pe.wait_ge(wT_made, 1)
            for j in range(3):
                mm = pe.matmul(psB[:, j * P:j * P + NB], bias_w[:, j, :], wT[:, :], start=j == 0, stop=True,
                               skip_group_check=True)
            mm.then_inc(pe_done, 1)

        @block.scalar
        def _(act):
            act.wait_ge(pooled_done, NT)
            act.activation(pooled[:, :], psP[:, 0:NB], ACT.Copy).then_inc(act_done, 1)
            act.wait_ge(pe_done, 1)
            act.activation(hidden[:, :], psH[:, 0:NB], ACT.Relu, bias=bg1).then_inc(act_done, 1)
            act.wait_ge(exp_in, 1)
            act.activation(lg[:, :], lg[:, :], ACT.Exp).then_inc(act_done, 1)

        @block.sync
        def _(sp):
            sp.wait_ge(w_made, 1)
            sp.dma_start(scratch[0:NB, :], w[:, :]).then_inc(written, 16)
            sp.wait_ge(written, 16)
            for b in range(B2):
                sp.dma_start(moe["w_tok"][S * b:S * b + S, :, :],
                             bass.AP(scratch.tensor, b * E, [[0, S], [B2 * E, NT], [1, E]])).then_inc(spread, 16)
            sp.wait_ge(spread, 16 * B2)


def store_x(c, out, sems):
    NT = c.NT
    with ExitStack() as ctx:
        block = ctx.enter_context(c.nc.Block())
        stored = sems("x_stored")

        @block.sync
        def _(sp):
            CH = 8
            for q in range(NT // CH):
                sp.dma_start(out[q * CH * P:(q + 1) * CH * P, :].rearrange("(t p) d -> p t d", p=P),
                             c.x[:, q * CH:(q + 1) * CH, :]).then_inc(stored, 16)
            sp.wait_ge(stored, 16 * (NT // CH))


def column(v):
    return v.rearrange("(p o) -> p o", o=1)


def everywhere(v):
    return v.rearrange("(o n) -> o n", o=1).broadcast_to([P, v.shape[0]])


def row(v):
    return v.rearrange("(o n) -> o n", o=1)


def program(nc, a, out, NT, stages):
    with ExitStack() as outer:
        c = Core()

        in_use = []

        def sems(name):
            in_use.append(nc.alloc_semaphore(name=name))
            return in_use[-1]

        def free_semaphores():
            nc.all_engine_barrier()
            nc.clear_and_free_semaphores(in_use)
            nc.all_engine_barrier()
            in_use.clear()

        allocate(c, nc, outer, NT)
        build_constants(c, sems)
        load_x(c, a["x"], sems)
        SC = DH ** -0.5

        def stage(name):
            ctx = ExitStack()
            parts = []

            def sb(n, shape, dt=F32):
                return ctx.enter_context(nc.sbuf_tensor(f"{name}_w_{n}", shape, dt))

            def take(n, shape, src, dt=F32):
                t = sb(n, shape, dt)
                parts.append((t[tuple(slice(None) for _ in shape)], src))
                return t
            return ctx, sb, take, parts

        def scaled(name, dst, src):
            with ExitStack() as ctx:
                block = ctx.enter_context(nc.Block())
                done = sems(name + "_bias_scaled")

                @block.vector
                def _(dve):
                    dve.tensor_scalar(dst, src, SC, None, ALU.mult).then_inc(done, 1)
                    dve.wait_ge(done, 1)

        def projections(take, fmt):
            w = {n: take(n, [P, 1, P], a[fmt.format(n)].rearrange("k (o n) -> k o n", o=1)) for n in "qkv"}
            w["o"] = take("o", [P, P], a[fmt.format("o")])
            return w

        if "L0a" in stages:
            free_semaphores()
            ctx, sb, take, parts = stage("L0a")
            with ctx:
                w = projections(take, "L0_xattn_W_{}")
                bq, bk, bv = (take(f"b{n}", [P, 1], column(a[f"L0_xattn_b_{n}"])) for n in "qkv")
                bo = take("bo", [P, P], everywhere(a["L0_xattn_b_o"]))
                bqs = sb("bq_scaled", [P, 1])
                load_weights(c, parts, lambda n: sems("L0a_" + n))
                scaled("L0a", bqs[:, :], bq[:, :])
                layernorm_scales(c, "L0a", sems)
                attention(c, "L0a", sems, w, mask=a["mask0"], scale=SC, ctxT=a["ctx_T"],
                          q_bias=bqs[:, :], k_bias=bk[:, :], v_bias_col=bv[:, :], out_bias=bo[:, :])
        if "L0f" in stages:
            free_semaphores()
            ctx, sb, take, parts = stage("L0f")
            with ctx:
                E = 8
                c.logits = sb("logits", [P, NT, E])
                gh, gl = sb("gate_hi", [P, E], F32R), sb("gate_lo", [P, E], F32R)
                eh, el = sb("ew_hi", [P, E * P], F32R), sb("ew_lo", [P, E * P], F32R)
                gb = take("gate_b", [E, 1], a["L0_ffn_gate_b"].rearrange("(p o) -> p o", o=1))
                eb = sb("eb_blocks", [GT * E, GT, P])
                with ExitStack() as zctx:
                    block = zctx.enter_context(nc.Block())
                    cleared = sems("L0f_cleared")

                    @block.gpsimd
                    def _(pool):
                        pool.memset(eb[:, :, :], 0.0).then_inc(cleared, 1)
                        pool.wait_ge(cleared, 1)
                for k in range(GT):
                    parts.append((eb[E * k:E * k + E, k, :], a["L0_ffn_expert_b"]))
                load_weights(c, parts, lambda n: sems("L0f_" + n))
                split_weights(c, "L0f_split", [
                    ([P, E], [(lambda t: t[:, :], a["L0_ffn_gate_w"])], gh[:, :], gl[:, :]),
                    ([P, E, P], [(lambda t: t[:, :, :], a["L0_ffn_expert_w"].rearrange("e k n -> k e n"))],
                     eh[:, :].rearrange("p (e n) -> p e n", e=E), el[:, :].rearrange("p (e n) -> p e n", e=E)),
                ], sems)
                layernorm_scales(c, "L0f", sems)
                gate_logits(c, "L0f_gate", sems, (gh[:, :], gl[:, :]), gb[:, :], E)
                soft_moe(c, "L0f", sems, eh, el, eb[:, :, :].rearrange("p t n -> p (t n)"))
        if "L1a" in stages:
            free_semaphores()
            ctx, sb, take, parts = stage("L1a")
            with ctx:
                w = projections(take, "L1_xattn_W{}")
                rel = {"flip": sb("flip", [P, P], F32R), "hi": sb("rel_hi", [P, H, S], F32R),
                       "lo": sb("rel_lo", [P, H, S], F32R)}
                load_weights(c, parts, lambda n: sems("L1a_" + n))
                relative_bias(c, "L1a_rel", sems, a["L1_xattn_rel_bias"],
                              nc.dram_tensor("rel_scratch", [H, 2 * S], F32, kind="Internal").ap(), rel)
                layernorm_scales(c, "L1a", sems)
                attention(c, "L1a", sems, w, mask=a["mask1"], key_mask=True, rel=rel, ctxT=a["ctx_T"])
        if "L1f" in stages:
            free_semaphores()
            ctx, sb, take, parts = stage("L1f")
            with ctx:
                HID = a["L1_ffn_w1"].shape[2]
                HC = HID // P
                U = 3 * HC
                w1h, w1l = sb("w1_hi", [P, 3 * HID], F32R), sb("w1_lo", [P, 3 * HID], F32R)
                w2h, w2l = sb("w2_hi", [P, U, P], F32R), sb("w2_lo", [P, U, P], F32R)
                gdh, gdl = sb("gd_hi", [P, P], F32R), sb("gd_lo", [P, P], F32R)
                b1 = sb("b1", [P, U])
                for q in range(U):
                    bias = a["L1_ffn_b1"][q // HC] if q < 2 * HC else a["L1_ffn_sb1"]
                    parts.append((b1[:, q:q + 1], column(bias[q % HC * P:q % HC * P + P])))
                ob = [take(f"ob{i}", [P, P], everywhere(v)) for i, v in
                      enumerate((a["L1_ffn_b2"][0], a["L1_ffn_b2"][1], a["L1_ffn_sb2"]))]
                g = take("gate", [P, 2], a["L1_ffn_gate_w"])
                load_weights(c, parts, lambda n: sems("L1f_" + n))
                with ExitStack() as pctx:
                    gd = pctx.enter_context(nc.sbuf_tensor("L1f_gd", [P, 1], F32))
                    block = pctx.enter_context(nc.Block())
                    done = sems("L1f_prepared")

                    @block.vector
                    def _(dve):
                        run = chain(dve, done)
                        run(dve.tensor_tensor(ob[0][:, :], ob[0][:, :], ob[1][:, :], ALU.add))
                        run(dve.tensor_tensor(ob[0][:, :], ob[0][:, :], ob[2][:, :], ALU.add))
                        run(dve.tensor_tensor(gd[:, :], g[:, 1:2], g[:, 0:1], ALU.subtract))
                        run(dve.tensor_copy(gdh[:, :], gd[:, 0:1].broadcast_to([P, P])))
                        run(dve.tensor_tensor(gdl[:, :], gd[:, 0:1].broadcast_to([P, P]), gdh[:, :], ALU.subtract))
                split_weights(c, "L1f_split", [
                    ([P, 3 * HID],
                     [(lambda t, e=e: t[:, e * HID:e * HID + HID], a["L1_ffn_w1"][e]) for e in range(2)]
                     + [(lambda t: t[:, 2 * HID:3 * HID], a["L1_ffn_sw1"])], w1h[:, :], w1l[:, :]),
                    ([P, U, P],
                     [(lambda t, e=e: t[:, e * HC:e * HC + HC, :], a["L1_ffn_w2"][e].rearrange("(c p) d -> p c d", p=P))
                      for e in range(2)]
                     + [(lambda t: t[:, 2 * HC:U, :], a["L1_ffn_sw2"].rearrange("(c p) d -> p c d", p=P))],
                     w2h[:, :, :], w2l[:, :, :]),
                ], sems)
                layernorm_scales(c, "L1f", sems)
                routed_relu(c, "L1f", sems, (gdh[:, :], gdl[:, :]), (w1h, w1l), b1, (w2h, w2l), ob[0][:, :], HC)
        if "L2a" in stages:
            free_semaphores()
            ctx, sb, take, parts = stage("L2a")
            with ctx:
                w = projections(take, "L2_xattn_W{}")
                bq, bk = (take(f"b{n}", [P, 1], column(a[f"L2_xattn_b{n}"])) for n in "qk")
                bv = take("bv", [1, P], row(a["L2_xattn_bv"]))
                bo = take("bo", [P, P], everywhere(a["L2_xattn_bo"]))
                bqs = sb("bq_scaled", [P, 1])
                load_weights(c, parts, lambda n: sems("L2a_" + n))
                scaled("L2a", bqs[:, :], bq[:, :])
                layernorm_scales(c, "L2a", sems)
                attention(c, "L2a", sems, w, linear=True, mask=a["mask2"], scale=SC, ctxT=a["ctx_T"],
                          q_bias=bqs[:, :], k_bias=bk[:, :], v_bias_row=bv, out_bias=bo[:, :])
        if "L2f" in stages:
            free_semaphores()
            ctx, sb, take, parts = stage("L2f")
            with ctx:
                E, C, I = a["L2_ffn_ew1"].shape
                IC = -(-I // P)
                c.logits = sb("logits", [P, NT, E])
                gh, gl = sb("gate_hi", [P, E], F32R), sb("gate_lo", [P, E], F32R)
                rb = take("router_b", [E, 1], a["L2_ffn_routing_bias"].rearrange("(p o) -> p o", o=1))
                w13 = {n: (sb(n + "_hi", [P, (E + 1) * I], F32R), sb(n + "_lo", [P, (E + 1) * I], F32R))
                       for n in ("w1", "w3")}
                w2 = (sb("w2_hi", [P, (E + 1) * IC, P], F32R), sb("w2_lo", [P, (E + 1) * IC, P], F32R))
                load_weights(c, parts, lambda n: sems("L2f_" + n))
                full = I // P
                rest = I - full * P
                split_weights(c, "L2f_gates", [([P, E], [(lambda t: t[:, :], a["L2_ffn_router_w"])], gh[:, :], gl[:, :])],
                              sems)
                for n in ("w1", "w3"):
                    split_weights(c, f"L2f_{n}", [
                        ([P, (E + 1) * I],
                         [(lambda t: t[:, 0:E * I].rearrange("p (e i) -> p e i", e=E),
                           a[f"L2_ffn_e{n}"].rearrange("e k i -> k e i")),
                          (lambda t: t[:, E * I:(E + 1) * I], a[f"L2_ffn_s{n}"])],
                         w13[n][0][:, :], w13[n][1][:, :])], sems)
                for lo_p, rows, js in ((0, P, range(full)), (0, rest, [full])):
                    for j in js:
                        split_weights(c, f"L2f_w2_{j}", [
                            ([rows, E + 1, P],
                             [(lambda t: t[:, 0:E, :],
                               a["L2_ffn_ew2"][:, j * P:j * P + rows, :].rearrange("e i d -> i e d")),
                              (lambda t: t[:, E, :], a["L2_ffn_sw2"][j * P:j * P + rows, :])],
                             w2[0][0:rows, j::IC, :], w2[1][0:rows, j::IC, :])], sems)
                layernorm_scales(c, "L2f", sems)
                gate_logits(c, "L2f_gate", sems, (gh[:, :], gl[:, :]), rb[:, :], E)
                routed_swiglu(c, "L2f", sems, w13["w1"], w13["w3"], w2, I, E)
        if "L3a" in stages:
            free_semaphores()
            ctx, sb, take, parts = stage("L3a")
            with ctx:
                gamma, beta = (take(n, [P, P], everywhere(a[f"L3_xattn_{n}"])) for n in ("gamma", "beta"))
                load_weights(c, parts, lambda n: sems("L3a_" + n))
                layernorm_scales(c, "L3a", sems)
                context_attention(c, "L3a", sems, a["ctx"], a["ctx_T"], a["mask3"], gamma[:, :], beta[:, :],
                                  P ** -0.5)
        if "L3f" in stages:
            free_semaphores()
            ctx, sb, take, parts = stage("L3f")
            with ctx:
                E = 4
                w = {n: take(n, [P, E, P], a[f"L3_ffn_W{n}"].rearrange("e k n -> k e n")) for n in "qkv"}
                w["o"] = take("o", [P, P], a["L3_ffn_Wo"])
                bo = take("bo", [P, P], everywhere(a["L3_ffn_bo"]))
                wg1, wg2 = take("wg1", [P, P], a["L3_ffn_Wg1"]), take("wg2", [P, E], a["L3_ffn_Wg2"])
                bg1 = take("bg1", [P, 1], column(a["L3_ffn_bg1"]))
                bg2 = take("bg2", [P, E], everywhere(a["L3_ffn_bg2"]))
                bias_w = sb("bias_w", [E, 3, P])
                for j, n in enumerate("qkv"):
                    parts.append((bias_w[:, j, :], a[f"L3_ffn_b{n}"]))
                moe = {"xn": sb("xn", [P, RING, P]), "w_tok": sb("w_tok", [P, NT, E]),
                       "q_bias": sb("q_bias", [P, P]), "k_bias": sb("k_bias", [P, P]),
                       "v_bias": sb("v_bias", [P, P])}
                load_weights(c, parts, lambda n: sems("L3f_" + n))
                layernorm_scales(c, "L3f", sems)
                mixture_gates(c, "L3f_gate", sems, wg1[:, :], bg1[:, :], wg2[:, :], bg2[0:B2 * NT, :], bias_w,
                              nc.dram_tensor("gate_scratch", [P, E], F32, kind="Internal").ap(), moe, SC)
                attention(c, "L3f", sems, w, moe=moe, scale=SC, out_bias=bo[:, :])
        store_x(c, out, sems)


def layout(inp):
    T = np.ascontiguousarray
    d = {}
    d["x"] = inp["x"].reshape(-1, P)
    d["ctx"] = inp["ctx_1024"].reshape(-1, P)
    d["ctx_T"] = T(d["ctx"].T)
    d["mask0"] = inp["mask_Bx1xSxS2_if1"].reshape(-1, S)
    d["mask1"] = inp["mask_Bx1x1xS2_bk0"].reshape(-1, S)
    d["mask2"] = inp["mask_Bx1xSxS2_ik1"].reshape(-1, S)
    d["mask3"] = inp["mask_BxSxS2_ik1"].reshape(-1, S)
    for n in inp:
        if n[0] == "L":
            v = inp[n]
            if n.startswith(("L1_xattn_W", "L2_xattn_W")) or n in ("L2_ffn_router_w", "L1_ffn_gate_w"):
                v = T(v.T)
            if n.startswith(("L2_ffn_ew", "L2_ffn_sw")):
                v = T(np.swapaxes(v, -1, -2))
            d[n] = v
    return d


def kernel(**inputs):
    import concourse.bacc as bacc
    from concourse.bass_utils import run_bass_kernel_spmd

    nc = bacc.Bacc("TRN2", target_bir_lowering=False, num_devices=1)
    arrays = layout({n: np.asarray(v) for n, v in inputs.items()})
    tokens = arrays["x"].shape[0]
    a = {n: nc.dram_tensor(n, v.shape, mybir.dt.from_np(v.dtype), kind="ExternalInput").ap()
         for n, v in arrays.items()}
    out = nc.dram_tensor("out", [tokens, P], F32, kind="ExternalOutput").ap()
    program(nc, a, out, tokens // P, ("L0a", "L0f", "L1a", "L1f", "L2a", "L2f", "L3a", "L3f"))
    result = run_bass_kernel_spmd(nc, [arrays], core_ids=[0])
    return result.results[0]["out"].reshape(np.asarray(inputs["x"]).shape)
```

```python
from contextlib import ExitStack
import math

import numpy as np
import concourse.bass as bass
from concourse import mybir

ALU = mybir.AluOpType
ACT = mybir.ActivationFunctionType
AX = mybir.AxisListType
F32 = mybir.dt.float32
F32R = mybir.dt.float32r
BF16 = mybir.dt.bfloat16
I32 = mybir.dt.int32
U8 = mybir.dt.uint8

P = 128
S = 64
B2 = 2
H = 16
DH = P // H
RING = 4
EPS = 1e-5
MASKED = -(2.0 ** 100)


def wait(eng, sem, n, last=None):
    if isinstance(n, int):
        if last is not None:
            n = min(n, last)
        if n <= 0:
            return
    eng.wait_ge(sem, n)


def run_steps(eng, count, depth, ring, step):
    head = depth + ring
    assert depth % ring == 0 and (count - head) % ring == 0 and count >= head
    for i in range(head):
        step(i, i % ring)
    if count > head:
        with eng.Fori(0, (count - head) // ring) as turn:
            for r in range(ring):
                step(turn * ring + (head + r), r)
    for i in range(count, count + depth):
        step(i, i % ring)


def rel_bucket(rp, buckets=32, max_distance=128):
    nb = buckets // 2
    out = (rp > 0).astype(np.int32) * nb
    rp = np.abs(rp)
    exact = nb // 2
    large = exact + (np.log(np.maximum(rp, 1).astype(np.float32) / np.float32(exact))
                     / np.float32(math.log(max_distance / exact)) * np.float32(nb - exact)).astype(np.int32)
    return out + np.where(rp < exact, rp, np.minimum(large, nb - 1))


class Core:
    pass


def allocate(c, nc, ctx, NT):
    c.nc, c.NT = nc, NT
    c.sb = lambda name, shape, dt=F32: ctx.enter_context(nc.sbuf_tensor(name, shape, dt))
    c.x = c.sb("x_all", [P, NT, P])
    c.stats = c.sb("ln_stats", [P, NT, 6])
    c.rstd = c.sb("ln_rstd", [P, NT])
    c.nmr = c.sb("ln_neg_mean_rstd", [P, NT])
    c.ln_tmp = c.sb("ln_tmp", [P, 3, NT])
    c.ident = c.sb("ident", [P, P])
    c.ident_bf = c.sb("ident_bf", [P, P], BF16)
    c.head_of_row = c.sb("head_of_row", [P, 4])


def build_constants(c, sems):
    with ExitStack() as ctx:
        block = ctx.enter_context(c.nc.Block())
        made = sems("const_made")

        @block.gpsimd
        def _(pool):
            n = 0

            def made_next(instruction):
                nonlocal n
                n += 1
                instruction.then_inc(made, 1)
                pool.wait_ge(made, n)

            made_next(pool.memset(c.ident[:, :], 0.0))
            made_next(pool.memset(c.head_of_row[:, :], 1.0))
            made_next(pool.affine_select(out=c.ident[:, :], in_=c.ident[:, :], compare_op=ALU.not_equal, fill=1.0,
                                         base=0, pattern=[[-1, P]], channel_multiplier=1))
            made_next(pool.tensor_copy(c.ident_bf[:, :], c.ident[:, :]))
            for g in range(4):
                part = c.head_of_row[32 * g:32 * g + 32, :]
                made_next(pool.affine_select(out=part, in_=part, compare_op=ALU.is_ge, fill=0.0,
                                             base=0, pattern=[[-8, 4]], channel_multiplier=1))
                made_next(pool.affine_select(out=part, in_=part, compare_op=ALU.is_ge, fill=0.0,
                                             base=7, pattern=[[8, 4]], channel_multiplier=-1))


def load_weights(c, parts, sems):
    with ExitStack() as ctx:
        block = ctx.enter_context(c.nc.Block())
        s_sp, s_act = sems("weights_sp"), sems("weights_act")
        half = (len(parts) + 1) // 2

        @block.sync
        def _(sp):
            for dst, src in parts[:half]:
                sp.dma_start(dst, src).then_inc(s_sp, 16)
            sp.wait_ge(s_sp, 16 * half)

        @block.scalar
        def _(act):
            for dst, src in parts[half:]:
                act.dma_start(dst, src).then_inc(s_act, 16)
            if parts[half:]:
                act.wait_ge(s_act, 16 * (len(parts) - half))


def load_x(c, x_dram, parts, sems):
    NT = c.NT
    CH = 8
    with ExitStack() as ctx:
        block = ctx.enter_context(c.nc.Block())
        landed = [sems(f"x_landed{q}") for q in range(NT // CH)]
        stats_made, weights_landed = sems("x_stats_made"), sems("weights_landed")

        @block.sync
        def _(sp):
            for q in range(NT // CH):
                sp.dma_start(c.x[:, q * CH:(q + 1) * CH, :],
                             x_dram[q * CH * P:(q + 1) * CH * P, :].rearrange("(t p) d -> p t d", p=P)
                             ).then_inc(landed[q], 16)

        @block.scalar
        def _(act):
            for dst, src in parts:
                act.dma_start(dst, src).then_inc(weights_landed, 16)
            if parts:
                act.wait_ge(weights_landed, 16 * len(parts))

        @block.vector
        def _(dve):
            for q in range(NT // CH):
                dve.wait_ge(landed[q], 16)
                for t in range(q * CH, (q + 1) * CH):
                    dve.bn_stats(c.stats[:, t, :], c.x[:, t, :]).then_inc(stats_made, 1)
            dve.wait_ge(stats_made, NT)


def layernorm_scales(c, name, sems):
    with ExitStack() as ctx:
        block = ctx.enter_context(c.nc.Block())
        step, var_made, root_made = sems(name + "_ln"), sems(name + "_var"), sems(name + "_root")
        st = c.stats
        mean_e, m2_e, mean_o, m2_o = st[:, :, 1], st[:, :, 2], st[:, :, 4], st[:, :, 5]
        mean, diff, var = c.ln_tmp[:, 0, :], c.ln_tmp[:, 1, :], c.ln_tmp[:, 2, :]

        @block.vector
        def _(dve):
            dve.tensor_tensor(mean, mean_e, mean_o, ALU.add).then_inc(step, 1)
            dve.tensor_tensor(diff, mean_e, mean_o, ALU.subtract).then_inc(step, 1)
            dve.tensor_tensor(var, m2_e, m2_o, ALU.add).then_inc(step, 1)
            dve.wait_ge(step, 3)
            dve.scalar_tensor_tensor(out=diff, in0=diff, scalar=P / 4.0, in1=diff,
                                     op0=ALU.mult, op1=ALU.mult).then_inc(step, 1)
            dve.wait_ge(step, 4)
            dve.tensor_tensor(var, var, diff, ALU.add).then_inc(step, 1)
            dve.wait_ge(step, 5)
            dve.tensor_scalar(var, var, 1.0 / P, EPS, ALU.mult, ALU.add).then_inc(var_made, 1)
            dve.wait_ge(root_made, 1)
            dve.reciprocal(c.rstd[:, :], diff).then_inc(step, 1)
            dve.wait_ge(step, 6)
            dve.scalar_tensor_tensor(out=c.nmr[:, :], in0=mean, scalar=-0.5, in1=c.rstd[:, :],
                                     op0=ALU.mult, op1=ALU.mult).then_inc(step, 1)
            dve.wait_ge(step, 7)

        @block.scalar
        def _(act):
            act.wait_ge(var_made, 1)
            act.activation(diff, var, ACT.Sqrt).then_inc(root_made, 1)


def attention(c, name, sems, w, linear=False, mask=None, key_mask=False, rel=None, scale=1.0,
              ctxT=None, q_bias=None, k_bias=None, v_bias_col=None, v_bias_row=None, out_bias=None,
              moe=None, split_pv=False):
    nc, NT = c.nc, c.NT
    DEPTH = 8
    NE = 4 if moe else 1
    masked = mask is not None
    with ExitStack() as ctx:
        sb = lambda n, shape, dt=F32: ctx.enter_context(nc.sbuf_tensor(f"{name}_{n}", shape, dt))
        pb = lambda n, shape: ctx.enter_context(nc.psum_tensor(f"{name}_{n}", shape, F32))
        sem = lambda n: sems(f"{name}_{n}")
        xhat = sb("xhat", [P, RING, NE, P])
        xT = sb("xT", [P, RING, NE, P])
        ctx_sb = None if moe else sb("ctxT", [P, RING, P])
        still = sb("still", [P, RING, P])
        flat = sb("flat", [P, RING, P])
        wide = sb("wide", [P, RING, B2, 4, S])
        Pr = sb("probs", [P, 2, H, S])
        On = sb("On", [P, RING, P])
        oT = sb("oT", [P, RING, P])
        less = sb("less_max", [P, 2, H, S])
        PT = sb("probs_T", [P, 2, 8, P])
        Vb = sb("Vblk", [P, RING, B2, 8, 2, DH + 1])
        mx = sb("mx", [P, RING, H])
        rden = sb("rden", [P, RING, H])
        if masked:
            M_raw = sb("mask_raw", [P, RING, S], U8 if key_mask else I32)
            if linear:
                keep = sb("keep", [P, RING, S])
                fill = sb("fill", [P, RING, S])
            else:
                Mb = sb("mask_bias", [P, RING, S], BF16)

        psS = pb("S", [P, 1024])
        psPT = pb("PT", [P, 1024])
        psT = pb("T", [P, 512])
        psQKV = pb("QKV", [P, 512])
        psO = pb("O", [P, 512])
        psOY = pb("OY", [P, 512])

        ctx_loaded = [] if moe else [sem(f"ctx_loaded{r}") for r in range(RING)]
        mask_loaded = [sem(f"mask_loaded{r}") for r in range(RING)] if masked else []
        xn_made = sem("xn_made") if moe else None
        if linear:
            v_part, v_part_made = sb("v_part", [P, H, DH]), sem("v_part_made")
        xhat_made, xT_done, xT_kept = sem("xhat_made"), sem("xT_done"), sem("xT_kept")
        qk_done, qk_kept, v_done, v_kept = sem("qk_done"), sem("qk_kept"), sem("v_done"), sem("v_kept")
        wide_made, mask_made, s_rows, s_done = sem("wide_made"), sem("mask_made"), sem("s_rows"), sem("s_done")
        max_made, less_made, p_made = sem("max_made"), sem("less_made"), sem("p_made")
        pt0_done, pt1_done, pt0_kept, pt1_kept = sem("pt0_done"), sem("pt1_done"), sem("pt0_kept"), sem("pt1_kept")
        o_done, rden_made, on_made = sem("o_done"), sem("rden_made"), sem("on_made")
        oT_done, oT_kept, y_done = sem("oT_done"), sem("oT_kept"), sem("y_done")
        x_based, x_summed, stats_made, zeroed = sem("x_based"), sem("x_summed"), sem("stats_made"), sem("zeroed")

        def at(i, r, lag):
            u = i - lag
            if not isinstance(u, int) or 0 <= u < NT:
                yield u, (r - lag) % RING

        def turns(u, s, n):
            return (u - s) * (n // RING) + n

        block = ctx.enter_context(nc.Block())

        @block.sync
        def _(sp):
            def step(i, r):
                for u, s in at(i, r, 0):
                    if not moe:
                        wait(sp, v_done, u - 3)
                        sp.dma_start(ctx_sb[:, s, :], ctxT[:, bass.ds(u * P, P)]).then_inc(ctx_loaded[s], 16)
                    if masked:
                        wait(sp, mask_made, u - 3)
                        if key_mask:
                            for b in range(B2):
                                sp.dma_start(M_raw[S * b:S * b + S, s, :],
                                             mask[bass.ds(u * B2 + b, 1), :].broadcast_to([S, S])
                                             ).then_inc(mask_loaded[s], 16)
                        else:
                            sp.dma_start(M_raw[:, s, :], mask[bass.ds(u * P, P), :]).then_inc(mask_loaded[s], 16)
            if not moe or masked:
                run_steps(sp, NT, DEPTH, RING, step)

        @block.gpsimd
        def _(pool):
            pool.memset(Vb[:, :, :, :, :, :], 0.0).then_inc(zeroed, 1)
            pool.wait_ge(zeroed, 1)
            pool.memset(Vb[0:S, :, :, :, 0, DH:DH + 1], 1.0).then_inc(zeroed, 1)
            pool.memset(Vb[S:P, :, :, :, 1, DH:DH + 1], 1.0).then_inc(zeroed, 1)
            pool.wait_ge(zeroed, 3)

            def step(i, r):
                if linear:
                    for u, s in at(i, r, 4):
                        wait(pool, less_made, u + 1)
                        wait(pool, pt1_done, u - 1)
                        pool.tensor_tensor(Pr[:, s % 2], less[:, s % 2],
                                           fill[:, s, :].unsqueeze(1).broadcast_to([P, H, S]), ALU.add
                                           ).then_inc(p_made, 1)
                for u, s in at(i, r, 3):
                    wait(pool, qk_kept, u + 1)
                    wait(pool, s_done, u - 3)
                    pool.tensor_tensor(
                        wide[:, s],
                        flat[:, s, :].rearrange("p (b n) -> p b n", b=B2).unsqueeze(2).broadcast_to([P, B2, 4, S]),
                        c.head_of_row[:, :].unsqueeze(1).unsqueeze(3).broadcast_to([P, B2, 4, S]),
                        ALU.mult).then_inc(wide_made, 1)
            run_steps(pool, NT, DEPTH, RING, step)

        @block.tensor
        def _(pe):
            def pv(i, r, b):
                for u, s in at(i, r, 6):
                    if b == 0:
                        wait(pe, on_made, u)
                        wait(pe, v_kept, u + 1)
                        wait(pe, pt0_kept, u + 1)
                        wait(pe, pt1_kept, u + 1)
                    for gj in range(8):
                        mm = pe.matmul(psO[S * b:S * b + S, 18 * gj:18 * gj + 18],
                                       PT[:, s % 2, gj, S * b:S * b + S],
                                       Vb[:, s, b, gj].rearrange("p h d -> p (h d)"),
                                       start=gj == 0, stop=True, skip_group_check=True)
                    if b == 1:
                        mm.then_inc(o_done, 1)

            def step(i, r):
                for u, s in at(i, r, 4):
                    wait(pe, wide_made, u + 1)
                    wait(pe, less_made, u)
                    if masked and not linear:
                        wait(pe, mask_made, u + 1)
                        for hb in range(2):
                            pe.matmul(psS[:, 512 * hb:512 * hb + 512], c.ident_bf[:, :],
                                      Mb[:, s, :].unsqueeze(1).broadcast_to([P, 8, S]),
                                      start=True, stop=True, skip_group_check=True)
                    if rel is not None:
                        for hb in range(2):
                            for part in ("hi", "lo"):
                                pe.matmul(psS[:, 512 * hb:512 * hb + 512], rel["flip"][:, :],
                                          rel[part][:, 8 * hb:8 * hb + 8, :].rearrange("p h k -> p (h k)"),
                                          start=False, stop=True, skip_group_check=True)
                    for order, g in enumerate((0, 2, 1, 3)):
                        if order >= 2:
                            pe.wait_ge(s_rows, 2 * u + order - 1)
                        for b in range(B2):
                            mm = pe.matmul(psS[S * b:S * b + S, 256 * g:256 * g + 256],
                                           still[32 * g:32 * g + 32, s, S * b:S * b + S],
                                           wide[32 * g:32 * g + 32, s, b].rearrange("p j n -> p (j n)"),
                                           start=order < 2 and (linear or not masked), stop=True,
                                           skip_group_check=True)
                        if order < 2:
                            mm.then_inc(s_rows, 1)
                    mm.then_inc(s_done, 1)
                for u, s in at(i, r, 4):
                    wait(pe, qk_kept, u + 2, NT)
                    wait(pe, v_kept, u)
                    for b in range(B2):
                        for h in range(2):
                            o = psQKV[S * h:S * h + S, 256 + S * b:256 + S * b + S].rearrange("p (g d) -> p g d", d=DH)
                            for e in range(NE):
                                src = xT[:, s, e, :] if moe else ctx_sb[:, s, :]
                                mm = pe.matmul(o, src[:, b * S:b * S + S],
                                               w["v"][:, e, :].rearrange("k (g h d) -> k g h d", g=8, h=2)[:, :, h, :],
                                               start=b == 0 and e == 0, stop=e == NE - 1, skip_group_check=True)
                    mm.then_inc(v_done, 1)
                for u, s in at(i, r, 1):
                    wait(pe, xhat_made, u + 1)
                    wait(pe, xT_kept, u)
                    for e in range(NE):
                        mm = pe.transpose(psT[:, P * e:P * e + P], xhat[:, s, e, :], c.ident[:, :])
                    mm.then_inc(xT_done, 1)
                for u, s in at(i, r, 7):
                    wait(pe, on_made, u + 1)
                    wait(pe, x_summed, u - 1)
                    pe.transpose(psOY[:, 0:P], On[:, s, :], c.ident[:, :]).then_inc(oT_done, 1)
                for u, s in at(i, r, 5):
                    wait(pe, p_made, u + 1)
                    for half, (kept, done) in enumerate(((pt0_kept, pt0_done), (pt1_kept, pt1_done))):
                        wait(pe, kept, u)
                        for gj in range(4 * half, 4 * half + 4):
                            mm = pe.transpose(psPT[:, P * gj:P * gj + P],
                                              Pr[:, s % 2, 2 * gj:2 * gj + 2, :].rearrange("p h k -> p (h k)"),
                                              c.ident[:, :])
                        mm.then_inc(done, 1)
                if split_pv:
                    pv(i, r, 0)
                for u, s in at(i, r, 2):
                    wait(pe, xT_kept, u + 1)
                    wait(pe, qk_kept, u)
                    wait(pe, v_kept, u - 1)
                    if not moe:
                        wait(pe, ctx_loaded[s], turns(u, s, 16))
                    for o, key in ((0, "q"), (P, "k")):
                        for e in range(NE):
                            src = ctx_sb[:, s, :] if key == "k" and not moe else xT[:, s, e, :]
                            mm = pe.matmul(psQKV[:, o:o + P], w[key][:, e, :], src,
                                           start=o == 0 and e == 0, stop=e == NE - 1, skip_group_check=True)
                    mm.then_inc(qk_done, 1)
                for u, s in at(i, r, 8):
                    wait(pe, oT_kept, u + 2, NT)
                    wait(pe, x_summed, u)
                    pe.matmul(psOY[:, P:2 * P], oT[:, s, :], w["o"][:, :], start=True, stop=True
                              ).then_inc(y_done, 1)
                if not split_pv:
                    pv(i, r, 0)
                pv(i, r, 1)
            run_steps(pe, NT, DEPTH, RING, step)

        @block.scalar
        def _(act):
            act.wait_ge(zeroed, 3)

            def step(i, r):
                for u, s in at(i, r, 4):
                    wait(act, v_done, u + 1)
                    wait(act, o_done, u - 3)
                    for h in range(2):
                        last = act.activation(
                            Vb[S * h:S * h + S, s, :, :, h, 0:DH],
                            psQKV[S * h:S * h + S, 256:384].rearrange("p (b g d) -> p b g d", b=B2, g=8), ACT.Copy)
                    last.then_inc(v_kept, 1)
                for u, s in at(i, r, 1):
                    wait(act, xT_done, u + 1)
                    wait(act, v_done if moe else qk_done, u - 3)
                    act.activation(xT[:, s].rearrange("p e n -> p (e n)"), psT[:, 0:P * NE], ACT.Copy
                                   ).then_inc(xT_kept, 1)
                for u, s in at(i, r, 7):
                    wait(act, oT_done, u + 1)
                    wait(act, y_done, u - 3)
                    if moe:
                        for b in range(B2):
                            last = act.activation(oT[:, s, S * b:S * b + S], psOY[:, S * b:S * b + S], ACT.Identity,
                                                  bias=moe["v_bias"][:, bass.ds(B2 * u + b, 1)])
                        last.then_inc(oT_kept, 1)
                    elif v_bias_col is not None:
                        act.activation(oT[:, s, :], psOY[:, 0:P], ACT.Identity, bias=v_bias_col).then_inc(oT_kept, 1)
                    else:
                        act.activation(oT[:, s, :], psOY[:, 0:P], ACT.Copy).then_inc(oT_kept, 1)
                for u, s in at(i, r, 5):
                    wait(act, pt0_done, u + 1)
                    wait(act, o_done, u - 1)
                    act.activation(PT[:, s % 2, 0:4, :].rearrange("p g n -> p (g n)"), psPT[:, 0:512], ACT.Copy
                                   ).then_inc(pt0_kept, 1)
                for u, s in at(i, r, 2):
                    wait(act, qk_done, u + 1)
                    wait(act, s_done, u - 3)
                    wait(act, wide_made, u - 3)
                    qd, kd = still, flat
                    if moe:
                        for b in range(B2):
                            cols = slice(S * b, S * b + S)
                            act.activation(qd[:, s, cols], psQKV[:, cols], ACT.Identity, scale=scale,
                                           bias=moe["q_bias"][:, bass.ds(B2 * u + b, 1)])
                            last = act.activation(kd[:, s, cols], psQKV[:, P + S * b:P + S * b + S], ACT.Identity,
                                                  bias=moe["k_bias"][:, bass.ds(B2 * u + b, 1)])
                        last.then_inc(qk_kept, 1)
                    elif q_bias is not None:
                        act.activation(qd[:, s, :], psQKV[:, 0:P], ACT.Identity, scale=scale, bias=q_bias)
                        act.activation(kd[:, s, :], psQKV[:, P:2 * P], ACT.Identity, bias=k_bias).then_inc(qk_kept, 1)
                    else:
                        act.activation(qd[:, s, :], psQKV[:, 0:P], ACT.Copy)
                        act.activation(kd[:, s, :], psQKV[:, P:2 * P], ACT.Copy).then_inc(qk_kept, 1)
                if not linear:
                    for u, s in at(i, r, 4):
                        wait(act, less_made, u + 1)
                        wait(act, pt1_done, u - 1)
                        act.activation(Pr[:, s % 2].rearrange("p h n -> p (h n)"),
                                       less[:, s % 2].rearrange("p h n -> p (h n)"), ACT.Exp).then_inc(p_made, 1)
            run_steps(act, NT, DEPTH, RING, step)

        @block.vector
        def _(dve):
            def step(i, r):
                for u, s in at(i, r, 4):
                    wait(dve, s_done, u + 1)
                    S3 = psS[:, :].rearrange("p (h k) -> p h k", k=S)
                    if linear:
                        wait(dve, mask_made, u + 1)
                        wait(dve, p_made, u - 1)
                        dve.tensor_tensor(less[:, s % 2], S3, keep[:, s, :].unsqueeze(1).broadcast_to([P, H, S]),
                                          ALU.mult).then_inc(less_made, 1)
                    else:
                        dve.tensor_reduce(mx[:, s, :], S3, AX.X, ALU.max).then_inc(max_made, 1)
                        wait(dve, max_made, u + 1)
                        wait(dve, p_made, u - 1)
                        dve.tensor_tensor(less[:, s % 2], S3, mx[:, s, :].unsqueeze(2).broadcast_to([P, H, S]),
                                          ALU.subtract).then_inc(less_made, 1)
                for u, s in at(i, r, 0):
                    wait(dve, xT_done, u - 3)
                    if moe:
                        dve.tensor_scalar(moe["xn"][:, s, :], c.x[:, u, :], c.rstd[:, bass.ds(u, 1)],
                                          c.nmr[:, bass.ds(u, 1)], ALU.mult, ALU.add).then_inc(xn_made, 1)
                        wait(dve, xn_made, u + 1)
                        for e in range(NE):
                            last = dve.tensor_scalar(xhat[:, s, e, :], moe["xn"][:, s, :],
                                                     moe["w_tok"][:, u, e:e + 1], None, ALU.mult)
                        last.then_inc(xhat_made, 1)
                    else:
                        dve.tensor_scalar(xhat[:, s, 0, :], c.x[:, u, :], c.rstd[:, bass.ds(u, 1)],
                                          c.nmr[:, bass.ds(u, 1)], ALU.mult, ALU.add).then_inc(xhat_made, 1)
                    if out_bias is not None:
                        wait(dve, xhat_made, u + 1)
                        dve.tensor_tensor(c.x[:, u, :], c.x[:, u, :], out_bias, ALU.add).then_inc(x_based, 1)
                if masked:
                    for u, s in at(i, r, 2):
                        wait(dve, mask_loaded[s], turns(u, s, 32 if key_mask else 16))
                        if linear:
                            wait(dve, p_made, u - 3)
                            dve.tensor_scalar(keep[:, s], M_raw[:, s], 0.0, None, ALU.not_equal)
                            dve.tensor_scalar(fill[:, s], M_raw[:, s], 0.0, 1e-9, ALU.is_equal, ALU.mult
                                              ).then_inc(mask_made, 1)
                        else:
                            wait(dve, s_done, u - 3)
                            dve.tensor_scalar(Mb[:, s], M_raw[:, s], 0.0, MASKED, ALU.is_equal, ALU.mult
                                              ).then_inc(mask_made, 1)
                for u, s in at(i, r, 5):
                    wait(dve, pt1_done, u + 1)
                    wait(dve, o_done, u - 1)
                    dve.tensor_copy(PT[:, s % 2, 4:8, :].rearrange("p g n -> p (g n)"), psPT[:, 512:1024]
                                    ).then_inc(pt1_kept, 1)
                for u, s in at(i, r, 8):
                    wait(dve, y_done, u + 1)
                    if out_bias is not None:
                        wait(dve, x_based, u + 1)
                    dve.tensor_tensor(c.x[:, u, :], psOY[:, P:2 * P], c.x[:, u, :], ALU.add).then_inc(x_summed, 1)
                    wait(dve, x_summed, u + 1)
                    dve.bn_stats(c.stats[:, u, :], c.x[:, u, :]).then_inc(stats_made, 1)
                for u, s in at(i, r, 6):
                    wait(dve, o_done, u + 1)
                    wait(dve, oT_done, u - 3)
                    Ov = psO[:, 0:144].rearrange("p (h d) -> p h d", d=DH + 1)
                    if linear:
                        dve.tensor_copy(rden[:, s, :].unsqueeze(2), Ov[:, :, DH:DH + 1]).then_inc(rden_made, 1)
                        wait(dve, rden_made, u + 1)
                        dve.tensor_tensor(v_part[:, :, :], rden[:, s, :].unsqueeze(2).broadcast_to([P, H, DH]),
                                          v_bias_row.rearrange("p (h d) -> p h d", d=DH), ALU.mult
                                          ).then_inc(v_part_made, 1)
                        wait(dve, v_part_made, u + 1)
                        dve.tensor_tensor(On[:, s, :].rearrange("p (h d) -> p h d", d=DH), Ov[:, :, 0:DH],
                                          v_part[:, :, :], ALU.add).then_inc(on_made, 1)
                    else:
                        dve.reciprocal(rden[:, s, :].unsqueeze(2), Ov[:, :, DH:DH + 1]).then_inc(rden_made, 1)
                        wait(dve, rden_made, u + 1)
                        dve.tensor_tensor(On[:, s, :].rearrange("p (h d) -> p h d", d=DH), Ov[:, :, 0:DH],
                                          rden[:, s, :].unsqueeze(2).broadcast_to([P, H, DH]), ALU.mult
                                          ).then_inc(on_made, 1)
            run_steps(dve, NT, DEPTH, RING, step)
            dve.wait_ge(stats_made, NT)


def split_weights(c, name, parts, sems, whole=()):
    nc = c.nc
    with ExitStack() as ctx:
        staged = [ctx.enter_context(nc.sbuf_tensor(f"{name}_staged{i}", shape, F32))
                  for i, (shape, _, _, _) in enumerate(parts)]
        load_weights(c, [*whole] + [(pick(t), src) for t, (_, loads, _, _) in zip(staged, parts)
                                    for pick, src in loads],
                     lambda n: sems(f"{name}_{n}"))
        block = ctx.enter_context(nc.Block())
        hi_made, lo_made = sems(name + "_hi"), sems(name + "_lo")

        @block.scalar
        def _(act):
            for t, (shape, _, hi, lo) in zip(staged, parts):
                act.activation(hi, t[tuple(slice(None) for _ in shape)], ACT.Copy).then_inc(hi_made, 1)

        @block.vector
        def _(dve):
            for i, (t, (shape, _, hi, lo)) in enumerate(zip(staged, parts)):
                dve.wait_ge(hi_made, i + 1)
                dve.tensor_tensor(lo, t[tuple(slice(None) for _ in shape)], hi, ALU.subtract).then_inc(lo_made, 1)
            dve.wait_ge(lo_made, len(parts))


def products(pe, out, whi, wlo, xhi, xlo, first=True, last=True):
    pe.matmul(out, whi, xlo, start=first, stop=False, skip_group_check=True)
    pe.matmul(out, wlo, xhi, start=False, stop=False, skip_group_check=True)
    return pe.matmul(out, whi, xhi, start=False, stop=last, skip_group_check=True)


GT = 4
N4 = GT * P


class Front:

    def __init__(self, c, name, ctx, sems):
        nc = c.nc
        self.c = c
        self.xhat = ctx.enter_context(nc.sbuf_tensor(name + "_xhat", [P, 2, GT, P], F32))
        self.xh = ctx.enter_context(nc.sbuf_tensor(name + "_xh", [P, 2, N4], F32R))
        self.xl = ctx.enter_context(nc.sbuf_tensor(name + "_xl", [P, 2, N4], F32R))
        self.psT = ctx.enter_context(nc.psum_tensor(name + "_psT", [P, N4], F32))
        self.xhat_made, self.xT_done = sems(name + "_xhat_made"), sems(name + "_xT_done")
        self.hi_made, self.lo_made = sems(name + "_xh_made"), sems(name + "_xl_made")

    def vector_norm(self, dve, u, s):
        wait(dve, self.xT_done, u - 1)
        for k in range(GT):
            t = u * GT + k
            last = dve.tensor_scalar(self.xhat[:, s, k, :], self.c.x[:, t, :], self.c.rstd[:, bass.ds(t, 1)],
                                     self.c.nmr[:, bass.ds(t, 1)], ALU.mult, ALU.add)
        last.then_inc(self.xhat_made, 1)

    def scalar_norm(self, act, u, s):
        wait(act, self.xT_done, u - 1)
        for k in range(GT):
            t = u * GT + k
            last = act.activation(self.xhat[:, s, k, :], self.c.x[:, t, :], ACT.Identity,
                                  bias=self.c.nmr[:, bass.ds(t, 1)], scale=self.c.rstd[:, bass.ds(t, 1)])
        last.then_inc(self.xhat_made, 1)

    def tensor_transpose(self, pe, u, s):
        wait(pe, self.xhat_made, u + 1)
        wait(pe, self.lo_made, u)
        for k in range(GT):
            last = pe.transpose(self.psT[:, P * k:P * k + P], self.xhat[:, s, k, :], self.c.ident[:, :])
        last.then_inc(self.xT_done, 1)

    def scalar_hi(self, act, u, s):
        wait(act, self.xT_done, u + 1)
        act.activation(self.xh[:, s, :], self.psT[:, :], ACT.Copy).then_inc(self.hi_made, 1)

    def vector_lo(self, dve, u, s):
        wait(dve, self.hi_made, u + 1)
        dve.tensor_tensor(self.xl[:, s, :], self.psT[:, :], self.xh[:, s, :], ALU.subtract).then_inc(self.lo_made, 1)


def steps_of(NG):
    def at(i, r, lag):
        u = i - lag
        if not isinstance(u, int) or 0 <= u < NG:
            yield u, (r - lag) % 2
    return at


def gate_logits(c, name, sems, gate, bias, E, r=None):
    nc, NG = c.nc, c.NT // GT
    with ExitStack() as ctx:
        f = Front(c, name, ctx, sems)
        lT = ctx.enter_context(nc.sbuf_tensor(name + "_logitsT", [P, 2, N4], F32))
        psL = ctx.enter_context(nc.psum_tensor(name + "_psL", [P, N4], F32))
        psG = ctx.enter_context(nc.psum_tensor(name + "_psG", [P, N4], F32))
        l_done, l_kept = sems(name + "_l_done"), sems(name + "_l_kept")
        g_done, g_kept, cleared = sems(name + "_g_done"), sems(name + "_g_kept"), sems(name + "_cleared")
        if r:
            zero = ctx.enter_context(nc.sbuf_tensor(name + "_zero", [P, N4], F32))
            zero_made, zeroed, normed = sems(name + "_zero"), sems(name + "_zeroed"), sems(name + "_normed")
        block = ctx.enter_context(nc.Block())
        at = steps_of(NG)

        @block.vector
        def _(dve):
            def step(i, r):
                for u, s in at(i, r, 3):
                    wait(dve, g_done, u + 1)
                    dve.tensor_copy(c.logits[:, bass.ds(u * GT, GT), 0:E],
                                    psG[:, :].rearrange("p (t e) -> p t e", e=P)[:, :, 0:E]).then_inc(g_kept, 1)
                for u, s in at(i, r, 0):
                    f.vector_norm(dve, u, s)
                for u, s in at(i, r, 1):
                    wait(dve, l_done, u - 1)
                    f.vector_lo(dve, u, s)
            run_steps(dve, NG, 4, 2, step)
            dve.wait_ge(g_kept, NG)

        @block.gpsimd
        def _(pool):
            if r:
                pool.memset(zero[:, :], 0.0).then_inc(zero_made, 1)
            pool.memset(lT[:, :, :], 0.0).then_inc(cleared, 1)

        @block.sync
        def _(sp):
            if r:
                sp.wait_ge(zero_made, 1)
                for g in range(r.groups):
                    sp.dma_start(r.sorted_x[g * N4:g * N4 + N4, :].rearrange("(t p) d -> p t d", p=P),
                                 zero[:, :].rearrange("p (t d) -> p t d", d=P)).then_inc(zeroed, 16)
                sp.wait_ge(zeroed, 16 * r.groups)

        @block.scalar
        def _(act):
            act.wait_ge(cleared, 1)

            def step(i, r_):
                for u, s in at(i, r_, 0):
                    for k in range(GT if r else 0):
                        t = u * GT + k
                        act.activation(r.xhat[:, t, :], c.x[:, t, :], ACT.Identity, bias=c.nmr[:, bass.ds(t, 1)],
                                       scale=c.rstd[:, bass.ds(t, 1)]).then_inc(normed, 1)
                for u, s in at(i, r_, 1):
                    wait(act, l_done, u - 1)
                    f.scalar_hi(act, u, s)
                for u, s in at(i, r_, 2):
                    wait(act, l_done, u + 1)
                    wait(act, g_done, u - 1)
                    act.activation(lT[0:E, s, :], psL[0:E, :], ACT.Identity, bias=bias).then_inc(l_kept, 1)
            run_steps(act, NG, 4, 2, step)
            if r:
                act.wait_ge(normed, c.NT)

        @block.tensor
        def _(pe):
            def step(i, r):
                for u, s in at(i, r, 1):
                    f.tensor_transpose(pe, u, s)
                for u, s in at(i, r, 2):
                    wait(pe, f.lo_made, u + 1)
                    wait(pe, l_kept, u)
                    products(pe, psL[0:E, :], gate[0], gate[1], f.xh[:, s, :], f.xl[:, s, :]).then_inc(l_done, 1)
                for u, s in at(i, r, 3):
                    wait(pe, l_kept, u + 1)
                    wait(pe, g_kept, u)
                    for k in range(GT):
                        last = pe.transpose(psG[:, P * k:P * k + P], lT[:, s, P * k:P * k + P], c.ident[:, :])
                    last.then_inc(g_done, 1)
            run_steps(pe, NG, 4, 2, step)


def chain(eng, sem):
    n = 0

    def run(instruction):
        nonlocal n
        n += 1
        instruction.then_inc(sem, 1)
        eng.wait_ge(sem, n)
    return run


def soft_moe(c, name, sems, ew_hi, ew_lo, eb_blocks, E=8, THRESHOLD=0.1, HALF=4):
    nc, NT, NG = c.nc, c.NT, c.NT // GT
    with ExitStack() as ctx:
        block = ctx.enter_context(nc.Block())
        red = ctx.enter_context(nc.sbuf_tensor(name + "_red", [P, NT], F32))
        less, ex, step = sems(name + "_less"), sems(name + "_exp"), sems(name + "_gates")
        L = c.logits[:, :, 0:E]
        R = red[:, :].unsqueeze(2).broadcast_to([P, NT, E])

        @block.vector
        def _(dve):
            run = chain(dve, step)
            run(dve.tensor_reduce(red[:, :], L, AX.X, ALU.max))
            dve.tensor_tensor(L, L, R, ALU.subtract).then_inc(less, 1)
            dve.wait_ge(ex, 1)
            run(dve.tensor_reduce(red[:, :], L, AX.X, ALU.add))
            run(dve.reciprocal(red[:, :], red[:, :]))
            run(dve.tensor_tensor(L, L, R, ALU.mult))
            run(dve.scalar_tensor_tensor(out=L, in0=L, scalar=THRESHOLD, in1=L, op0=ALU.is_ge, op1=ALU.mult))
            run(dve.tensor_reduce(red[:, :], L, AX.X, ALU.add))
            run(dve.scalar_tensor_tensor(out=red[:, :], in0=red[:, :], scalar=0.0, in1=red[:, :],
                                         op0=ALU.is_equal, op1=ALU.add))
            run(dve.reciprocal(red[:, :], red[:, :]))
            run(dve.tensor_tensor(L, L, R, ALU.mult))

        @block.scalar
        def _(act):
            act.wait_ge(less, 1)
            act.activation(L, L, ACT.Exp).then_inc(ex, 1)

    with ExitStack() as ctx:
        f = Front(c, name, ctx, sems)
        wq = ctx.enter_context(nc.sbuf_tensor(name + "_w4", [P, 2, GT * E], F32))
        wT = ctx.enter_context(nc.sbuf_tensor(name + "_w4T", [GT * E, 2, P], F32))
        psE = ctx.enter_context(nc.psum_tensor(name + "_psE", [P, 2, E * P], F32))
        psW = ctx.enter_context(nc.psum_tensor(name + "_psW", [P, N4], F32))
        psB = ctx.enter_context(nc.psum_tensor(name + "_psB", [P, N4], F32))
        wq_made, wT_done, wT_kept = sems(name + "_w4_made"), sems(name + "_w4T_done"), sems(name + "_w4T_kept")
        bias_done, bias_summed = sems(name + "_bias_done"), sems(name + "_bias_summed")
        parts = ctx.enter_context(nc.sbuf_tensor(name + "_parts", [P, 2, HALF, P], F32))
        total = ctx.enter_context(nc.sbuf_tensor(name + "_total", [P, 2, GT, P], F32))
        odd = ctx.enter_context(nc.sbuf_tensor(name + "_odd", [P, 2, GT, P], F32))
        odd_added = sems(name + "_odd_added")
        e_done, summed, stats_made = sems(name + "_e_done"), sems(name + "_summed"), sems(name + "_stats")
        added = sems(name + "_added")
        parts_made, folded, parts_summed = sems(name + "_parts_made"), sems(name + "_folded"), sems(name + "_psummed")
        block = ctx.enter_context(nc.Block())
        at = steps_of(NG)
        SUMS = E - HALF

        @block.tensor
        def _(pe):
            def step(i, r):
                for k in range(GT):
                    for u, s in at(i, r, 2):
                        if k == 0:
                            wait(pe, wT_kept, u + 1)
                            wait(pe, bias_summed, u)
                            pe.matmul(psB[:, :], wT[:, s, :], eb_blocks, start=True, stop=True
                                      ).then_inc(bias_done, 1)
                            wait(pe, f.lo_made, u + 1)
                        t = u * GT + k
                        tok = slice(P * k, P * k + P)
                        wait(pe, summed, (t - 1) * SUMS)
                        wait(pe, parts_made, t - 1)
                        for half in (1, 0):
                            cols = slice(512 * half, 512 * half + 512)
                            out = psE[:, k % 2, cols]
                            pe.matmul(out, f.xl[:, s, tok], ew_hi[:, cols], start=True, stop=False,
                                      skip_group_check=True)
                            pe.matmul(out, f.xh[:, s, tok], ew_lo[:, cols], start=False, stop=False,
                                      skip_group_check=True)
                            mm = pe.matmul(out, f.xh[:, s, tok], ew_hi[:, cols], start=False, stop=True,
                                           skip_group_check=True)
                            mm.then_inc(e_done, 1)
                    if k == 1:
                        for u, s in at(i, r, 1):
                            f.tensor_transpose(pe, u, s)
                            wait(pe, wq_made, u + 1)
                            wait(pe, wT_kept, u)
                            pe.transpose(psW[0:GT * E, 0:P], wq[:, s, :], c.ident[:, :]).then_inc(wT_done, 1)
            run_steps(pe, NG, 4, 2, step)

        @block.scalar
        def _(act):
            def step(i, r):
                for k in range(GT):
                    for u, s in at(i, r, 2):
                        t = u * GT + k
                        wait(act, e_done, 2 * t + 1)
                        wait(act, parts_summed, t - 1)
                        for j in range(HALF):
                            e = SUMS + j
                            last = act.activation(parts[:, k % 2, j, :], psE[:, k % 2, P * e:P * e + P], ACT.Copy,
                                                  scale=c.logits[:, t, e:e + 1])
                        last.then_inc(parts_made, 1)
                    if k == 1:
                        for u, s in at(i, r, 1):
                            wait(act, e_done, 2 * (u - 1) * GT)
                            f.scalar_hi(act, u, s)
                            wait(act, wT_done, u + 1)
                            wait(act, bias_done, u - 1)
                            act.activation(wT[:, s, :], psW[0:GT * E, 0:P], ACT.Copy).then_inc(wT_kept, 1)
                    if k == 3:
                        for u, s in at(i, r, 0):
                            f.scalar_norm(act, u, s)
            run_steps(act, NG, 4, 2, step)

        @block.gpsimd
        def _(pool):
            def step(i, r):
                for k in range(GT):
                    for u, s in at(i, r, 2):
                        t = u * GT + k
                        wait(pool, parts_made, t + 1)
                        pool.tensor_tensor(parts[:, k % 2, 0:2, :], parts[:, k % 2, 0:2, :],
                                           parts[:, k % 2, 2:4, :], ALU.add).then_inc(folded, 1)
                        wait(pool, added, u - 1)
                        wait(pool, folded, t + 1)
                        pool.tensor_tensor(total[:, s, k, :], parts[:, k % 2, 0, :], parts[:, k % 2, 1, :], ALU.add
                                           ).then_inc(parts_summed, 1)
            run_steps(pool, NG, 4, 2, step)

        @block.vector
        def _(dve):
            def step(i, r):
                for k in range(GT):
                    for u, s in at(i, r, 2):
                        if k == 0:
                            wait(dve, bias_done, u + 1)
                            dve.tensor_tensor(c.x[:, bass.ds(u * GT, GT), :],
                                              psB[:, :].rearrange("p (t d) -> p t d", d=P),
                                              c.x[:, bass.ds(u * GT, GT), :], ALU.add).then_inc(bias_summed, 1)
                            wait(dve, bias_summed, u + 1)
                        t = u * GT + k
                        wait(dve, e_done, 2 * t + 2)
                        for e in range(SUMS):
                            if e >= 2:
                                wait(dve, summed, t * SUMS + e - 1)
                            out_of = psE[:, k % 2, P * e:P * e + P]
                            if e == 1:
                                dve.tensor_scalar(odd[:, s, k, :], out_of, c.logits[:, t, e:e + 1], None, ALU.mult
                                                  ).then_inc(summed, 1)
                            else:
                                onto = odd[:, s, k, :] if e % 2 else c.x[:, t, :]
                                dve.scalar_tensor_tensor(out=onto, in0=out_of, scalar=c.logits[:, t, e:e + 1],
                                                         in1=onto, op0=ALU.mult, op1=ALU.add).then_inc(summed, 1)
                    for u, s in at(i, r, 3):
                        t = u * GT + k
                        if k == 0:
                            wait(dve, parts_summed, (u + 1) * GT)
                            wait(dve, summed, (u + 1) * GT * SUMS)
                            x4 = c.x[:, bass.ds(u * GT, GT), :]
                            dve.tensor_tensor(x4, x4, total[:, s], ALU.add).then_inc(added, 1)
                            wait(dve, added, u + 1)
                            dve.tensor_tensor(x4, x4, odd[:, s], ALU.add).then_inc(odd_added, 1)
                            wait(dve, odd_added, u + 1)
                        dve.bn_stats(c.stats[:, t, :], c.x[:, t, :]).then_inc(stats_made, 1)
                    for u, s in at(i, r, 0):
                        if k == 3:
                            wait(dve, wT_done, u - 1)
                            dve.tensor_copy(wq[:, s, :].rearrange("p (t e) -> p t e", e=E),
                                            c.logits[:, bass.ds(u * GT, GT), 0:E]).then_inc(wq_made, 1)
                    for u, s in at(i, r, 1):
                        if k == 2:
                            wait(dve, e_done, 2 * (u - 1) * GT)
                            f.vector_lo(dve, u, s)
            run_steps(dve, NG, 4, 2, step)
            dve.wait_ge(stats_made, NT)


def routed_relu(c, name, sems, gd, w1, b1, w2, out_bias, HC=4):
    nc, NT, NG = c.nc, c.NT, c.NT // GT
    UNITS = 3 * HC
    with ExitStack() as ctx:
        f = Front(c, name, ctx, sems)
        sb = lambda n, shape, dt=F32: ctx.enter_context(nc.sbuf_tensor(f"{name}_{n}", shape, dt))
        pb = lambda n, shape: ctx.enter_context(nc.psum_tensor(f"{name}_{n}", shape, F32))
        sem = lambda n: sems(f"{name}_{n}")
        eh, el = sb("eh", [P, 2, 2, N4], F32R), sb("el", [P, 2, 2, N4], F32R)
        h = sb("h", [P, 3, N4])
        hh, hl = sb("hh", [P, 3, N4], F32R), sb("hl", [P, 3, N4], F32R)
        ysb = sb("y", [P, 2, N4])
        psD, psH, psY, psO = pb("D", [P, N4]), pb("H", [P, 2, N4]), pb("Y", [P, 2, N4]), pb("O", [P, N4])
        d_done, masked = sem("d_done"), sem("masked")
        h_done, h_kept, hh_made = sem("h_done"), sem("h_kept"), sem("hh_made")
        hl_dve, hl_pool = sem("hl_dve"), sem("hl_pool")
        used, y_done, y_kept, o_done = sem("used"), sem("y_done"), sem("y_kept"), sem("o_done")
        based, summed, stats_made, split0 = sem("based"), sem("summed"), sem("stats"), sem("split0")
        block = ctx.enter_context(nc.Block())
        at = steps_of(NG)

        def hl_made(u, q):
            if q % 3 == 0:
                return hl_dve, u * (UNITS // 3) + q // 3 + 1
            return hl_pool, u * (2 * UNITS // 3) + 2 * (q // 3) + q % 3

        def hl_made_before(u, q):
            s_, n_ = hl_made(u, q)
            return s_, n_ - (1 if q % 3 == 0 else 2)

        @block.tensor
        def _(pe):
            def second(u, s, q):
                wait(pe, *hl_made(u, q))
                if q == 0:
                    wait(pe, y_kept, u - 1)
                mm = products(pe, psY[:, s, :], w2[0][:, q, :], w2[1][:, q, :], hh[:, q % 3, :], hl[:, q % 3, :],
                              first=q == 0, last=q == UNITS - 1)
                mm.then_inc(used, 1)

            def step(i, r):
                for q in range(UNITS):
                    for u, s in at(i, r, 1):
                        n = u * UNITS + q
                        if q == 0:
                            wait(pe, f.lo_made, u + 1)
                        if q == HC:
                            wait(pe, split0, u + 1)
                        wait(pe, h_kept, n - 1)
                        e = q // HC - 1
                        xh, xl = (f.xh[:, s, :], f.xl[:, s, :]) if e < 0 else (eh[:, s, e, :], el[:, s, e, :])
                        products(pe, psH[:, q % 2, :], w1[0][:, q * P:q * P + P], w1[1][:, q * P:q * P + P],
                                 xh, xl).then_inc(h_done, 1)
                        if q >= 3:
                            second(u, s, q - 3)
                    for u, s in at(i, r, 2):
                        if q < 3:
                            second(u, s, q + UNITS - 3)
                        if q == 4:
                            wait(pe, y_kept, u + 1)
                            wait(pe, summed, u * GT)
                            for k in range(GT):
                                mm = pe.transpose(psO[:, P * k:P * k + P], ysb[:, s, P * k:P * k + P],
                                                  c.ident[:, :])
                            mm.then_inc(o_done, 1)
                    for u, s in at(i, r, 0):
                        if q == 5:
                            f.tensor_transpose(pe, u, s)
                        if q == 8:
                            wait(pe, f.lo_made, u + 1)
                            wait(pe, masked, 2 * u)
                            products(pe, psD[:, :], gd[0], gd[1], f.xh[:, s, :], f.xl[:, s, :]).then_inc(d_done, 1)
            run_steps(pe, NG, 2, 2, step)

        @block.scalar
        def _(act):
            def step(i, r):
                for q in range(UNITS):
                    for u, s in at(i, r, 1):
                        n = u * UNITS + q
                        wait(act, h_done, n + 1)
                        wait(act, hh_made, n - 2)
                        wait(act, *hl_made_before(u, q))
                        act.activation(h[:, q % 3, :], psH[:, q % 2, :], ACT.Relu, bias=b1[:, q:q + 1]
                                       ).then_inc(h_kept, 1)
                    for u, s in at(i, r, 2):
                        if q == 2:
                            wait(act, used, u * UNITS + UNITS)
                            wait(act, o_done, u - 1)
                            act.activation(ysb[:, s, :], psY[:, s, :], ACT.Copy).then_inc(y_kept, 1)
                    for u, s in at(i, r, 0):
                        if q == 5:
                            wait(act, h_done, (u - 1) * UNITS)
                            f.scalar_hi(act, u, s)
            run_steps(act, NG, 2, 2, step)

        @block.gpsimd
        def _(pool):
            def step(i, r):
                for q in range(UNITS):
                    for u, s in at(i, r, 1):
                        n = u * UNITS + q
                        if q % 3:
                            wait(pool, hh_made, n + 1)
                            wait(pool, used, n - 2)
                            pool.tensor_tensor(hl[:, q % 3, :], h[:, q % 3, :], hh[:, q % 3, :], ALU.subtract
                                               ).then_inc(hl_pool, 1)
            run_steps(pool, NG, 2, 2, step)

        @block.vector
        def _(dve):
            def step(i, r):
                for q in range(UNITS):
                    for u, s in at(i, r, 1):
                        n = u * UNITS + q
                        wait(dve, h_kept, n + 1)
                        wait(dve, used, n - 2)
                        dve.tensor_copy(hh[:, q % 3, :], h[:, q % 3, :]).then_inc(hh_made, 1)
                        if q % 3 == 0:
                            wait(dve, hh_made, n + 1)
                            dve.tensor_tensor(hl[:, q % 3, :], h[:, q % 3, :], hh[:, q % 3, :], ALU.subtract
                                              ).then_inc(hl_dve, 1)
                    for u, s in at(i, r, 2):
                        xs = c.x[:, bass.ds(u * GT, GT), :]
                        if q == 3:
                            dve.tensor_tensor(xs, xs, out_bias.unsqueeze(1).broadcast_to([P, GT, P]), ALU.add
                                              ).then_inc(based, 1)
                        if q == 5:
                            wait(dve, based, u + 1)
                            wait(dve, o_done, u + 1)
                            for k in range(GT):
                                t = u * GT + k
                                dve.tensor_tensor(c.x[:, t, :], psO[:, P * k:P * k + P], c.x[:, t, :], ALU.add
                                                  ).then_inc(summed, 1)
                        if q == 7:
                            for k in range(GT):
                                t = u * GT + k
                                wait(dve, summed, t + 1)
                                dve.bn_stats(c.stats[:, t, :], c.x[:, t, :]).then_inc(stats_made, 1)
                    for u, s in at(i, r, 0):
                        if q == 3:
                            f.vector_norm(dve, u, s)
                        if q == 6:
                            wait(dve, h_done, (u - 1) * UNITS)
                            f.vector_lo(dve, u, s)
                        for at_q, dst, src in ((9, eh, f.xh), (10, el, f.xl)):
                            if q == at_q:
                                wait(dve, d_done, u + 1)
                                wait(dve, f.lo_made, u + 1)
                                dve.scalar_tensor_tensor(out=dst[:, s, 1, :], in0=psD[:, :], scalar=0.0,
                                                         in1=src[:, s, :], op0=ALU.is_gt, op1=ALU.mult
                                                         ).then_inc(masked, 1)
                        if q == 11:
                            wait(dve, masked, 2 * u + 2)
                            dve.tensor_tensor(eh[:, s, 0, :], f.xh[:, s, :], eh[:, s, 1, :], ALU.subtract)
                            dve.tensor_tensor(el[:, s, 0, :], f.xl[:, s, :], el[:, s, 1, :], ALU.subtract
                                              ).then_inc(split0, 1)
            run_steps(dve, NG, 2, 2, step)
            dve.wait_ge(stats_made, NT)


def route_tokens(c, name, sems, r, E):
    nc, NT = c.nc, c.NT
    NR = r.groups
    MOST = -(-NT * P // N4)
    with ExitStack() as ctx:
        sb = lambda n, shape, dt=F32: ctx.enter_context(nc.sbuf_tensor(f"{name}_{n}", shape, dt))
        sem = lambda n: sems(f"{name}_{n}")
        red = sb("red", [P, NT])
        first = sb("first", [P, E])
        hot, hot_bf = sb("hot", [P, NT, E]), sb("hot_bf", [P, NT, E], BF16)
        before, one = sb("before", [P, P], BF16), sb("one", [P, P], BF16)
        counts = sb("counts", [P, 2, NT, E])
        steps_of_n, group_no = sb("steps_of_n", [P, MOST]), sb("group_no", [P, NR])
        over = sb("over", [P, E, MOST])
        need, start = sb("need", [P, E]), sb("start", [P, E + 1])
        row0 = sb("row0", [P, NR])
        past = sb("past", [P, NR, E - 1])
        own = sb("own", [P, 1])
        psW = ctx.enter_context(nc.psum_tensor(name + "_psW", [P, NT * E], F32))
        psC = ctx.enter_context(nc.psum_tensor(name + "_psC", [P, NT * E], F32))
        psI = ctx.enter_context(nc.psum_tensor(name + "_psI", [P, 2], F32))
        clipped, sig, step, const = sem("clipped"), sem("sigmoid"), sem("route"), sem("const")
        hot_made, counted = sem("hot_made"), sem("counted")
        block = ctx.enter_context(nc.Block())
        L = c.logits[:, :, 0:E]
        R = red[:, :].unsqueeze(2).broadcast_to([P, NT, E])
        CONSTS = E + MOST + NR + 3

        @block.gpsimd
        def _(pool):
            run = chain(pool, const)
            for e in range(E):
                run(pool.memset(first[:, e:e + 1], float(E - e)))
            for m in range(MOST):
                run(pool.memset(steps_of_n[:, m:m + 1], float(m * N4)))
            for g in range(NR):
                run(pool.memset(group_no[:, g:g + 1], float(g)))
            run(pool.memset(one[:, :], 1.0))
            run(pool.memset(before[:, :], 1.0))
            run(pool.affine_select(out=before[:, :], in_=before[:, :], compare_op=ALU.is_gt, fill=0.0,
                                   base=0, pattern=[[1, P]], channel_multiplier=-1))

        @block.scalar
        def _(act):
            act.wait_ge(clipped, 1)
            act.activation(L, L, ACT.Sigmoid).then_inc(sig, 1)

        @block.tensor
        def _(pe):
            pe.wait_ge(const, CONSTS)
            pe.matmul(psI[:, 0:2], before[:, :], one[:, 0:2], start=True, stop=True)
            pe.wait_ge(hot_made, 1)
            rhs = hot_bf[:, :, :].rearrange("p t e -> p (t e)")
            pe.matmul(psW[:, :], before[:, :], rhs, start=True, stop=True)
            pe.matmul(psC[:, :], one[:, :], rhs, start=True, stop=True).then_inc(counted, 1)

        @block.vector
        def _(dve):
            run = chain(dve, step)
            dve.tensor_scalar(L, L, -50.0, 50.0, ALU.max, ALU.min).then_inc(clipped, 1)
            dve.wait_ge(sig, 1)
            run(dve.tensor_reduce(red[:, :], L, AX.X, ALU.max))
            run(dve.tensor_scalar(r.w_routed[:, :], red[:, :], 1e-8, 1.0 - 1e-8, ALU.max, ALU.min))
            run(dve.tensor_scalar(r.w_shared[:, :], r.w_routed[:, :], 0.5, 1e-8, ALU.add, ALU.add))
            run(dve.tensor_scalar(r.w_shared[:, :], r.w_shared[:, :], 0.5, 2.0, ALU.max, ALU.min))
            run(dve.reciprocal(r.w_shared[:, :], r.w_shared[:, :]))
            run(dve.tensor_tensor(r.w_routed[:, :], r.w_routed[:, :], r.w_shared[:, :], ALU.mult))
            run(dve.tensor_scalar(r.w_shared[:, :], r.w_shared[:, :], 0.5, None, ALU.mult))
            dve.wait_ge(const, CONSTS)
            run(dve.tensor_tensor(L, L, R, ALU.is_equal))
            run(dve.tensor_tensor(L, L, first[:, :].unsqueeze(1).broadcast_to([P, NT, E]), ALU.mult))
            run(dve.tensor_reduce(red[:, :], L, AX.X, ALU.max))
            run(dve.tensor_tensor(hot[:, :, :], L, R, ALU.is_equal))
            dve.tensor_copy(hot_bf[:, :, :], hot[:, :, :]).then_inc(hot_made, 1)
            dve.wait_ge(counted, 1)
            run(dve.tensor_copy(own[:, :], psI[:, 0:1]))
            run(dve.tensor_copy(counts[:, 0], psC[:, :].rearrange("p (t e) -> p t e", e=E)))
            now, stride = 0, 1
            while stride < NT:
                run(dve.tensor_tensor(counts[:, 1 - now, stride:NT], counts[:, now, stride:NT],
                                      counts[:, now, 0:NT - stride], ALU.add))
                run(dve.tensor_copy(counts[:, 1 - now, 0:stride], counts[:, now, 0:stride]))
                now, stride = 1 - now, stride * 2
            up_to, mine = counts[:, now], counts[:, 1 - now]
            run(dve.tensor_tensor(over[:, :, :], up_to[:, NT - 1, :].unsqueeze(2).broadcast_to([P, E, MOST]),
                                  steps_of_n[:, :].unsqueeze(1).broadcast_to([P, E, MOST]), ALU.is_gt))
            run(dve.tensor_reduce(need[:, :], over[:, :, :], AX.X, ALU.add))
            run(dve.memset(start[:, 0:1], 0.0))
            for e in range(E):
                run(dve.tensor_tensor(start[:, e + 1:e + 2], start[:, e:e + 1], need[:, e:e + 1], ALU.add))
            run(dve.tensor_tensor(past[:, :, :], group_no[:, :].unsqueeze(2).broadcast_to([P, NR, E - 1]),
                                  start[:, 1:E].unsqueeze(1).broadcast_to([P, NR, E - 1]), ALU.is_ge))
            run(dve.tensor_reduce(row0[:, :], past[:, :, :], AX.X, ALU.add))
            run(dve.tensor_scalar(row0[:, :], row0[:, :], float(P), own[:, 0:1], ALU.mult, ALU.add))
            run(dve.tensor_copy(r.weight_row[:, :], row0[:, :]))
            run(dve.tensor_tensor(mine, up_to, psC[:, :].rearrange("p (t e) -> p t e", e=E), ALU.subtract))
            run(dve.tensor_tensor(mine, mine, psW[:, :].rearrange("p (t e) -> p t e", e=E), ALU.add))
            run(dve.tensor_scalar(start[:, :], start[:, :], float(N4), None, ALU.mult))
            run(dve.tensor_tensor(mine, mine, start[:, 0:E].unsqueeze(1).broadcast_to([P, NT, E]), ALU.add))
            run(dve.tensor_tensor(mine, mine, hot[:, :, :], ALU.mult))
            run(dve.tensor_reduce(red[:, :], mine, AX.X, ALU.add))
            run(dve.tensor_copy(r.place[:, :], red[:, :]))


def swiglu(c, name, sems, r, routed, IP):
    nc, NT = c.nc, c.NT
    NG = r.groups if routed else NT // GT
    IC = IP // P
    WS = 2 if routed else 1
    with ExitStack() as ctx:
        f = Front(c, name, ctx, sems)
        sb = lambda n, shape, dt=F32: ctx.enter_context(nc.sbuf_tensor(f"{name}_{n}", shape, dt))
        pb = lambda n, shape: ctx.enter_context(nc.psum_tensor(f"{name}_{n}", shape, F32))
        sem = lambda n: sems(f"{name}_{n}")
        w, wh, wl = sb("w", [P, WS, 3 * IP]), sb("wh", [P, WS, 3 * IP], F32R), sb("wl", [P, WS, 3 * IP], F32R)
        act_sb, h = sb("act", [P, 2, N4]), sb("h", [P, 2, N4])
        hh, hl = sb("hh", [P, 2, N4], F32R), sb("hl", [P, 2, N4], F32R)
        yT = sb("yT", [P, 2, N4])
        psA, psG, psY, psO = pb("A", [P, 2, N4]), pb("G", [P, 2, N4]), pb("Y", [P, 2, N4]), pb("O", [P, N4])
        a_done, a_kept, h_made = sem("a_done"), sem("a_kept"), sem("h_made")
        hh_made, hl_made, used = sem("hh_made"), sem("hl_made"), sem("used")
        y_kept, o_done, o_kept = sem("y_kept"), sem("o_done"), sem("o_kept")
        w_hi, w_lo = sem("w_hi"), sem("w_lo")
        W13, W2 = slice(0, 2 * IP), slice(2 * IP, 3 * IP)
        w_loaded = [sem(f"w_loaded{q}") for q in range(WS)]
        if routed:
            y_out = sb("y_out", [P, 2, GT, P])
            row = sb("row", [P, 2, 1], I32)
            x_loaded = [sem(f"x_loaded{q}") for q in range(2)]
            y_stored = [sem(f"y_stored{q}") for q in range(2)]
            row_made = sem("row_made")
        else:
            scattered = sem("scattered")
        block = ctx.enter_context(nc.Block())
        at = steps_of(NG)

        @block.sync
        def _(sp):
            if routed:
                def step(i, r_):
                    for u, s in at(i, r_, 0):
                        wait(sp, f.xT_done, u - 1)
                        sp.dma_start(f.xhat[:, s],
                                     r.sorted_x[bass.ds(u * N4, N4), :].rearrange("(t p) d -> p t d", p=P)
                                     ).then_inc(x_loaded[s], 16)
                    for u, s in at(i, r_, 3):
                        wait(sp, o_kept, u + 1)
                        sp.dma_start(r.sorted_y[bass.ds(u * N4, N4), :].rearrange("(t p) d -> p t d", p=P),
                                     y_out[:, s]).then_inc(y_stored[s], 16)
                run_steps(sp, NG, 4, 2, step)
                for q in range(2):
                    sp.wait_ge(y_stored[q], 16 * (NG // 2))
            else:
                sp.dma_start(w[:, 0, :], r.shared_w).then_inc(w_loaded[0], 16)

        @block.gpsimd
        def _(pool):
            if routed:
                def step(i, r_):
                    for u, s in at(i, r_, 0):
                        wait(pool, w_lo, 2 * u - 2)
                        pool.tensor_copy(row[:, s, :], r.weight_row[:, bass.ds(u, 1)]).then_inc(row_made, 1)
                        wait(pool, row_made, u + 1)
                    for q in range(IC):
                        for u, s in at(i, r_, 2):
                            n, z = u * IC + q, (s + q) % 2
                            wait(pool, hh_made, n + 1)
                            wait(pool, used, n - 1)
                            pool.tensor_tensor(hl[:, z, :], h[:, z, :], hh[:, z, :], ALU.subtract
                                               ).then_inc(hl_made, 1)
                        for u, s in at(i, r_, 0):
                            if q == 0:
                                pool.indirect_dma_start(w[:, s, :], None, r.expert_w,
                                                        bass.IndirectOffsetOnAxis(ap=row[:, s, :], axis=0)
                                                        ).then_inc(w_loaded[s], 16)
                run_steps(pool, NG, 4, 2, step)
            else:
                for t in range(NT):
                    pool.indirect_dma_start(r.sorted_x, bass.IndirectOffsetOnAxis(ap=r.place[:, t:t + 1], axis=0),
                                            r.xhat[:, t, :], None).then_inc(scattered, 16)
                pool.wait_ge(scattered, 16 * NT)

        @block.tensor
        def _(pe):
            def second(u, s, q):
                n, z = u * IC + q, (s + q) % 2
                wait(pe, hl_made, n + 1)
                if q == 0:
                    wait(pe, y_kept, u - 1)
                    if routed:
                        wait(pe, w_lo, 2 * u + 2)
                ws = s if routed else 0
                cols = slice(2 * IP + q * P, 2 * IP + q * P + P)
                products(pe, psY[:, s, :], wh[:, ws, cols], wl[:, ws, cols], hh[:, z, :], hl[:, z, :],
                         first=q == 0, last=q == IC - 1).then_inc(used, 1)

            def step(i, r_):
                for q in range(IC):
                    for u, s in at(i, r_, 2):
                        n, z = u * IC + q, (s + q) % 2
                        if q == 0:
                            wait(pe, w_lo, 2 * u + 1 if routed else 2)
                            wait(pe, f.lo_made, u + 1)
                        wait(pe, a_kept, n - 1)
                        wait(pe, h_made, n - 1)
                        ws = s if routed else 0
                        for ps, o in ((psA, 0), (psG, IP)):
                            cols = slice(o + q * P, o + q * P + P)
                            mm = products(pe, ps[:, z, :], wh[:, ws, cols], wl[:, ws, cols], f.xh[:, s, :],
                                          f.xl[:, s, :])
                        mm.then_inc(a_done, 1)
                        if q >= 2:
                            second(u, s, q - 2)
                    if q < 2:
                        for u, s in at(i, r_, 3):
                            second(u, s, q + IC - 2)
                    if q == 1:
                        for u, s in at(i, r_, 1):
                            if routed:
                                wait(pe, x_loaded[s], (u - s) * 8 + 16)
                            else:
                                wait(pe, f.xhat_made, u + 1)
                            wait(pe, f.lo_made, u)
                            for k in range(GT):
                                mm = pe.transpose(f.psT[:, P * k:P * k + P], f.xhat[:, s, k, :], c.ident[:, :])
                            mm.then_inc(f.xT_done, 1)
                for u, s in at(i, r_, 3):
                    wait(pe, y_kept, u + 1)
                    wait(pe, o_kept, u if routed else u * GT)
                    for k in range(GT):
                        mm = pe.transpose(psO[:, P * k:P * k + P], yT[:, s, P * k:P * k + P], c.ident[:, :])
                    mm.then_inc(o_done, 1)
            run_steps(pe, NG, 4, 2, step)

        @block.scalar
        def _(act):
            def weights_hi(s, part):
                act.activation(wh[:, s, part], w[:, s, part], ACT.Copy).then_inc(w_hi, 1)

            if not routed:
                act.wait_ge(w_loaded[0], 16)
                weights_hi(0, W13)
                weights_hi(0, W2)

            def step(i, r_):
                for u, s in at(i, r_, 1):
                    if routed:
                        wait(act, a_done, (u - 1) * IC)
                        wait(act, w_loaded[s], (u - s) * 8 + 16)
                        weights_hi(s, W13)
                for q in range(IC):
                    for u, s in at(i, r_, 2):
                        n, z = u * IC + q, (s + q) % 2
                        wait(act, a_done, n + 1)
                        wait(act, h_made, n - 1)
                        act.activation(act_sb[:, z, :], psA[:, z, :], ACT.Silu).then_inc(a_kept, 1)
                        wait(act, h_made, n + 1)
                        wait(act, used, n - 1)
                        act.activation(hh[:, z, :], h[:, z, :], ACT.Copy).then_inc(hh_made, 1)
                    if q == 1:
                        for u, s in at(i, r_, 3):
                            wait(act, used, u * IC + IC)
                            wait(act, o_done, u - 1)
                            act.activation(yT[:, s, :], psY[:, s, :], ACT.Copy).then_inc(y_kept, 1)
                        for u, s in at(i, r_, 1):
                            wait(act, a_done, (u - 1) * IC)
                            f.scalar_hi(act, u, s)
                            if routed:
                                wait(act, used, (u - 1) * IC)
                                weights_hi(s, W2)
            run_steps(act, NG, 4, 2, step)

        @block.vector
        def _(dve):
            def weights_lo(s, part):
                dve.tensor_tensor(wl[:, s, part], w[:, s, part], wh[:, s, part], ALU.subtract).then_inc(w_lo, 1)

            if not routed:
                dve.wait_ge(w_hi, 2)
                weights_lo(0, W13)
                weights_lo(0, W2)

            def hidden_lo(u, s, q):
                n, z = u * IC + q, (s + q) % 2
                wait(dve, hh_made, n + 1)
                wait(dve, used, n - 1)
                dve.tensor_tensor(hl[:, z, :], h[:, z, :], hh[:, z, :], ALU.subtract).then_inc(hl_made, 1)

            def step(i, r_):
                for u, s in at(i, r_, 1):
                    if routed:
                        wait(dve, w_hi, 2 * u + 1)
                        weights_lo(s, W13)
                for q in range(IC):
                    for u, s in at(i, r_, 2):
                        n, z = u * IC + q, (s + q) % 2
                        wait(dve, a_kept, n + 1)
                        wait(dve, hl_made, n - 1)
                        dve.tensor_tensor(h[:, z, :], psG[:, z, :], act_sb[:, z, :], ALU.mult).then_inc(h_made, 1)
                        if q and not routed:
                            hidden_lo(u, s, q - 1)
                    if q == 0 and not routed:
                        for u, s in at(i, r_, 3):
                            hidden_lo(u, s, IC - 1)
                        for u, s in at(i, r_, 0):
                            f.vector_norm(dve, u, s)
                    if q == 1:
                        for u, s in at(i, r_, 1):
                            wait(dve, a_done, (u - 1) * IC)
                            f.vector_lo(dve, u, s)
                            if routed:
                                wait(dve, w_hi, 2 * u + 2)
                                weights_lo(s, W2)
                for u, s in at(i, r_, 3):
                    wait(dve, o_done, u + 1)
                    if routed:
                        wait(dve, y_stored[s], (u - s) * 8)
                        dve.tensor_copy(y_out[:, s].rearrange("p t d -> p (t d)"), psO[:, :]).then_inc(o_kept, 1)
                    else:
                        for k in range(GT):
                            t = u * GT + k
                            dve.scalar_tensor_tensor(out=c.x[:, t, :], in0=psO[:, P * k:P * k + P],
                                                     scalar=r.w_shared[:, bass.ds(t, 1)], in1=c.x[:, t, :],
                                                     op0=ALU.mult, op1=ALU.add).then_inc(o_kept, 1)
            run_steps(dve, NG, 4, 2, step)


def add_routed(c, name, sems, r):
    nc, NT = c.nc, c.NT
    BATCH = 8
    with ExitStack() as ctx:
        gathered = [sems(f"{name}_gathered{q}") for q in range(NT // BATCH)]
        summed, stats_made = sems(name + "_summed"), sems(name + "_stats")
        block = ctx.enter_context(nc.Block())

        @block.gpsimd
        def _(pool):
            for t in range(NT):
                pool.indirect_dma_start(r.xhat[:, t, :], None, r.sorted_y,
                                        bass.IndirectOffsetOnAxis(ap=r.place[:, t:t + 1], axis=0)
                                        ).then_inc(gathered[t // BATCH], 16)

        @block.vector
        def _(dve):
            for q in range(NT // BATCH):
                dve.wait_ge(gathered[q], 16 * BATCH)
                for t in range(q * BATCH, (q + 1) * BATCH):
                    dve.scalar_tensor_tensor(out=c.x[:, t, :], in0=r.xhat[:, t, :], scalar=r.w_routed[:, t:t + 1],
                                             in1=c.x[:, t, :], op0=ALU.mult, op1=ALU.add).then_inc(summed, 1)
                dve.wait_ge(summed, (q + 1) * BATCH)
                for t in range(q * BATCH, (q + 1) * BATCH):
                    dve.bn_stats(c.stats[:, t, :], c.x[:, t, :]).then_inc(stats_made, 1)
            dve.wait_ge(stats_made, NT)


def relative_bias(c, name, sems, rel_dram, scratch, rel):
    nc = c.nc
    buckets = rel_bucket(np.arange(2 * S - 1) - (S - 1))
    with ExitStack() as ctx:
        table = ctx.enter_context(nc.sbuf_tensor(name + "_table", [H, 32], F32))
        line = ctx.enter_context(nc.sbuf_tensor(name + "_line", [H, 2 * S], F32))
        bias = ctx.enter_context(nc.sbuf_tensor(name + "_bias", [P, H, S], F32))
        flip = ctx.enter_context(nc.sbuf_tensor(name + "_flip", [P, P], F32))
        loaded, lined, written = sems(name + "_loaded"), sems(name + "_lined"), sems(name + "_written")
        spread, flipped, split = sems(name + "_spread"), sems(name + "_flipped"), sems(name + "_split")
        block = ctx.enter_context(nc.Block())

        @block.sync
        def _(sp):
            sp.dma_start(table[:, :], rel_dram).then_inc(loaded, 16)
            sp.wait_ge(lined, 2 * S)
            sp.dma_start(scratch, line[:, :]).then_inc(written, 16)
            sp.wait_ge(written, 16)
            for b in range(B2):
                sp.dma_start(bias[S * b:S * b + S, :, :], bass.AP(scratch.tensor, 0, [[1, S], [2 * S, H], [1, S]])
                             ).then_inc(spread, 16)

        @block.gpsimd
        def _(pool):
            run = chain(pool, flipped)
            run(pool.memset(flip[:, :], 0.0))
            for total in (S - 1, S - 1 + P):
                run(pool.affine_select(out=flip[:, :], in_=flip[:, :], compare_op=ALU.not_equal, fill=1.0,
                                       base=-total, pattern=[[1, P]], channel_multiplier=1))
            run(pool.tensor_copy(rel["flip"][:, :], flip[:, :]))

        @block.vector
        def _(dve):
            dve.wait_ge(loaded, 16)
            for j, bucket in enumerate(list(buckets) + [0]):
                dve.tensor_copy(line[:, j:j + 1], table[:, int(bucket):int(bucket) + 1]).then_inc(lined, 1)
            dve.wait_ge(spread, 32)
            dve.tensor_copy(rel["hi"][:, :, :], bias[:, :, :]).then_inc(split, 1)
            dve.wait_ge(split, 1)
            dve.tensor_tensor(rel["lo"][:, :, :], bias[:, :, :], rel["hi"][:, :, :], ALU.subtract).then_inc(split, 1)
            dve.wait_ge(split, 2)


def context_attention(c, name, sems, ctx_dram, ctxT, mask, gamma, beta, scale):
    nc, NT = c.nc, c.NT
    DEPTH = 8
    with ExitStack() as octx:
        o_all = octx.enter_context(nc.sbuf_tensor(name + "_o_all", [P, NT, P], F32))
        with ExitStack() as ctx:
            sb = lambda n, shape, dt=F32: ctx.enter_context(nc.sbuf_tensor(f"{name}_{n}", shape, dt))
            pb = lambda n, shape: ctx.enter_context(nc.psum_tensor(f"{name}_{n}", shape, F32))
            sem = lambda n: sems(f"{name}_{n}")
            xhat, xT = sb("xhat", [P, RING, P]), sb("xT", [P, RING, P])
            kT, v = sb("ctxT", [P, RING, P]), sb("ctx", [P, RING, P])
            m_raw, mb = sb("mask_raw", [P, RING, S], I32), sb("mask_bias", [P, RING, S])
            sc, less = sb("scores", [P, RING, S]), sb("less_max", [P, RING])
            pr, prT = sb("probs", [P, RING, P]), sb("probs_T", [P, RING, P])
            den, inv = sb("den", [P, RING]), sb("inv_den", [P, RING])
            psX, psS, psP, psO = (pb("X", [P, 2, 512]), pb("S", [P, 2, 512]), pb("P", [P, 2, 512]),
                                  pb("O", [P, 2, 512]))
            k_loaded = [sem(f"ctxT_loaded{r}") for r in range(RING)]
            v_loaded = [sem(f"ctx_loaded{r}") for r in range(RING)]
            m_loaded = [sem(f"mask_loaded{r}") for r in range(RING)]
            zeroed, xhat_made, xT_done, xT_kept = sem("zeroed"), sem("xhat_made"), sem("xT_done"), sem("xT_kept")
            mb_made, s_done, scored, max_made = sem("mb_made"), sem("s_done"), sem("scored"), sem("max_made")
            p_made, pT_done, pT_kept, o_done = sem("p_made"), sem("pT_done"), sem("pT_kept"), sem("o_done")
            den_made, o_kept, stats_made = sem("den_made"), sem("o_kept"), sem("stats")
            block = ctx.enter_context(nc.Block())

            def at(i, r, lag):
                u = i - lag
                if not isinstance(u, int) or 0 <= u < NT:
                    yield u, (r - lag) % RING

            def turns(u, s):
                return (u - s) * 4 + 16

            @block.sync
            def _(sp):
                def step(i, r):
                    for u, s in at(i, r, 0):
                        rows = bass.ds(u * P, P)
                        wait(sp, s_done, u - 3)
                        sp.dma_start(kT[:, s, :], ctxT[:, rows]).then_inc(k_loaded[s], 16)
                        wait(sp, mb_made, u - 3)
                        sp.dma_start(m_raw[:, s, :], mask[rows, :]).then_inc(m_loaded[s], 16)
                    for u, s in at(i, r, 3):
                        wait(sp, o_done, u - 3)
                        sp.dma_start(v[:, s, :], ctx_dram[bass.ds(u * P, P), :]).then_inc(v_loaded[s], 16)
                run_steps(sp, NT, DEPTH, RING, step)

            @block.gpsimd
            def _(pool):
                pool.memset(pr[:, :, :], 0.0).then_inc(zeroed, 1)

            @block.tensor
            def _(pe):
                def step(i, r):
                    for u, s in at(i, r, 6):
                        wait(pe, pT_kept, u + 1)
                        wait(pe, v_loaded[s], turns(u, s))
                        wait(pe, o_kept, u - 1)
                        pe.matmul(psO[:, s % 2, 0:P], prT[:, s, :], v[:, s, :], start=True, stop=True
                                  ).then_inc(o_done, 1)
                    for u, s in at(i, r, 4):
                        wait(pe, p_made, u + 1)
                        wait(pe, pT_kept, u - 1)
                        pe.transpose(psP[:, s % 2, 0:P], pr[:, s, :], c.ident[:, :]).then_inc(pT_done, 1)
                    for u, s in at(i, r, 2):
                        wait(pe, k_loaded[s], turns(u, s))
                        wait(pe, xT_kept, u + 1)
                        wait(pe, scored, u - 1)
                        for b in range(B2):
                            half = slice(S * b, S * b + S)
                            mm = pe.matmul(psS[half, s % 2, 0:S], xT[:, s, half], kT[:, s, half],
                                           start=True, stop=True, skip_group_check=True)
                        mm.then_inc(s_done, 1)
                    for u, s in at(i, r, 1):
                        wait(pe, xhat_made, u + 1)
                        wait(pe, xT_kept, u - 1)
                        pe.transpose(psX[:, s % 2, 0:P], xhat[:, s, :], c.ident[:, :]).then_inc(xT_done, 1)
                run_steps(pe, NT, DEPTH, RING, step)

            @block.scalar
            def _(act):
                act.wait_ge(zeroed, 1)

                def step(i, r):
                    for u, s in at(i, r, 4):
                        wait(act, pT_done, u + 1)
                        wait(act, o_done, u - 3)
                        act.activation(prT[:, s, :], psP[:, s % 2, 0:P], ACT.Copy).then_inc(pT_kept, 1)
                    for u, s in at(i, r, 3):
                        wait(act, max_made, u + 1)
                        wait(act, pT_done, u - 3)
                        wait(act, den_made, u - 3)
                        for b in range(B2):
                            half = slice(S * b, S * b + S)
                            last = act.activation(pr[half, s, half], sc[half, s, :], ACT.Exp,
                                                  bias=less[half, s:s + 1], accum_out=den[half, s:s + 1])
                        last.then_inc(p_made, 1)
                    for u, s in at(i, r, 1):
                        wait(act, xT_done, u + 1)
                        wait(act, s_done, u - 3)
                        act.activation(xT[:, s, :], psX[:, s % 2, 0:P], ACT.Copy).then_inc(xT_kept, 1)
                run_steps(act, NT, DEPTH, RING, step)

            @block.vector
            def _(dve):
                def step(i, r):
                    for u, s in at(i, r, 7):
                        wait(dve, o_done, u + 1)
                        wait(dve, den_made, u + 1)
                        dve.tensor_scalar(o_all[:, u, :], psO[:, s % 2, 0:P], inv[:, s:s + 1], None, ALU.mult
                                          ).then_inc(o_kept, 1)
                        wait(dve, o_kept, u + 1)
                        dve.bn_stats(c.stats[:, u, :], o_all[:, u, :]).then_inc(stats_made, 1)
                    for u, s in at(i, r, 2):
                        wait(dve, s_done, u + 1)
                        wait(dve, p_made, u - 3)
                        wait(dve, mb_made, u + 1)
                        dve.scalar_tensor_tensor(out=sc[:, s, :], in0=psS[:, s % 2, 0:S], scalar=scale,
                                                 in1=mb[:, s, :], op0=ALU.mult, op1=ALU.add).then_inc(scored, 1)
                    for u, s in at(i, r, 0):
                        wait(dve, xT_done, u - 3)
                        dve.tensor_scalar(xhat[:, s, :], c.x[:, u, :], c.rstd[:, bass.ds(u, 1)],
                                          c.nmr[:, bass.ds(u, 1)], ALU.mult, ALU.add).then_inc(xhat_made, 1)
                        wait(dve, m_loaded[s], turns(u, s))
                        dve.tensor_scalar(mb[:, s, :], m_raw[:, s, :], 0.0, MASKED, ALU.is_equal, ALU.mult
                                          ).then_inc(mb_made, 1)
                    for u, s in at(i, r, 2):
                        wait(dve, scored, u + 1)
                        dve.tensor_reduce(less[:, s:s + 1], sc[:, s, :], AX.X, ALU.max, negate=True
                                          ).then_inc(max_made, 1)
                    for u, s in at(i, r, 4):
                        wait(dve, p_made, u + 1)
                        dve.reciprocal(inv[:, s:s + 1], den[:, s:s + 1]).then_inc(den_made, 1)
                run_steps(dve, NT, DEPTH, RING, step)
                dve.wait_ge(stats_made, NT)

        layernorm_scales(c, name + "_o", sems)
        with ExitStack() as ctx:
            normed, scaled, summed = sems(name + "_normed"), sems(name + "_scaled"), sems(name + "_summed")
            based, stats2 = sems(name + "_based"), sems(name + "_stats2")
            block = ctx.enter_context(nc.Block())

            @block.scalar
            def _(act):
                with act.Fori(0, NT) as t:
                    act.activation(o_all[:, t, :], o_all[:, t, :], ACT.Identity, bias=c.nmr[:, bass.ds(t, 1)],
                                   scale=c.rstd[:, bass.ds(t, 1)]).then_inc(normed, 1)

            @block.gpsimd
            def _(pool):
                with pool.Fori(0, NT // GT) as u:
                    o4 = o_all[:, bass.ds(u * GT, GT), :]
                    x4 = c.x[:, bass.ds(u * GT, GT), :]
                    pool.tensor_tensor(x4, x4, beta.unsqueeze(1).broadcast_to([P, GT, P]), ALU.add)
                    pool.wait_ge(normed, (u + 1) * GT)
                    pool.tensor_tensor(o4, o4, gamma.unsqueeze(1).broadcast_to([P, GT, P]), ALU.mult
                                       ).then_inc(scaled, 1)

            @block.vector
            def _(dve):
                with dve.Fori(0, NT // GT) as u:
                    o4 = o_all[:, bass.ds(u * GT, GT), :]
                    x4 = c.x[:, bass.ds(u * GT, GT), :]
                    dve.wait_ge(scaled, u + 1)
                    dve.tensor_tensor(x4, x4, o4, ALU.add).then_inc(summed, 1)
                    dve.wait_ge(summed, u + 1)
                    for k in range(GT):
                        dve.bn_stats(c.stats[:, u * GT + k, :], c.x[:, u * GT + k, :]).then_inc(stats2, 1)
                dve.wait_ge(stats2, NT)


def mixture_gates(c, name, sems, wg1, bg1, wg2, bg2, bias_w, scratch, moe, scale, E=4, TOP_K=2):
    nc, NT = c.nc, c.NT
    NB = B2 * NT
    with ExitStack() as ctx:
        sb = lambda n, shape, dt=F32: ctx.enter_context(nc.sbuf_tensor(f"{name}_{n}", shape, dt))
        pb = lambda n, shape: ctx.enter_context(nc.psum_tensor(f"{name}_{n}", shape, F32))
        sem = lambda n: sems(f"{name}_{n}")
        xhat = sb("xhat", [P, 2, GT, P])
        mean_of = sb("mean_of", [P, B2])
        pooled, hidden = sb("pooled", [P, NB]), sb("hidden", [P, NB])
        lg, red, rank = sb("lg", [NB, E]), sb("red", [NB, 1]), sb("rank", [NB, E])
        pair, tie, w, wT = sb("pair", [NB, E, E]), sb("tie", [NB, E, E]), sb("w", [NB, E]), sb("wT", [E, NB])
        earlier = sb("earlier", [NB, E, E])
        psP, psH, psL, psW, psB = (pb("P", [P, 512]), pb("Hd", [P, 512]), pb("L", [P, 512]), pb("W", [P, 512]),
                                   pb("B", [P, 512]))
        const, xhat_made, pooled_done = sem("const"), sem("xhat_made"), sem("pooled_done")
        pe_done, act_done, dve_step = sem("pe_done"), sem("act_done"), sem("dve")
        w_made, exp_in, written, spread = sem("w_made"), sem("exp_in"), sem("written"), sem("spread")
        lg_made, wT_made = sem("lg_made"), sem("wT_made")
        block = ctx.enter_context(nc.Block())

        @block.gpsimd
        def _(pool):
            run = chain(pool, const)
            for b in range(B2):
                for half in range(B2):
                    run(pool.memset(mean_of[S * half:S * half + S, b:b + 1], 1.0 / S if half == b else 0.0))
            for e in range(E):
                for j in range(E):
                    run(pool.memset(earlier[:, e, j:j + 1], 1.0 if j < e else 0.0))

        @block.vector
        def _(dve):
            run = chain(dve, dve_step)
            dve.wait_ge(const, B2 * B2 + E * E)

            def step(u, s):
                wait(dve, pooled_done, (u - 1) * GT)
                for k in range(GT):
                    t = u * GT + k
                    last = dve.tensor_scalar(xhat[:, s, k, :], c.x[:, t, :], c.rstd[:, bass.ds(t, 1)],
                                             c.nmr[:, bass.ds(t, 1)], ALU.mult, ALU.add)
                last.then_inc(xhat_made, 1)
            run_steps(dve, NT // GT, 0, 2, step)
            dve.wait_ge(pe_done, 2)
            dve.tensor_tensor(lg[:, :], psL[0:NB, 0:E], bg2, ALU.add).then_inc(lg_made, 1)
            dve.wait_ge(lg_made, 1)
            run(dve.tensor_reduce(red[:, :], lg[:, :], AX.X, ALU.max))
            mine = lg[:, :].unsqueeze(2).broadcast_to([NB, E, E])
            other = lg[:, :].unsqueeze(1).broadcast_to([NB, E, E])
            run(dve.tensor_tensor(pair[:, :, :], other, mine, ALU.is_gt))
            run(dve.tensor_tensor(tie[:, :, :], other, mine, ALU.is_equal))
            run(dve.tensor_tensor(tie[:, :, :], tie[:, :, :], earlier[:, :, :], ALU.mult))
            run(dve.tensor_tensor(pair[:, :, :], pair[:, :, :], tie[:, :, :], ALU.add))
            run(dve.tensor_reduce(rank[:, :], pair[:, :, :], AX.X, ALU.add))
            run(dve.tensor_scalar(rank[:, :], rank[:, :], float(TOP_K), None, ALU.is_lt))
            dve.tensor_scalar(lg[:, :], lg[:, :], red[:, 0:1], None, ALU.subtract).then_inc(exp_in, 1)
            dve.wait_ge(act_done, 3)
            run(dve.tensor_tensor(w[:, :], lg[:, :], rank[:, :], ALU.mult))
            run(dve.tensor_reduce(red[:, :], w[:, :], AX.X, ALU.add))
            run(dve.reciprocal(red[:, :], red[:, :]))
            dve.tensor_scalar(w[:, :], w[:, :], red[:, 0:1], None, ALU.mult).then_inc(w_made, 1)
            dve.wait_ge(pe_done, 3)
            dve.tensor_copy(wT[:, :], psW[0:E, 0:NB]).then_inc(wT_made, 1)
            dve.wait_ge(pe_done, 4)
            run(dve.tensor_scalar(moe["q_bias"][:, 0:NB], psB[:, 0:NB], scale, None, ALU.mult))
            run(dve.tensor_copy(moe["k_bias"][:, 0:NB], psB[:, P:P + NB]))
            run(dve.tensor_copy(moe["v_bias"][:, 0:NB], psB[:, 2 * P:2 * P + NB]))

        @block.tensor
        def _(pe):
            def step(u, s):
                wait(pe, xhat_made, u + 1)
                for k in range(GT):
                    t = u * GT + k
                    pe.matmul(psP[:, bass.ds(t * B2, B2)], xhat[:, s, k, :], mean_of[:, :], start=True,
                              stop=True, skip_group_check=True).then_inc(pooled_done, 1)
            run_steps(pe, NT // GT, 0, 2, step)
            pe.wait_ge(act_done, 1)
            pe.matmul(psH[:, 0:NB], wg1, pooled[:, :], start=True, stop=True).then_inc(pe_done, 1)
            pe.wait_ge(act_done, 2)
            pe.matmul(psL[0:NB, 0:E], hidden[:, :], wg2, start=True, stop=True).then_inc(pe_done, 1)
            pe.wait_ge(w_made, 1)
            pe.transpose(psW[0:E, 0:NB], w[:, :], c.ident[0:NB, 0:NB]).then_inc(pe_done, 1)
            pe.wait_ge(wT_made, 1)
            for j in range(3):
                mm = pe.matmul(psB[:, j * P:j * P + NB], bias_w[:, j, :], wT[:, :], start=j == 0, stop=True,
                               skip_group_check=True)
            mm.then_inc(pe_done, 1)

        @block.scalar
        def _(act):
            act.wait_ge(pooled_done, NT)
            act.activation(pooled[:, :], psP[:, 0:NB], ACT.Copy).then_inc(act_done, 1)
            act.wait_ge(pe_done, 1)
            act.activation(hidden[:, :], psH[:, 0:NB], ACT.Relu, bias=bg1).then_inc(act_done, 1)
            act.wait_ge(exp_in, 1)
            act.activation(lg[:, :], lg[:, :], ACT.Exp).then_inc(act_done, 1)

        @block.sync
        def _(sp):
            sp.wait_ge(w_made, 1)
            sp.dma_start(scratch[0:NB, :], w[:, :]).then_inc(written, 16)
            sp.wait_ge(written, 16)
            for b in range(B2):
                sp.dma_start(moe["w_tok"][S * b:S * b + S, :, :],
                             bass.AP(scratch.tensor, b * E, [[0, S], [B2 * E, NT], [1, E]])).then_inc(spread, 16)
            sp.wait_ge(spread, 16 * B2)


def store_x(c, out, sems):
    NT = c.NT
    with ExitStack() as ctx:
        block = ctx.enter_context(c.nc.Block())
        stored = sems("x_stored")

        @block.sync
        def _(sp):
            CH = 8
            for q in range(NT // CH):
                sp.dma_start(out[q * CH * P:(q + 1) * CH * P, :].rearrange("(t p) d -> p t d", p=P),
                             c.x[:, q * CH:(q + 1) * CH, :]).then_inc(stored, 16)
            sp.wait_ge(stored, 16 * (NT // CH))


def column(v):
    return v.rearrange("(p o) -> p o", o=1)


def everywhere(v):
    return v.rearrange("(o n) -> o n", o=1).broadcast_to([P, v.shape[0]])


def program(nc, a, out, NT, stages):
    with ExitStack() as outer:
        c = Core()

        in_use = []

        def sems(name):
            in_use.append(nc.alloc_semaphore(name=name))
            return in_use[-1]

        def free_semaphores():
            nc.all_engine_barrier()
            nc.clear_and_free_semaphores(in_use)
            nc.all_engine_barrier()
            in_use.clear()

        allocate(c, nc, outer, NT)
        build_constants(c, sems)
        SC = DH ** -0.5

        def stage(name):
            ctx = ExitStack()
            parts = []

            def sb(n, shape, dt=F32):
                return ctx.enter_context(nc.sbuf_tensor(f"{name}_w_{n}", shape, dt))

            def take(n, shape, src, dt=F32):
                t = sb(n, shape, dt)
                parts.append((t[tuple(slice(None) for _ in shape)], src))
                return t
            return ctx, sb, take, parts

        def scaled(name, dst, src):
            with ExitStack() as ctx:
                block = ctx.enter_context(nc.Block())
                done = sems(name + "_bias_scaled")

                @block.vector
                def _(dve):
                    dve.tensor_scalar(dst, src, SC, None, ALU.mult).then_inc(done, 1)
                    dve.wait_ge(done, 1)

        def projections(take, fmt):
            w = {n: take(n, [P, 1, P], a[fmt.format(n)].rearrange("k (o n) -> k o n", o=1)) for n in "qkv"}
            w["o"] = take("o", [P, P], a[fmt.format("o")])
            return w

        early_parts = []

        def early(name):
            def sb(n, shape, dt=F32):
                return c.sb(f"{name}_w_{n}", shape, dt)

            def take(n, shape, src, dt=F32):
                t = sb(n, shape, dt)
                early_parts.append((t[tuple(slice(None) for _ in shape)], src))
                return t
            return sb, take, early_parts

        if "L0a" in stages:
            sb, take, parts = early("L0a")
            w = projections(take, "L0_xattn_W_{}")
            bq, bk, bv = (take(f"b{n}", [P, 1], column(a[f"L0_xattn_b_{n}"])) for n in "qkv")
            bo = take("bo", [P, P], everywhere(a["L0_xattn_b_o"]))
            bqs = sb("bq_scaled", [P, 1])
            L0a_set = (w, bq, bk, bv, bo, bqs)
        if "L1a" in stages:
            sb, take, parts = early("L1a")
            w = projections(take, "L1_xattn_W{}")
            rel = {"flip": sb("flip", [P, P], F32R), "hi": sb("rel_hi", [P, H, S], F32R),
                   "lo": sb("rel_lo", [P, H, S], F32R)}
            L1a_set = (w, rel)
        if "L2a" in stages:
            sb, take, parts = early("L2a")
            w = projections(take, "L2_xattn_W{}")
            bq, bk = (take(f"b{n}", [P, 1], column(a[f"L2_xattn_b{n}"])) for n in "qk")
            bv = take("bv", [P, P], everywhere(a["L2_xattn_bv"]))
            bo = take("bo", [P, P], everywhere(a["L2_xattn_bo"]))
            bqs = sb("bq_scaled", [P, 1])
            L2a_set = (w, bq, bk, bv, bo, bqs)
        if "L3a" in stages:
            sb, take, parts = early("L3a")
            gamma, beta = (take(n, [P, P], everywhere(a[f"L3_xattn_{n}"])) for n in ("gamma", "beta"))
            L3a_set = (gamma, beta)
        if "L3f" in stages:
            sb, take, parts = early("L3f")
            E = 4
            w = {n: take(n, [P, E, P], a[f"L3_ffn_W{n}"].rearrange("e k n -> k e n")) for n in "qkv"}
            w["o"] = take("o", [P, P], a["L3_ffn_Wo"])
            bo = take("bo", [P, P], everywhere(a["L3_ffn_bo"]))
            wg1, wg2 = take("wg1", [P, P], a["L3_ffn_Wg1"]), take("wg2", [P, E], a["L3_ffn_Wg2"])
            bg1 = take("bg1", [P, 1], column(a["L3_ffn_bg1"]))
            bg2 = take("bg2", [P, E], everywhere(a["L3_ffn_bg2"]))
            bias_w = sb("bias_w", [E, 3, P])
            for j, n in enumerate("qkv"):
                parts.append((bias_w[:, j, :], a[f"L3_ffn_b{n}"]))
            moe = {"xn": sb("xn", [P, RING, P]), "w_tok": sb("w_tok", [P, NT, E]),
                   "q_bias": sb("q_bias", [P, P]), "k_bias": sb("k_bias", [P, P]),
                   "v_bias": sb("v_bias", [P, P])}
            L3f_set = (w, bo, wg1, wg2, bg1, bg2, bias_w, moe)
        load_x(c, a["x"], early_parts, sems)

        if "L0a" in stages:
            free_semaphores()
            w, bq, bk, bv, bo, bqs = L0a_set
            scaled("L0a", bqs[:, :], bq[:, :])
            layernorm_scales(c, "L0a", sems)
            attention(c, "L0a", sems, w, mask=a["mask0"], scale=SC, ctxT=a["ctx_T"],
                      q_bias=bqs[:, :], k_bias=bk[:, :], v_bias_col=bv[:, :], out_bias=bo[:, :], split_pv=True)
        if "L0f" in stages:
            free_semaphores()
            ctx, sb, take, parts = stage("L0f")
            with ctx:
                E = 8
                c.logits = sb("logits", [P, NT, E])
                gh, gl = sb("gate_hi", [P, E], F32R), sb("gate_lo", [P, E], F32R)
                eh, el = sb("ew_hi", [P, E * P], F32R), sb("ew_lo", [P, E * P], F32R)
                gb = take("gate_b", [E, 1], a["L0_ffn_gate_b"].rearrange("(p o) -> p o", o=1))
                eb = sb("eb_blocks", [GT * E, GT, P])
                with ExitStack() as zctx:
                    block = zctx.enter_context(nc.Block())
                    cleared = sems("L0f_cleared")

                    @block.gpsimd
                    def _(pool):
                        pool.memset(eb[:, :, :], 0.0).then_inc(cleared, 1)
                        pool.wait_ge(cleared, 1)
                for k in range(GT):
                    parts.append((eb[E * k:E * k + E, k, :], a["L0_ffn_expert_b"]))
                split_weights(c, "L0f_split", [
                    ([P, E], [(lambda t: t[:, :], a["L0_ffn_gate_w"])], gh[:, :], gl[:, :]),
                    ([P, E, P], [(lambda t: t[:, :, :], a["L0_ffn_expert_w"].rearrange("e k n -> k e n"))],
                     eh[:, :].rearrange("p (e n) -> p e n", e=E), el[:, :].rearrange("p (e n) -> p e n", e=E)),
                ], sems, whole=parts)
                layernorm_scales(c, "L0f", sems)
                gate_logits(c, "L0f_gate", sems, (gh[:, :], gl[:, :]), gb[:, :], E)
                soft_moe(c, "L0f", sems, eh, el, eb[:, :, :].rearrange("p t n -> p (t n)"))
        if "L1a" in stages:
            free_semaphores()
            w, rel = L1a_set
            relative_bias(c, "L1a_rel", sems, a["L1_xattn_rel_bias"],
                          nc.dram_tensor("rel_scratch", [H, 2 * S], F32, kind="Internal").ap(), rel)
            layernorm_scales(c, "L1a", sems)
            attention(c, "L1a", sems, w, mask=a["mask1"], key_mask=True, rel=rel, ctxT=a["ctx_T"])
        if "L1f" in stages:
            free_semaphores()
            ctx, sb, take, parts = stage("L1f")
            with ctx:
                HID = a["L1_ffn_w1"].shape[2]
                HC = HID // P
                U = 3 * HC
                w1h, w1l = sb("w1_hi", [P, 3 * HID], F32R), sb("w1_lo", [P, 3 * HID], F32R)
                w2h, w2l = sb("w2_hi", [P, U, P], F32R), sb("w2_lo", [P, U, P], F32R)
                gdh, gdl = sb("gd_hi", [P, P], F32R), sb("gd_lo", [P, P], F32R)
                b1 = sb("b1", [P, U])
                for q in range(U):
                    bias = a["L1_ffn_b1"][q // HC - 1] if q >= HC else a["L1_ffn_sb1"]
                    parts.append((b1[:, q:q + 1], column(bias[q % HC * P:q % HC * P + P])))
                ob = [take(f"ob{i}", [P, P], everywhere(v)) for i, v in
                      enumerate((a["L1_ffn_b2"][0], a["L1_ffn_b2"][1], a["L1_ffn_sb2"]))]
                g = take("gate", [P, 2], a["L1_ffn_gate_w"])
                split_weights(c, "L1f_split", [
                    ([P, 3 * HID],
                     [(lambda t, e=e: t[:, (e + 1) * HID:(e + 2) * HID], a["L1_ffn_w1"][e]) for e in range(2)]
                     + [(lambda t: t[:, 0:HID], a["L1_ffn_sw1"])], w1h[:, :], w1l[:, :]),
                    ([P, U, P],
                     [(lambda t, e=e: t[:, (e + 1) * HC:(e + 2) * HC, :], a["L1_ffn_w2"][e].rearrange("(c p) d -> p c d", p=P))
                      for e in range(2)]
                     + [(lambda t: t[:, 0:HC, :], a["L1_ffn_sw2"].rearrange("(c p) d -> p c d", p=P))],
                     w2h[:, :, :], w2l[:, :, :]),
                ], sems, whole=parts)
                with ExitStack() as pctx:
                    gd = pctx.enter_context(nc.sbuf_tensor("L1f_gd", [P, 1], F32))
                    block = pctx.enter_context(nc.Block())
                    done = sems("L1f_prepared")

                    @block.vector
                    def _(dve):
                        run = chain(dve, done)
                        run(dve.tensor_tensor(ob[0][:, :], ob[0][:, :], ob[1][:, :], ALU.add))
                        run(dve.tensor_tensor(ob[0][:, :], ob[0][:, :], ob[2][:, :], ALU.add))
                        run(dve.tensor_tensor(gd[:, :], g[:, 1:2], g[:, 0:1], ALU.subtract))
                        run(dve.tensor_copy(gdh[:, :], gd[:, 0:1].broadcast_to([P, P])))
                        run(dve.tensor_tensor(gdl[:, :], gd[:, 0:1].broadcast_to([P, P]), gdh[:, :], ALU.subtract))
                layernorm_scales(c, "L1f", sems)
                routed_relu(c, "L1f", sems, (gdh[:, :], gdl[:, :]), (w1h, w1l), b1, (w2h, w2l), ob[0][:, :], HC)
        if "L2a" in stages:
            free_semaphores()
            w, bq, bk, bv, bo, bqs = L2a_set
            scaled("L2a", bqs[:, :], bq[:, :])
            layernorm_scales(c, "L2a", sems)
            attention(c, "L2a", sems, w, linear=True, mask=a["mask2"], scale=SC, ctxT=a["ctx_T"],
                      q_bias=bqs[:, :], k_bias=bk[:, :], v_bias_row=bv[:, :], out_bias=bo[:, :])
        if "L2f" in stages:
            free_semaphores()
            ctx, sb, take, parts = stage("L2f")
            with ctx:
                E = a["L2_ffn_router_w"].shape[1]
                IP = a["L2_ffn_w"].shape[1] // 3
                c.logits = sb("logits", [P, NT, E])
                gh, gl = sb("gate_hi", [P, E], F32R), sb("gate_lo", [P, E], F32R)
                rb = take("router_b", [E, 1], a["L2_ffn_routing_bias"].rearrange("(p o) -> p o", o=1))
                split_weights(c, "L2f_gates", [([P, E], [(lambda t: t[:, :], a["L2_ffn_router_w"])],
                                                gh[:, :], gl[:, :])], sems, whole=parts)
                layernorm_scales(c, "L2f", sems)
                r = Core()
                r.groups = (NT * P + E * (N4 - 1)) // N4
                r.expert_w, r.shared_w = a["L2_ffn_w"], a["L2_ffn_w"][E * P:(E + 1) * P, :]
                r.sorted_x = nc.dram_tensor("sorted_x", [r.groups * N4, P], F32, kind="Internal").ap()
                r.sorted_y = nc.dram_tensor("sorted_y", [r.groups * N4, P], F32, kind="Internal").ap()
                r.xhat = sb("xhat_all", [P, NT, P])
                r.place, r.weight_row = sb("place", [P, NT], I32), sb("weight_row", [P, r.groups], I32)
                r.w_routed, r.w_shared = sb("w_routed", [P, NT]), sb("w_shared", [P, NT])
                gate_logits(c, "L2f_gate", sems, (gh[:, :], gl[:, :]), rb[:, :], E, r)
                route_tokens(c, "L2f_route", sems, r, E)
                swiglu(c, "L2f_shared", sems, r, False, IP)
                swiglu(c, "L2f_routed", sems, r, True, IP)
                add_routed(c, "L2f_add", sems, r)

        if "L3a" in stages:
            free_semaphores()
            gamma, beta = L3a_set
            layernorm_scales(c, "L3a", sems)
            context_attention(c, "L3a", sems, a["ctx"], a["ctx_T"], a["mask3"], gamma[:, :], beta[:, :],
                              P ** -0.5)
        if "L3f" in stages:
            free_semaphores()
            w, bo, wg1, wg2, bg1, bg2, bias_w, moe = L3f_set
            layernorm_scales(c, "L3f", sems)
            mixture_gates(c, "L3f_gate", sems, wg1[:, :], bg1[:, :], wg2[:, :], bg2[0:B2 * NT, :], bias_w,
                          nc.dram_tensor("gate_scratch", [P, a["L3_ffn_Wq"].shape[0]], F32, kind="Internal").ap(), moe, SC)
            attention(c, "L3f", sems, w, moe=moe, scale=SC, out_bias=bo[:, :], split_pv=True)
        store_x(c, out, sems)


def layout(inp):
    T = np.ascontiguousarray
    d = {}
    d["x"] = inp["x"].reshape(-1, P)
    d["ctx"] = inp["ctx_1024"].reshape(-1, P)
    d["ctx_T"] = T(d["ctx"].T)
    d["mask0"] = inp["mask_Bx1xSxS2_if1"].reshape(-1, S)
    d["mask1"] = inp["mask_Bx1x1xS2_bk0"].reshape(-1, S)
    d["mask2"] = inp["mask_Bx1xSxS2_ik1"].reshape(-1, S)
    d["mask3"] = inp["mask_BxSxS2_ik1"].reshape(-1, S)
    for n in inp:
        if n[0] == "L":
            v = inp[n]
            if n.startswith(("L1_xattn_W", "L2_xattn_W")) or n in ("L2_ffn_router_w", "L1_ffn_gate_w"):
                v = T(v.T)
            if not n.startswith(("L2_ffn_ew", "L2_ffn_sw")):
                d[n] = v
    I = inp["L2_ffn_sw1"].shape[0]
    IC = -(-I // P)
    rows = []
    for w1, w3, w2 in [*zip(inp["L2_ffn_ew1"], inp["L2_ffn_ew3"], inp["L2_ffn_ew2"]),
                       (inp["L2_ffn_sw1"], inp["L2_ffn_sw3"], inp["L2_ffn_sw2"])]:
        up = [np.pad(w.T, ((0, 0), (0, IC * P - I))) for w in (w1, w3)]
        down = np.pad(w2.T, ((0, IC * P - I), (0, 0))).reshape(IC, P, P).transpose(1, 0, 2).reshape(P, IC * P)
        rows.append(np.concatenate([*up, down], axis=1))
    d["L2_ffn_w"] = np.concatenate(rows, axis=0)
    return d


def kernel(**inputs):
    import concourse.bacc as bacc
    from concourse.bass_utils import run_bass_kernel_spmd

    nc = bacc.Bacc("TRN2", target_bir_lowering=False, num_devices=1)
    arrays = layout({n: np.asarray(v) for n, v in inputs.items()})
    tokens = arrays["x"].shape[0]
    a = {n: nc.dram_tensor(n, v.shape, mybir.dt.from_np(v.dtype), kind="ExternalInput").ap()
         for n, v in arrays.items()}
    out = nc.dram_tensor("out", [tokens, P], F32, kind="ExternalOutput").ap()
    program(nc, a, out, tokens // P, ("L0a", "L0f", "L1a", "L1f", "L2a", "L2f", "L3a", "L3f"))
    result = run_bass_kernel_spmd(nc, [arrays], core_ids=[0])
    return result.results[0]["out"].reshape(np.asarray(inputs["x"]).shape)
```
